# Optimizing a Trainium2 kernel written in Bass

```python
import numpy as np
import jax
import jax.numpy as jnp

def _softmax(x, axis=-1):
    return jax.nn.softmax(x, axis=axis)
def _gelu(x):
    return jax.nn.gelu(x, approximate=True)
def _silu(x):
    return jax.nn.silu(x)
def _sigmoid(x):
    return jax.nn.sigmoid(x)
def _layernorm(x, axis=-1, eps=1e-5):
    m = jnp.mean(x, axis=axis, keepdims=True)
    v = jnp.var(x, axis=axis, keepdims=True)
    return (x - m) / jnp.sqrt(v + eps)
def _scatter_add(tgt, idx, src, axis=0):
    return tgt.at[idx].add(src)
def _segment_sum(src, seg, n):
    return jax.ops.segment_sum(src, seg, n)

kernel_name = 'mk_conv_attn_hybrid_d2_conv_nchw256_58ef96'

def setup_inputs(seed: int = 0):
    np.random.seed(seed)
    _w = jnp.asarray
    def _rec_inputs():
        import jax
        import jax.numpy as jnp
        _gk = jax.random.key(seed)
        x = -0.0005207 + 1.001 * jax.random.normal(jax.random.fold_in(_gk, 1), (2, 256, 64, 64), jnp.float32)
        return x
    x = _rec_inputs()
    def _L0_conv_setup():
        import jax, jax.numpy as jnp
        import numpy as np
        import math
        from jax import lax
        GROUPS = 4
        EPS = 1e-05

        def _gconv3x3(x, w):
            return lax.conv_general_dilated(x, w, (1, 1), 'SAME', feature_group_count=GROUPS, dimension_numbers=('NCHW', 'OIHW', 'NCHW'))
        key = jax.random.key(seed)
        ks = jax.random.split(key, 8)
        b, c, h, w = (2, 256, 64, 64)
        cq = c // GROUPS
        return {'x': jax.random.normal(ks[0], (b, c, h, w), jnp.float32), 'qw': jax.random.normal(ks[1], (cq, cq // GROUPS, 3, 3), jnp.float32) * 0.05, 'kw': jax.random.normal(ks[2], (cq, cq // GROUPS, 3, 3), jnp.float32) * 0.05, 'vw': jax.random.normal(ks[3], (cq, cq // GROUPS, 3, 3), jnp.float32) * 0.05, 'c1w': jax.random.normal(ks[4], (cq, cq, 1, 1), jnp.float32) * 0.05, 'c1b': jnp.zeros((cq,), jnp.float32), 'gnw': jnp.ones((cq,), jnp.float32), 'gnb': jnp.zeros((cq,), jnp.float32)}
    _L0_conv_all = _L0_conv_setup()
    _L0_conv_in = {k: v for k, v in _L0_conv_all.items() if k in ('qw', 'kw', 'vw', 'c1w', 'c1b', 'gnw', 'gnb', )}
    del _L0_conv_all

    def _L1_attn_setup():
        import jax, jax.numpy as jnp
        import numpy as np
        B, L, D = (4, 2048, 256)
        DI, DS, DR, K = (512, 16, 16, 4)

        def _mamba(x, in_proj_w, conv_w, conv_b, x_proj_w, dt_proj_w, dt_proj_b, A_log, Dp, out_proj_w):
            Bsz, Ls, _ = x.shape
            xz = jnp.einsum('bld,ed->ble', x, in_proj_w)
            xc, z = jnp.split(xz, 2, axis=-1)
            xp = jnp.pad(xc, ((0, 0), (K - 1, 0), (0, 0)))
            xc = sum((xp[:, k:k + Ls, :] * conv_w[:, k] for k in range(K))) + conv_b
            xc = jax.nn.silu(xc)
            x_dbl = jnp.einsum('bld,ed->ble', xc, x_proj_w)
            dt = x_dbl[..., :DR]
            Bm = x_dbl[..., DR:DR + DS]
            Cm = x_dbl[..., DR + DS:]
            dt = jax.nn.softplus(jnp.einsum('blr,dr->bld', dt, dt_proj_w) + dt_proj_b)
            A = -jnp.exp(A_log)
            dA = jnp.exp(dt[..., None] * A)
            dBx = dt[..., None] * Bm[:, :, None, :] * xc[..., None]

            def step(h, inp):
                dA_t, dBx_t, C_t = inp
                h = dA_t * h + dBx_t
                y = jnp.einsum('bds,bs->bd', h, C_t)
                return (h, y)
            h0 = jnp.zeros((Bsz, DI, DS), x.dtype)
            _, ys = jax.lax.scan(step, h0, (dA.transpose(1, 0, 2, 3), dBx.transpose(1, 0, 2, 3), Cm.transpose(1, 0, 2)))
            y = ys.transpose(1, 0, 2) + xc * Dp
            y = y * jax.nn.silu(z)
            return jnp.einsum('bld,ed->ble', y, out_proj_w)
        key = jax.random.key(seed)
        ks = jax.random.split(key, 16)
        n = lambda k, s, sc=0.02: jax.random.normal(k, s, dtype=jnp.float32) * sc
        return {'x': jax.random.normal(ks[0], (B, L, D), dtype=jnp.float32), 'in_proj_w': n(ks[1], (2, 2 * DI, D)), 'conv_w': n(ks[2], (2, DI, K), 0.2), 'conv_b': n(ks[3], (2, DI)), 'x_proj_w': n(ks[4], (2, DR + 2 * DS, DI)), 'dt_proj_w': n(ks[5], (2, DI, DR), 0.1), 'dt_proj_b': n(ks[6], (2, DI)), 'A_log': jax.random.uniform(ks[7], (2, DI, DS), dtype=jnp.float32), 'Dp': n(ks[8], (2, DI), 1.0), 'out_proj_w': n(ks[9], (2, D, DI)), 'ln_g': jnp.ones((D,), jnp.float32), 'ln_b': jnp.zeros((D,), jnp.float32), 'w1': n(ks[10], (2 * D, D)), 'b1': jnp.zeros((2 * D,), jnp.float32), 'w2': n(ks[11], (D, 2 * D)), 'b2': jnp.zeros((D,), jnp.float32)}
    _L1_attn_all = _L1_attn_setup()
    _L1_attn_in = {k: v for k, v in _L1_attn_all.items() if k in ('in_proj_w', 'conv_w', 'conv_b', 'x_proj_w', 'dt_proj_w', 'dt_proj_b', 'A_log', 'Dp', 'out_proj_w', 'ln_g', 'ln_b', 'w1', 'b1', 'w2', 'b2', )}
    del _L1_attn_all

    def _L1_ffn_setup():
        import math
        import jax, jax.numpy as jnp
        import numpy as np
        CAPACITY_FACTOR = 1.25
        key = jax.random.key(seed)
        ks = jax.random.split(key, 5)
        B, L, D, F, E = (8, 8192, 256, 1024, 8)
        h = jax.random.normal(ks[0], (B, L, D), dtype=jnp.float32)
        gate_w = jax.random.normal(ks[1], (D, E), dtype=jnp.float32) * 0.02
        gate_b = jnp.zeros((E,), dtype=jnp.float32)
        w1 = jax.random.normal(ks[2], (E, D, F), dtype=jnp.float32) * (1.0 / math.sqrt(D))
        b1 = jnp.zeros((E, F), dtype=jnp.float32)
        w2 = jax.random.normal(ks[3], (E, F, D), dtype=jnp.float32) * (1.0 / math.sqrt(F))
        b2 = jnp.zeros((E, D), dtype=jnp.float32)
        return {'h': h, 'gate_w': gate_w, 'gate_b': gate_b, 'w1': w1, 'b1': b1, 'w2': w2, 'b2': b2}
    _L1_ffn_all = _L1_ffn_setup()
    _L1_ffn_in = {k: v for k, v in _L1_ffn_all.items() if k in ('gate_w', 'gate_b', 'w1', 'b1', 'w2', 'b2', )}
    del _L1_ffn_all

    return {
        "x": x,
        "L0_conv_qw": _L0_conv_in["qw"],
        "L0_conv_kw": _L0_conv_in["kw"],
        "L0_conv_vw": _L0_conv_in["vw"],
        "L0_conv_c1w": _L0_conv_in["c1w"],
        "L0_conv_c1b": _L0_conv_in["c1b"],
        "L0_conv_gnw": _L0_conv_in["gnw"],
        "L0_conv_gnb": _L0_conv_in["gnb"],
        "L1_attn_in_proj_w": _L1_attn_in["in_proj_w"],
        "L1_attn_conv_w": _L1_attn_in["conv_w"],
        "L1_attn_conv_b": _L1_attn_in["conv_b"],
        "L1_attn_x_proj_w": _L1_attn_in["x_proj_w"],
        "L1_attn_dt_proj_w": _L1_attn_in["dt_proj_w"],
        "L1_attn_dt_proj_b": _L1_attn_in["dt_proj_b"],
        "L1_attn_A_log": _L1_attn_in["A_log"],
        "L1_attn_Dp": _L1_attn_in["Dp"],
        "L1_attn_out_proj_w": _L1_attn_in["out_proj_w"],
        "L1_attn_ln_g": _L1_attn_in["ln_g"],
        "L1_attn_ln_b": _L1_attn_in["ln_b"],
        "L1_attn_w1": _L1_attn_in["w1"],
        "L1_attn_b1": _L1_attn_in["b1"],
        "L1_attn_w2": _L1_attn_in["w2"],
        "L1_attn_b2": _L1_attn_in["b2"],
        "L1_ffn_gate_w": _L1_ffn_in["gate_w"],
        "L1_ffn_gate_b": _L1_ffn_in["gate_b"],
        "L1_ffn_w1": _L1_ffn_in["w1"],
        "L1_ffn_b1": _L1_ffn_in["b1"],
        "L1_ffn_w2": _L1_ffn_in["w2"],
        "L1_ffn_b2": _L1_ffn_in["b2"],
    }

def reference(x, L0_conv_qw, L0_conv_kw, L0_conv_vw, L0_conv_c1w, L0_conv_c1b, L0_conv_gnw, L0_conv_gnb, L1_attn_in_proj_w, L1_attn_conv_w, L1_attn_conv_b, L1_attn_x_proj_w, L1_attn_dt_proj_w, L1_attn_dt_proj_b, L1_attn_A_log, L1_attn_Dp, L1_attn_out_proj_w, L1_attn_ln_g, L1_attn_ln_b, L1_attn_w1, L1_attn_b1, L1_attn_w2, L1_attn_b2, L1_ffn_gate_w, L1_ffn_gate_b, L1_ffn_w1, L1_ffn_b1, L1_ffn_w2, L1_ffn_b2):
    import jax
    import jax.numpy as jnp
    def _L0_conv_ref(x, qw, kw, vw, c1w, c1b, gnw, gnb):
        import jax, jax.numpy as jnp
        import numpy as np
        import math
        from jax import lax
        GROUPS = 4
        EPS = 1e-05

        def _gconv3x3(x, w):
            return lax.conv_general_dilated(x, w, (1, 1), 'SAME', feature_group_count=GROUPS, dimension_numbers=('NCHW', 'OIHW', 'NCHW'))
        b, c, h, w = x.shape
        g = GROUPS
        cq = c // g
        gx = x.reshape(b * g, cq, h, w)
        query = _gconv3x3(gx, qw)
        key_ = _gconv3x3(gx, kw)
        value = _gconv3x3(gx, vw)
        q_h = jnp.transpose(query.mean(axis=2, keepdims=True), (0, 1, 3, 2))
        q_w = query.mean(axis=3, keepdims=True)
        hw_cat = jnp.concatenate([q_h, q_w], axis=2)
        hw_cat = lax.conv_general_dilated(hw_cat, c1w, (1, 1), 'VALID', dimension_numbers=('NCHW', 'OIHW', 'NCHW'))
        hw_cat = hw_cat + c1b[None, :, None, None]
        g_h = hw_cat[:, :, :h, :]
        g_w = hw_cat[:, :, h:, :]
        gated = gx * jax.nn.sigmoid(jnp.transpose(g_h, (0, 1, 3, 2))) * jax.nn.sigmoid(g_w)
        mean = gated.mean(axis=(2, 3), keepdims=True)
        var = gated.var(axis=(2, 3), keepdims=True)
        qn = (gated - mean) * lax.rsqrt(var + EPS)
        qn = qn * gnw[None, :, None, None] + gnb[None, :, None, None]
        qf = jnp.transpose(qn.reshape(b, g, cq, h * w), (0, 1, 3, 2))
        kf = jnp.transpose(key_.reshape(b, g, cq, h * w), (0, 1, 3, 2))
        vf = jnp.transpose(value.reshape(b, g, cq, h * w), (0, 1, 3, 2))
        scores = jnp.einsum('bgnc,bgmc->bgnm', qf, kf) * (1.0 / math.sqrt(c))
        attn = jax.nn.softmax(scores, axis=-1)
        ctx = jnp.einsum('bgnm,bgmc->bgnc', attn, vf)
        out = jnp.transpose(ctx, (0, 1, 3, 2)).reshape(b, c, h, w)
        return out

    def _L1_attn_ref(x, in_proj_w, conv_w, conv_b, x_proj_w, dt_proj_w, dt_proj_b, A_log, Dp, out_proj_w, ln_g, ln_b, w1, b1, w2, b2):
        import jax, jax.numpy as jnp
        import numpy as np
        B, L, D = (4, 2048, 256)
        DI, DS, DR, K = (512, 16, 16, 4)

        def _mamba(x, in_proj_w, conv_w, conv_b, x_proj_w, dt_proj_w, dt_proj_b, A_log, Dp, out_proj_w):
            Bsz, Ls, _ = x.shape
            xz = jnp.einsum('bld,ed->ble', x, in_proj_w)
            xc, z = jnp.split(xz, 2, axis=-1)
            xp = jnp.pad(xc, ((0, 0), (K - 1, 0), (0, 0)))
            xc = sum((xp[:, k:k + Ls, :] * conv_w[:, k] for k in range(K))) + conv_b
            xc = jax.nn.silu(xc)
            x_dbl = jnp.einsum('bld,ed->ble', xc, x_proj_w)
            dt = x_dbl[..., :DR]
            Bm = x_dbl[..., DR:DR + DS]
            Cm = x_dbl[..., DR + DS:]
            dt = jax.nn.softplus(jnp.einsum('blr,dr->bld', dt, dt_proj_w) + dt_proj_b)
            A = -jnp.exp(A_log)
            dA = jnp.exp(dt[..., None] * A)
            dBx = dt[..., None] * Bm[:, :, None, :] * xc[..., None]

            def step(h, inp):
                dA_t, dBx_t, C_t = inp
                h = dA_t * h + dBx_t
                y = jnp.einsum('bds,bs->bd', h, C_t)
                return (h, y)
            h0 = jnp.zeros((Bsz, DI, DS), x.dtype)
            _, ys = jax.lax.scan(step, h0, (dA.transpose(1, 0, 2, 3), dBx.transpose(1, 0, 2, 3), Cm.transpose(1, 0, 2)))
            y = ys.transpose(1, 0, 2) + xc * Dp
            y = y * jax.nn.silu(z)
            return jnp.einsum('bld,ed->ble', y, out_proj_w)
        fwd = _mamba(x, in_proj_w[0], conv_w[0], conv_b[0], x_proj_w[0], dt_proj_w[0], dt_proj_b[0], A_log[0], Dp[0], out_proj_w[0])
        bwd = _mamba(x[:, ::-1, :], in_proj_w[1], conv_w[1], conv_b[1], x_proj_w[1], dt_proj_w[1], dt_proj_b[1], A_log[1], Dp[1], out_proj_w[1])
        m = fwd + bwd
        mu = jnp.mean(m, axis=-1, keepdims=True)
        var = jnp.mean(jnp.square(m - mu), axis=-1, keepdims=True)
        h = (m - mu) / jnp.sqrt(var + 1e-05) * ln_g + ln_b
        p = jax.nn.leaky_relu(h @ w1.T + b1, negative_slope=0.01) @ w2.T + b2
        return m + p

    def _L1_ffn_ref(h, gate_w, gate_b, w1, b1, w2, b2):
        import math
        import jax, jax.numpy as jnp
        import numpy as np
        CAPACITY_FACTOR = 1.25
        B, L, D = h.shape
        E = gate_w.shape[1]
        T = B * L
        C = max(1, math.ceil(CAPACITY_FACTOR * T / E))
        x = h.reshape(T, D)
        logits = x @ gate_w + gate_b
        probs = jax.nn.softmax(logits, axis=-1)
        idx = jnp.argmax(probs, axis=-1)
        prb = jnp.take_along_axis(probs, idx[:, None], axis=1)[:, 0]
        one_hot = jax.nn.one_hot(idx, E, dtype=jnp.float32)
        pos = (jnp.cumsum(one_hot, axis=0) * one_hot).sum(-1).astype(jnp.int32) - 1
        kept = pos < C
        pos_safe = jnp.where(kept, pos, C)
        buf = jnp.zeros((E, C, D), dtype=h.dtype).at[idx, pos_safe].set(x, mode='drop')
        hmid = jax.nn.relu(jnp.einsum('ecd,edf->ecf', buf, w1) + b1[:, None, :])
        ybuf = jnp.einsum('ecf,efd->ecd', hmid, w2) + b2[:, None, :]
        pos_g = jnp.minimum(pos, C - 1)
        y_tok = ybuf[idx, pos_g] * (prb * kept)[:, None]
        y = y_tok.reshape(B, L, D)
        y = jnp.nan_to_num(y, nan=0.0, posinf=10000.0, neginf=-10000.0)
        return y

    def _gn(v, G=32, eps=1e-5):
        B_, C_, H_, W_ = v.shape
        g = v.reshape(B_, G, C_ // G, H_, W_)
        m = jnp.mean(g, axis=(2, 3, 4), keepdims=True)
        s = jnp.var(g, axis=(2, 3, 4), keepdims=True)
        return ((g - m) / jnp.sqrt(s + eps)).reshape(v.shape)

    def _ln_c(v, eps=1e-6):
        m = jnp.mean(v, axis=1, keepdims=True)
        s = jnp.var(v, axis=1, keepdims=True)
        return (v - m) / jnp.sqrt(s + eps)

    def _ln_t(v, eps=1e-5):
        m = jnp.mean(v, axis=-1, keepdims=True)
        s = jnp.var(v, axis=-1, keepdims=True)
        return (v - m) / jnp.sqrt(s + eps)

    def _to_tokens(v):
        B_, C_, H_, W_ = v.shape
        return v.reshape(B_, C_, H_ * W_).transpose(0, 2, 1)
    def _from_tokens(t, like):
        B_, C_, H_, W_ = like.shape
        return t.transpose(0, 2, 1).reshape(B_, C_, H_, W_)

    x = x + _L0_conv_ref(_gn(x), L0_conv_qw, L0_conv_kw, L0_conv_vw, L0_conv_c1w, L0_conv_c1b, L0_conv_gnw, L0_conv_gnb)
    t = _to_tokens(x)
    t = t + _L1_attn_ref(_ln_t(t), L1_attn_in_proj_w, L1_attn_conv_w, L1_attn_conv_b, L1_attn_x_proj_w, L1_attn_dt_proj_w, L1_attn_dt_proj_b, L1_attn_A_log, L1_attn_Dp, L1_attn_out_proj_w, L1_attn_ln_g, L1_attn_ln_b, L1_attn_w1, L1_attn_b1, L1_attn_w2, L1_attn_b2)
    t = t + _L1_ffn_ref(_ln_t(t), L1_ffn_gate_w, L1_ffn_gate_b, L1_ffn_w1, L1_ffn_b1, L1_ffn_w2, L1_ffn_b2)
    x = _from_tokens(t, x)
    return x


_drawn_inputs = setup_inputs


def setup_inputs(seed=0):
    import zlib

    import numpy as np

    out = dict(_drawn_inputs(seed))
    spreads = {'L0_conv_c1b': (0.0, 0.8),
     'L0_conv_gnw': (1.0, 0.6),
     'L0_conv_gnb': (0.0, 0.8),
     'L1_attn_ln_g': (1.0, 0.6),
     'L1_attn_ln_b': (0.0, 0.39),
     'L1_attn_b1': (0.0, 0.1),
     'L1_attn_b2': (0.0, 0.1),
     'L1_ffn_gate_b': (0.0, 0.1),
     'L1_ffn_b1': (0.0, 0.595),
     'L1_ffn_b2': (0.0, 0.417)}
    factors = {'L0_conv_qw': 8.0,
     'L0_conv_kw': 3.951,
     'L0_conv_vw': 3.266,
     'L0_conv_c1w': 8.0,
     'L1_attn_conv_b': 2.898,
     'L1_attn_x_proj_w': 8.0,
     'L1_attn_dt_proj_w': 8.0,
     'L1_attn_dt_proj_b': 52.674,
     'L1_attn_A_log': 40.591}
    for name, (base, spread) in spreads.items():
        noise = np.random.default_rng([zlib.crc32(name.encode()), seed]).standard_normal(out[name].shape)
        drawn = base * np.exp(spread * noise) if base else spread * noise
        out[name] = jnp.asarray(drawn.astype(out[name].dtype))
    for name, factor in factors.items():
        out[name] = (out[name] * factor).astype(out[name].dtype)
    return out
```

```python
import concourse.bass as bass
from concourse import mybir
from contextlib import ExitStack

F32 = mybir.dt.float32
BF16 = mybir.dt.bfloat16
U32 = mybir.dt.uint32
I32 = mybir.dt.int32
ALU = mybir.AluOpType
ACT = mybir.ActivationFunctionType
AX = mybir.AxisListType
ds = bass.ds

P = 128
B, C, IMG = 2, 256, 64
L = IMG * IMG
HEADS = 8
DH = 64
PAIRS = HEADS // 2
PAD = IMG + 2
CH = 512
NCH = L // CH
QT = L // P
EXPERTS = 8
CAP = 1280
GN_EPS = 1e-5
FLT_MAX = 3.4028234663852886e38


def scratch(nc, name, shape, dt=F32):
    return nc.dram_tensor(name, shape, dt, kind="Internal").ap()


def stand(eng, sem):
    eng.sem_inc(sem, 1)


def phase_semaphores(nc, ctx, prefix):
    taken = []

    def put_back():
        with nc.Block() as block:
            @block.gpsimd
            def _(pool):
                for s in taken:
                    pool.sem_clear(s)
        for s in taken:
            nc.release_semaphore(s)

    def sem(name):
        taken.append(nc.alloc_semaphore(prefix + name))
        return taken[-1]

    ctx.callback(put_back)
    return sem


def conv_phase(nc, ctx, ident, x, qw, kw, vw, c1w, c1b, gnw, gnb, q_split, k_split, v_split):
    def sb(name, shape, dt=F32):
        return ctx.enter_context(nc.sbuf_tensor(name, shape, dt))

    sem = phase_semaphores(nc, ctx, "")

    wq, wk, wv = sb("wq", [P, 9, P]), sb("wk", [P, 9, P]), sb("wv", [P, 9, P])
    wc1 = sb("wc1", [P, P])
    vecs = sb("conv_vecs", [P, 3])
    group8 = sb("group8", [P, P])
    eps = sb("conv_eps", [P, 1])
    ximg = sb("ximg", [P, L])
    xpad = sb("xpad", [P, PAD, PAD])
    gated = sb("gated", [P, L])
    resid = sb("resid", [P, L])
    qp = [sb(f"q_part{n}", [P, L], BF16) for n in range(3)]
    kp = [sb(f"k_part{n}", [P, L], BF16) for n in range(3)]
    vparts = sb("v_parts", [P, 2, QT, 2 * DH], BF16)
    vc = sb("v_chunk", [P, 2, CH])
    kres = sb("k_resid", [P, 2, CH])
    stats = sb("conv_stats", [P, NCH, 6])
    mv = sb("conv_mv", [P, 2])
    chan = sb("chan", [P, 2])
    grp = sb("grp", [P, 2])
    col = sb("conv_cols", [P, 8])
    colsum = sb("colsum", [P, 3, PAD])
    rowsum = sb("rowsum", [P, 3, PAD])
    cat = sb("cat", [P, 2 * IMG])
    gates = sb("gates", [P, 2 * IMG])
    ps_g = ctx.enter_context(nc.psum_tensor("ps_g", [P, 2], F32))
    ps_k = ctx.enter_context(nc.psum_tensor("ps_k", [P, 2, CH], F32))
    ps_q = ctx.enter_context(nc.psum_tensor("ps_q", [P, 2 * IMG], F32))
    ps_c = ctx.enter_context(nc.psum_tensor("ps_c", [P, 2 * IMG], F32))
    ps_v = ctx.enter_context(nc.psum_tensor("ps_v", [P, 2, CH], F32))

    w_ready = sem("conv_w_ready")
    zeroed = sem("conv_zeroed")
    stood = sem("conv_stood")
    x_loaded = sem("x_loaded")
    stored = sem("conv_stored")
    dve_step = sem("conv_dve_step")
    chan_ready, grp_summed, var_ready, std_ready = (sem(n) for n in ("chan_ready", "grp_summed", "var_ready", "std_ready"))
    affine_ready, xn_ready, sums_ready, q_summed = (sem(n) for n in ("affine_ready", "xn_ready", "sums_ready", "q_summed"))
    cat_ready, c1_done, gates_ready = sem("cat_ready"), sem("c1_done"), sem("gates_ready")
    var2_ready, std2_ready, qaff_ready = sem("var2_ready"), sem("std2_ready"), sem("qaff_ready")
    vc_ready, v_turned = sem("vc_ready"), sem("v_turned")
    k_summed, k1_ready, kres_ready, k2_ready, k3_ready = (sem(n) for n in ("k_summed", "k1_ready", "kres_ready", "k2_ready", "k3_ready"))
    v_summed, v1_ready, v2_ready = sem("v_summed"), sem("v1_ready"), sem("v2_ready")
    q_ready, q1_ready, qres_ready, q2_ready, q3_ready = (sem(n) for n in ("q_ready", "q1_ready", "qres_ready", "q2_ready", "q3_ready"))

    inner = xpad[:, 1:IMG + 1, 1:IMG + 1]
    image = lambda t: t[:, :].rearrange("p (h w) -> p h w", w=IMG)
    STORES = 7
    TILE_GROUPS = QT // 4

    with nc.Block() as block:
        @block.gpsimd
        def _(pool):
            for t in (wq[:, :, :], wk[:, :, :], wv[:, :, :], wc1[:, :], xpad[:, :, :], colsum[:, :, :], rowsum[:, :, :]):
                pool.memset(t, 0.0).then_inc(zeroed, 1)
            pool.memset(eps[:, :], GN_EPS).then_inc(zeroed, 1)
            pool.memset(group8[:, :], 0.125).then_inc(zeroed, 1)
            pool.wait_ge(zeroed, 9)
            blocks = group8[:, :].rearrange("p (a b) -> p a b", b=8)
            pool.affine_select(out=blocks, in_=blocks, compare_op=ALU.is_ge, fill=0.0, base=0,
                               pattern=[[-8, 16], [0, 8]], channel_multiplier=1).then_inc(zeroed, 1)
            pool.wait_ge(zeroed, 10)
            pool.affine_select(out=blocks, in_=blocks, compare_op=ALU.is_ge, fill=0.0, base=7,
                               pattern=[[8, 16], [0, 8]], channel_multiplier=-1).then_inc(zeroed, 1)

        @block.sync
        def _(sp):
            sp.wait_ge(zeroed, 9)
            n = 0
            for dst, src in ((wk, kw), (wv, vw), (wq, qw)):
                for j in range(8):
                    sp.dma_start(dst[16 * j:16 * j + 16, :, 16 * j:16 * j + 16], src[j % 4]).then_inc(w_ready, 16)
                    n += 1
            for h in range(2):
                rows = slice(DH * h, DH * h + DH)
                sp.dma_start(wc1[rows, rows], c1w).then_inc(w_ready, 16)
                for j, v in enumerate((c1b, gnw, gnb)):
                    sp.dma_start(vecs[rows, j:j + 1], v.unsqueeze(1)).then_inc(w_ready, 16)
                n += 4
            assert n == N_CONV_W
            with sp.Fori(0, PAIRS) as i:
                sp.wait_ge(gates_ready, i)
                sp.wait_ge(xn_ready, i)
                stand(sp, stood)
                sp.dma_start(ximg[:, :], x[ds(i * P, P), :]).then_inc(x_loaded, 16)
                sp.wait_ge(k3_ready, (i + 1) * NCH)
                sp.wait_ge(k2_ready, (i + 1) * NCH)
                stand(sp, stood)
                for n in range(3):
                    sp.dma_start(k_split[n, ds(i * P, P), :], kp[n][:, :]).then_inc(stored, 16)
                sp.wait_ge(v2_ready, (i + 1) * TILE_GROUPS + 2)
                stand(sp, stood)
                sp.dma_start(v_split[ds(i * 2, 2)].rearrange("h p n -> p h n"),
                             vparts[:, :, :, :].rearrange("p h t c -> p h (t c)")).then_inc(stored, 16)
                sp.wait_ge(q3_ready, i + 1)
                stand(sp, stood)
                for n in range(3):
                    sp.dma_start(q_split[n, ds(i * P, P), :], qp[n][:, :]).then_inc(stored, 16)
            sp.wait_ge(stored, 16 * STORES * PAIRS)

        @block.tensor
        def _(pe):
            pe.wait_ge(w_ready, 16 * N_CONV_W)
            pe.wait_ge(zeroed, 11)
            with pe.Fori(0, PAIRS) as i:
                pe.wait_ge(chan_ready, i + 1)
                pe.matmul(ps_g[:, :], group8[:, :], chan[:, :], start=True, stop=True).then_inc(grp_summed, 1)
                pe.wait_ge(xn_ready, i + 1)
                for c in range(NCH):
                    if c < 2:
                        pe.wait_ge(vc_ready, i * NCH)
                    else:
                        pe.wait_ge(kres_ready, i * NCH + c - 1)
                    for t in range(9):
                        dy, dx = divmod(t, 3)
                        last = pe.matmul(ps_k[:, c % 2, :], wk[:, t, :],
                                         xpad[:, 8 * c + dy:8 * c + dy + 8, dx:dx + IMG],
                                         start=(t == 0), stop=(t == 8))
                    last.then_inc(k_summed, 1)
                pe.wait_ge(sums_ready, 2 * (i + 1))
                for t in range(9):
                    dy, dx = divmod(t, 3)
                    pe.matmul(ps_q[:, 0:IMG], wq[:, t, :], colsum[:, dy, dx:dx + IMG], start=(t == 0), stop=(t == 8))
                for t in range(9):
                    dy, dx = divmod(t, 3)
                    last = pe.matmul(ps_q[:, IMG:2 * IMG], wq[:, t, :], rowsum[:, dx, dy:dy + IMG],
                                     start=(t == 0), stop=(t == 8))
                last.then_inc(q_summed, 1)
                for c in range(NCH + 1):
                    if c == 2:
                        pe.wait_ge(cat_ready, i + 1)
                        pe.matmul(ps_c[:, :], wc1[:, :], cat[:, :], start=True, stop=True).then_inc(c1_done, 1)
                    if c < NCH:
                        if c < 2:
                            pe.wait_ge(kres_ready, i * NCH + NCH - 1 + c)
                        else:
                            pe.wait_ge(vc_ready, i * NCH + c - 1)
                        for t in range(9):
                            dy, dx = divmod(t, 3)
                            last = pe.matmul(ps_k[:, c % 2, :], wv[:, t, :],
                                             xpad[:, 8 * c + dy:8 * c + dy + 8, dx:dx + IMG],
                                             start=(t == 0), stop=(t == 8))
                        last.then_inc(v_summed, 1)
                    if c:
                        pe.wait_ge(vc_ready, i * NCH + c)
                        pe.wait_ge(v2_ready, i * NCH + c)
                        for k in range(4):
                            last = pe.transpose(ps_v[:, (c - 1) % 2, k * P:(k + 1) * P],
                                                vc[:, (c - 1) % 2, k * P:(k + 1) * P], ident[:, :])
                        last.then_inc(v_turned, 1)

        @block.scalar
        def _(act):
            act.wait_ge(zeroed, 11)
            act.wait_ge(w_ready, 16 * N_CONV_W)
            with act.Fori(0, PAIRS) as i:
                act.wait_ge(var_ready, i + 1)
                act.activation(col[:, 0:1], grp[:, 1:2], ACT.Sqrt, scale=-1.0, bias=eps[:, 0:1]).then_inc(std_ready, 1)
                act.wait_ge(affine_ready, i + 1)
                act.wait_ge(v_summed, i * TILE_GROUPS)
                act.activation(inner, image(ximg), ACT.Identity, scale=col[:, 1:2], bias=col[:, 2:3]).then_inc(xn_ready, 1)
                act.wait_ge(stored, i * 16 * STORES)
                for c in range(NCH):
                    cs = slice(c * CH, (c + 1) * CH)
                    act.wait_ge(k_summed, i * NCH + c + 1)
                    act.activation(kp[0][:, cs], ps_k[:, c % 2, :], ACT.Copy).then_inc(k1_ready, 1)
                    act.wait_ge(kres_ready, i * NCH + c + 1)
                    act.activation(kp[1][:, cs], kres[:, c % 2, :], ACT.Copy).then_inc(k2_ready, 1)
                act.wait_ge(q_summed, i + 1)
                act.activation(cat[:, :], ps_q[:, :], ACT.Copy, scale=1.0 / IMG).then_inc(cat_ready, 1)
                for c in range(NCH + 1):
                    if c < NCH:
                        act.wait_ge(v_summed, i * NCH + c + 1)
                        act.wait_ge(v_turned, i * NCH + c + 1)
                        act.activation(vc[:, c % 2, :], ps_k[:, c % 2, :], ACT.Copy).then_inc(vc_ready, 1)
                    if c:
                        g = c - 1
                        act.wait_ge(v_turned, i * NCH + c + 2)
                        act.activation(vparts[:, :, 4 * g:4 * g + 4, 0:DH],
                                       ps_v[:, g % 2, :].rearrange("p (t h c) -> p h t c", t=4, h=2),
                                       ACT.Copy).then_inc(v1_ready, 1)
                    if c == 3:
                        act.wait_ge(c1_done, i + 1)
                        act.activation(gates[:, :], ps_c[:, :], ACT.Sigmoid, bias=vecs[:, 0:1]).then_inc(gates_ready, 1)
                act.wait_ge(var2_ready, i + 1)
                act.activation(col[:, 3:4], mv[:, 1:2], ACT.Sqrt, bias=eps[:, 0:1]).then_inc(std2_ready, 1)
                act.wait_ge(qaff_ready, i + 1)
                act.activation(gated[:, :], gated[:, :], ACT.Identity, scale=col[:, 5:6], bias=col[:, 6:7]).then_inc(q_ready, 1)
                act.wait_ge(q_ready, i + 1)
                act.activation(qp[0][:, :], gated[:, :], ACT.Copy).then_inc(q1_ready, 1)
                act.wait_ge(qres_ready, i + 1)
                act.activation(qp[1][:, :], resid[:, :], ACT.Copy).then_inc(q2_ready, 1)

        @block.vector
        def _(dve):
            STEPS = 16
            dve.sem_inc(v_turned, 2)
            dve.sem_inc(v2_ready, 2)
            dve.wait_ge(zeroed, 11)
            dve.wait_ge(w_ready, 16 * N_CONV_W)
            with dve.Fori(0, PAIRS) as i:
                n = [0]

                def link(ins):
                    n[0] += 1
                    ins.then_inc(dve_step, 1)
                    dve.wait_ge(dve_step, i * STEPS + n[0])

                def channel_stats(t):
                    for c in range(NCH):
                        last = dve.bn_stats(stats[:, c, :], t[:, c * CH:(c + 1) * CH])
                    link(last)

                dve.wait_ge(x_loaded, (i + 1) * 16)
                channel_stats(ximg)
                stand(dve, stood)
                link(dve.bn_aggr(mv[:, :], stats[:, :, :].rearrange("p a b -> p (a b)")))
                dve.tensor_copy(chan[:, 0:1], mv[:, 0:1])
                dve.scalar_tensor_tensor(chan[:, 1:2], mv[:, 0:1], mv[:, 0:1], mv[:, 1:2],
                                         ALU.mult, ALU.add).then_inc(chan_ready, 1)
                dve.wait_ge(grp_summed, i + 1)
                link(dve.tensor_copy(grp[:, :], ps_g[:, :]))
                link(dve.tensor_tensor(col[:, 7:8], grp[:, 0:1], grp[:, 0:1], ALU.mult))
                dve.tensor_tensor(grp[:, 1:2], col[:, 7:8], grp[:, 1:2], ALU.subtract).then_inc(var_ready, 1)
                dve.wait_ge(std_ready, i + 1)
                link(dve.reciprocal(col[:, 1:2], col[:, 0:1]))
                dve.tensor_scalar(col[:, 2:3], grp[:, 0:1], -1.0, col[:, 1:2], ALU.mult, ALU.mult).then_inc(affine_ready, 1)
                dve.wait_ge(xn_ready, i + 1)
                dve.tensor_reduce(colsum[:, 1, 1:IMG + 1], inner.rearrange("p h w -> p w h"), AX.X, ALU.add)
                link(dve.tensor_reduce(rowsum[:, 1, 1:IMG + 1], inner, AX.X, ALU.add))
                for d, edge in ((0, IMG), (2, 1)):
                    dve.tensor_tensor(colsum[:, d, 1:IMG + 1], colsum[:, 1, 1:IMG + 1], xpad[:, edge, 1:IMG + 1], ALU.subtract)
                    dve.tensor_tensor(rowsum[:, d, 1:IMG + 1], rowsum[:, 1, 1:IMG + 1], xpad[:, 1:IMG + 1, edge],
                                      ALU.subtract).then_inc(sums_ready, 1)
                dve.wait_ge(stored, i * 16 * STORES)
                for c in range(NCH + 1):
                    if c < NCH:
                        dve.wait_ge(k1_ready, i * NCH + c + 1)
                        if c > 1:
                            dve.wait_ge(k3_ready, i * NCH + c - 1)
                        dve.tensor_tensor(kres[:, c % 2, :], ps_k[:, c % 2, :], kp[0][:, c * CH:(c + 1) * CH],
                                          ALU.subtract).then_inc(kres_ready, 1)
                    if c:
                        dve.wait_ge(k2_ready, i * NCH + c)
                        cs = slice((c - 1) * CH, c * CH)
                        dve.tensor_tensor(kp[2][:, cs], kres[:, (c - 1) % 2, :], kp[1][:, cs],
                                          ALU.subtract).then_inc(k3_ready, 1)
                for g in range(TILE_GROUPS):
                    dve.wait_ge(v1_ready, i * TILE_GROUPS + g + 1)
                    dve.tensor_tensor(vparts[:, :, 4 * g:4 * g + 4, DH:2 * DH],
                                      ps_v[:, g % 2, :].rearrange("p (t h c) -> p h t c", t=4, h=2),
                                      vparts[:, :, 4 * g:4 * g + 4, 0:DH], ALU.subtract).then_inc(v2_ready, 1)
                dve.wait_ge(gates_ready, i + 1)
                link(dve.tensor_tensor(image(gated), inner, gates[:, 0:IMG].unsqueeze(1).broadcast_to([P, IMG, IMG]), ALU.mult))
                link(dve.tensor_tensor(image(gated), image(gated),
                                       gates[:, IMG:2 * IMG].unsqueeze(2).broadcast_to([P, IMG, IMG]), ALU.mult))
                channel_stats(gated)
                stand(dve, stood)
                dve.bn_aggr(mv[:, :], stats[:, :, :].rearrange("p a b -> p (a b)")).then_inc(var2_ready, 1)
                dve.wait_ge(std2_ready, i + 1)
                link(dve.reciprocal(col[:, 4:5], col[:, 3:4]))
                link(dve.tensor_tensor(col[:, 5:6], col[:, 4:5], vecs[:, 1:2], ALU.mult))
                link(dve.tensor_tensor(col[:, 7:8], mv[:, 0:1], col[:, 5:6], ALU.mult))
                dve.tensor_tensor(col[:, 6:7], vecs[:, 2:3], col[:, 7:8], ALU.subtract).then_inc(qaff_ready, 1)
                dve.wait_ge(q1_ready, i + 1)
                dve.tensor_tensor(resid[:, :], gated[:, :], qp[0][:, :], ALU.subtract).then_inc(qres_ready, 1)
                dve.wait_ge(q2_ready, i + 1)
                link(dve.tensor_tensor(qp[2][:, :], resid[:, :], qp[1][:, :], ALU.subtract))
                dve.sem_inc(q3_ready, 1)
                for _ in range(STEPS - n[0]):
                    dve.sem_inc(dve_step, 1)
                assert n[0] <= STEPS


def attention_phase(nc, ctx, ident, q_split, k_split, v_split, attn_out):
    def sb(name, shape, dt=F32):
        return ctx.enter_context(nc.sbuf_tensor(name, shape, dt))

    sem = phase_semaphores(nc, ctx, "")

    qa, qb, ka, kb, kc = ([sb(f"{n}{j}", [P, L], BF16) for j in range(2)] for n in ("q12_", "q13_", "k11_", "k22_", "k31_"))
    vv = [sb(f"v12_{j}", [P, QT, P], BF16) for j in range(2)]
    prob = [sb(f"prob{j}", [P, L]) for j in range(2)]
    hi, lo = sb("p_hi", [P, 2, CH], BF16), sb("p_lo", [P, 2, CH], BF16)
    mx, nmx = sb("mx", [P, 2, 4]), sb("nmx", [P, 2])
    rs, rsum, rinv = sb("rs", [P, 2, 4]), sb("rsum", [P, 2]), sb("rinv", [P, 2])
    otmp = sb("otmp", [P, DH])
    oh = sb("o_head", [P, 2, QT, DH])
    ps_s = ctx.enter_context(nc.psum_tensor("ps_s", [P, 2, 2 * CH], F32))
    ps_t = ctx.enter_context(nc.psum_tensor("ps_t", [P, 2, CH], F32))
    ps_o = ctx.enter_context(nc.psum_tensor("ps_o", [P, 2, CH], F32))

    loaded = [sem(f"head_loaded{j}") for j in range(2)]
    s_ready, s_copied, max_ready, exp_ready = sem("s_ready"), sem("s_copied"), sem("max_ready"), sem("exp_ready")
    t_ready, hi_ready, lo_ready, pv_done = sem("t_ready"), sem("hi_ready"), sem("lo_ready"), sem("pv_done")
    o_ready, o_stored, fin_step = sem("o_ready"), sem("o_stored"), sem("fin_step")

    LOADS = 11
    SC = L // (2 * CH)
    TG = L // CH
    scale = 1.0 / 16.0

    def tiles(eng, head, step):
        with eng.Fori(0, QT // 2 - 1) as it:
            for u in range(2):
                step(head * QT + it * 2 + u, it * 2 + u, u, False)
        step(head * QT + QT - 2, QT - 2, 0, False)
        step(head * QT + QT - 1, QT - 1, 1, True)

    def heads(eng, body):
        with eng.Fori(0, HEADS // 2) as hp:
            for j in range(2):
                body(hp * 2 + j, j, hp)

    with nc.Block() as block:
        @block.sync
        def _(sp):
            def load(h, j):
                rows = ds(h * DH, DH)
                top, bottom = slice(0, DH), slice(DH, P)
                for dst, part, src in ((qa[j][top], 0, q_split), (qa[j][bottom], 1, q_split),
                                       (ka[j][top], 0, k_split), (ka[j][bottom], 0, k_split),
                                       (kb[j][top], 1, k_split), (kb[j][bottom], 1, k_split),
                                       (qb[j][top], 0, q_split), (qb[j][bottom], 2, q_split),
                                       (kc[j][top], 2, k_split), (kc[j][bottom], 0, k_split)):
                    sp.dma_start(dst, src[part, rows, :]).then_inc(loaded[j], 16)
                sp.dma_start(vv[j][:, :, :].rearrange("p t c -> p (t c)"), v_split[h]).then_inc(loaded[j], 16)

            def store(h, j):
                sp.wait_ge(o_ready, (h + 1) * QT)
                sp.dma_start(attn_out[h], oh[:, j, :, :].rearrange("p t c -> p (t c)")).then_inc(o_stored, 16)

            load(0, 0)
            load(1, 1)
            with sp.Fori(1, HEADS // 2) as hp:
                for j in range(2):
                    store(hp * 2 + j - 2, j)
                    load(hp * 2 + j, j)
            store(HEADS - 2, 0)
            store(HEADS - 1, 1)
            sp.wait_ge(o_stored, 16 * HEADS)

        @block.tensor
        def _(pe):
            def head(h, j, hp):
                def scores(g, t, u, c):
                    pe.wait_ge(s_copied, g * SC + c + 1)
                    for half in range(2):
                        keys = slice((2 * c + half) * CH, (2 * c + half + 1) * CH)
                        for n, (a, b) in enumerate(((qa, ka), (qa, kb), (qb, kc))):
                            last = pe.matmul(ps_s[:, c % 2, half * CH:(half + 1) * CH], a[j][:, ds(t * P, P)],
                                             b[j][:, keys], start=(n == 0), stop=(n == 2))
                    last.then_inc(s_ready, 1)

                def transposes(g, t, u, k):
                    pe.wait_ge(exp_ready, g * SC + k // 2 + 1)
                    pe.wait_ge(lo_ready, g * TG + k + 1)
                    for m in range(4):
                        last = pe.transpose(ps_t[:, k % 2, m * P:(m + 1) * P],
                                            prob[u][:, (4 * k + m) * P:(4 * k + m + 1) * P], ident[:, :])
                    last.then_inc(t_ready, 1)

                def values(g, t, u, k):
                    pe.wait_ge(lo_ready, g * TG + k + 3)
                    if k == 0:
                        pe.wait_ge(o_ready, g)
                    for m in range(4):
                        for n, part in enumerate((hi, lo)):
                            last = pe.matmul(ps_o[:, u, 0:P], part[:, k % 2, m * P:(m + 1) * P], vv[j][:, 4 * k + m, :],
                                             start=(k == 0 and m == 0 and n == 0), stop=(k == TG - 1 and m == 3 and n == 1))
                    last.then_inc(pv_done, 1)

                def step(g, t, u, final):
                    nxt = (g + 1, t + 1, 1 - u)
                    if not final:
                        scores(*nxt, 0)
                        scores(*nxt, 1)
                    transposes(g, t, u, 0)
                    transposes(g, t, u, 1)
                    if not final:
                        scores(*nxt, 2)
                    for k in range(2, TG):
                        values(g, t, u, k - 2)
                        transposes(g, t, u, k)
                    if not final:
                        scores(*nxt, 3)
                    values(g, t, u, TG - 2)
                    values(g, t, u, TG - 1)

                pe.wait_ge(loaded[j], (hp + 1) * 16 * LOADS)
                for c in range(SC):
                    scores(h * QT, 0, 0, c)
                tiles(pe, h, step)

            heads(pe, head)

        @block.scalar
        def _(act):
            def step(g, t, u, final):
                def exps(c):
                    cs = slice(c * 2 * CH, (c + 1) * 2 * CH)
                    act.activation(prob[u][:, cs], prob[u][:, cs], ACT.Exp, bias=nmx[:, u:u + 1],
                                   accum_out=rs[:, u, c:c + 1]).then_inc(exp_ready, 1)

                def his(k):
                    act.wait_ge(t_ready, g * TG + k + 1)
                    act.wait_ge(pv_done, g * TG + k + 1)
                    act.activation(hi[:, k % 2, :], ps_t[:, k % 2, :], ACT.Copy).then_inc(hi_ready, 1)

                act.wait_ge(max_ready, g + 1)
                exps(0)
                exps(1)
                his(0)
                his(1)
                exps(2)
                his(2)
                his(3)
                exps(3)
                for k in range(4, TG):
                    his(k)

            act.preload_act_table(ACT.Exp)
            heads(act, lambda h, j, hp: tiles(act, h, step))

        @block.vector
        def _(dve):
            def head(h, j, hp):
                def copies(g, u, c):
                    dve.wait_ge(s_ready, g * SC + c + 1)
                    dve.tensor_scalar(prob[u][:, c * 2 * CH:(c + 1) * 2 * CH], ps_s[:, c % 2, :], scale, -FLT_MAX,
                                      ALU.mult, ALU.max, accum_out=mx[:, u, c:c + 1]).then_inc(s_copied, 1)

                def maximum(g, u):
                    dve.wait_ge(s_copied, g * SC + SC + 2)
                    dve.tensor_reduce(nmx[:, u:u + 1], mx[:, u, :], AX.X, ALU.max, negate=True).then_inc(max_ready, 1)

                def los(g, u, k):
                    dve.wait_ge(hi_ready, g * TG + k + 1)
                    dve.tensor_tensor(lo[:, k % 2, :], ps_t[:, k % 2, :], hi[:, k % 2, :], ALU.subtract).then_inc(lo_ready, 1)

                def finish(g, t, u):
                    dve.tensor_reduce(rsum[:, u:u + 1], rs[:, u, :], AX.X, ALU.add).then_inc(fin_step, 1)
                    dve.wait_ge(fin_step, g * 3 + 1)
                    dve.reciprocal(rinv[:, u:u + 1], rsum[:, u:u + 1]).then_inc(fin_step, 1)
                    dve.wait_ge(fin_step, g * 3 + 2)
                    dve.wait_ge(pv_done, (g + 1) * TG + 2)
                    dve.tensor_scalar(otmp[:, :], ps_o[:, u, DH:P], rinv[:, u:u + 1], None, ALU.mult).then_inc(fin_step, 1)
                    dve.wait_ge(fin_step, g * 3 + 3)
                    dve.scalar_tensor_tensor(oh[:, j, ds(t, 1), :].rearrange("p a c -> p (a c)"), ps_o[:, u, 0:DH],
                                             rinv[:, u:u + 1], otmp[:, :], ALU.mult, ALU.add).then_inc(o_ready, 1)

                def step(g, t, u, final):
                    if not final:
                        copies(g + 1, 1 - u, 0)
                        copies(g + 1, 1 - u, 1)
                    los(g, u, 0)
                    los(g, u, 1)
                    if not final:
                        copies(g + 1, 1 - u, 2)
                    for k in range(2, TG):
                        los(g, u, k)
                    if not final:
                        copies(g + 1, 1 - u, 3)
                        maximum(g + 1, 1 - u)
                    finish(g, t, u)

                if j == 0:
                    dve.wait_ge(o_stored, hp * 32)
                for c in range(SC):
                    copies(h * QT, 0, c)
                maximum(h * QT, 0)
                tiles(dve, h, step)

            dve.sem_inc(s_copied, 2)
            dve.sem_inc(lo_ready, 2)
            dve.sem_inc(pv_done, 2)
            heads(dve, head)


def tokens_phase(nc, ctx, ident, x, attn_out, t1, u1):
    def sb(name, shape, dt=F32):
        return ctx.enter_context(nc.sbuf_tensor(name, shape, dt))

    sem = phase_semaphores(nc, ctx, "")

    xin = sb("tk_x", [P, 2, 2, CH])
    oin = sb("tk_o", [P, 2, 4, 4 * DH])
    tt = sb("tk_t", [P, 2, 4, C])
    nt = sb("tk_n", [P, 2, 4, C])
    ut = sb("tk_u", [P, 2, 2, CH])
    stats, mv = sb("tk_stats", [P, 4, 6]), sb("tk_mv", [P, 4, 2])
    std, rstd, eps = sb("tk_std", [P, 4]), sb("tk_rstd", [P, 4]), sb("tk_eps", [P, 1])
    ps_x = ctx.enter_context(nc.psum_tensor("tk_ps_x", [P, 2, 2, CH], F32))
    ps_u = ctx.enter_context(nc.psum_tensor("tk_ps_u", [P, 2, 2, CH], F32))
    eps_ready = sem("tk_eps_ready")
    in_loaded = [sem(f"tk_in_loaded{j}") for j in range(2)]
    x_turned, t_ready, stats_step, var_ready, std_ready = (sem(f"tk_{n}") for n in ("x_turned", "t_ready", "stats_step", "var_ready", "std_ready"))
    n_ready, u_turned, u_ready, stored, stood = (sem(f"tk_{n}") for n in ("n_ready", "u_turned", "u_ready", "stored", "stood"))
    N = B * NCH

    def chunks(eng, body):
        with eng.Fori(0, B) as b:
            with eng.Fori(0, NCH // 2) as h:
                for j in range(2):
                    body(b * NCH + h * 2 + j, j, b, h * 2 + j)

    with nc.Block() as block:
        @block.sync
        def _(sp):
            def body(n, j, b, c):
                sp.wait_ge(t_ready, n * 2)
                stand(sp, stood)
                sp.dma_start(xin[:, j, :, :], x[ds(b * C, C), ds(c * CH, CH)].rearrange("(k p) l -> p k l", p=P)).then_inc(in_loaded[j], 16)
                sp.dma_start(oin[:, j, :, :], attn_out[ds(b * 4, 4), :, ds(c * 4 * DH, 4 * DH)].rearrange("g p n -> p g n")).then_inc(in_loaded[j], 16)
                sp.wait_ge(t_ready, n * 2 + 6)
                stand(sp, stood)
                sp.dma_start(t1[n], tt[:, j, :, :].rearrange("p t c -> p (t c)")).then_inc(stored, 16)
                sp.wait_ge(u_ready, n + 1)
                stand(sp, stood)
                sp.dma_start(u1[n], ut[:, j, :, :].rearrange("p k l -> p (k l)")).then_inc(stored, 16)
            chunks(sp, body)
            sp.wait_ge(stored, 32 * N)

        @block.tensor
        def _(pe):
            def body(n, j, b, c):
                pe.wait_ge(in_loaded[j], b * (16 * NCH) + (c - j) * 16 + 32)
                pe.wait_ge(t_ready, n * 2)
                for t in range(4):
                    for k in range(2):
                        last = pe.transpose(ps_x[:, j, t // 2, (t % 2) * C + k * P:(t % 2) * C + (k + 1) * P],
                                            xin[:, j, k, t * P:(t + 1) * P], ident[:, :])
                last.then_inc(x_turned, 1)
                pe.wait_ge(n_ready, n + 1)
                pe.wait_ge(u_ready, n)
                for t in range(4):
                    for k in range(2):
                        last = pe.transpose(ps_u[:, j, k, t * P:(t + 1) * P], nt[:, j, t, k * P:(k + 1) * P], ident[:, :])
                last.then_inc(u_turned, 1)
            chunks(pe, body)

        @block.scalar
        def _(act):
            def body(n, j, b, c):
                act.wait_ge(var_ready, n + 1)
                act.activation(std[:, :], mv[:, :, 1], ACT.Sqrt, bias=eps[:, 0:1]).then_inc(std_ready, 1)
                act.wait_ge(u_turned, n + 1)
                act.wait_ge(stored, n * 32)
                act.activation(ut[:, j, :, :], ps_u[:, j, :, :], ACT.Copy).then_inc(u_ready, 1)
            act.wait_ge(eps_ready, 1)
            chunks(act, body)

        @block.vector
        def _(dve):
            def body(n, j, b, c):
                dve.wait_ge(x_turned, n + 1)
                dve.wait_ge(stored, n * 32)
                for h in range(2):
                    o = oin[:, j, :, :].rearrange("p g (t c) -> p t g c", t=4)[:, 2 * h:2 * h + 2]
                    dve.tensor_tensor(tt[:, j, 2 * h:2 * h + 2, :].rearrange("p t (g c) -> p t g c", g=4),
                                      ps_x[:, j, h, :].rearrange("p (t g c) -> p t g c", t=2, g=4), o, ALU.add).then_inc(t_ready, 1)
                dve.wait_ge(t_ready, n * 2 + 6)
                for t in range(4):
                    last = dve.bn_stats(stats[:, t, :], tt[:, j, t, :])
                last.then_inc(stats_step, 1)
                dve.wait_ge(stats_step, n * 2 + 1)
                stand(dve, stood)
                for t in range(4):
                    last = dve.bn_aggr(mv[:, t, :], stats[:, t, :])
                last.then_inc(var_ready, 1)
                dve.wait_ge(std_ready, n + 1)
                dve.reciprocal(rstd[:, :], std[:, :]).then_inc(stats_step, 1)
                dve.wait_ge(stats_step, n * 2 + 2)
                dve.wait_ge(u_turned, n)
                for t in range(4):
                    last = dve.tensor_scalar(nt[:, j, t, :], tt[:, j, t, :], mv[:, t, 0:1], rstd[:, t:t + 1],
                                             ALU.subtract, ALU.mult)
                last.then_inc(n_ready, 1)
            dve.memset(eps[:, :], GN_EPS).then_inc(eps_ready, 1)
            dve.sem_inc(t_ready, 4)
            chunks(dve, body)


def mamba_phase(nc, ctx, ident, w, u1, m_dirs):
    def sb(name, shape, dt=F32):
        return ctx.enter_context(nc.sbuf_tensor(name, shape, dt))

    sem = phase_semaphores(nc, ctx, "mb_")

    N = B * NCH
    K = 4
    S = 16
    R = 16
    BC = 2 * S
    NX = 3 * BC + R
    W = CH + 3

    win = sb("win", [P, 2, 2, 8 * P])
    wx = sb("wx", [P, 2, K, NX])
    wdt = sb("wdt", [NX, 2, K * P])
    wout = sb("wout", [P, 2, K, C])
    cw, cb = sb("cw", [P, 2, K, 4]), sb("cb", [P, 2, K])
    dtb, dskip = sb("dtb", [P, 2, K]), sb("dskip", [P, 2, K])
    amat = sb("amat", [P, 2, K, S])
    keep = sb("keep", [P, N])
    one = sb("one", [P, 1])
    u = sb("mb_u", [P, 2, 2, CH])
    xpre = sb("xpre", [P, K, W])
    halo = sb("halo", [P, 2, K, 3])
    xs = sb("xs", [P, 2, K, CH])
    zs = sb("zs", [P, 2, K, CH])
    dt = sb("dt", [P, 2, K, CH])
    dtx = sb("dtx", [P, 2, K, CH])
    sp_tmp = sb("sp_tmp", [P, K, CH])
    xdt = sb("xdt", [NX, CH])
    xbc = sb("xbc", [3 * BC, 2, CH], BF16)
    xres = sb("xres", [3 * BC, CH])
    pick = sb("pick", [3 * BC, BC], BF16)
    bb, cc = sb("bb", [P, 4, CH]), sb("cc", [P, 4, CH])
    da = sb("da", [P, 2, K, CH])
    hh = sb("hh", [P, 4, K, CH])
    state = sb("state", [P, 2, K, S])
    mo = sb("mo", [P, 4, C])
    ps_a = ctx.enter_context(nc.psum_tensor("mb_ps_a", [P, 2, CH], F32))
    ps_b = ctx.enter_context(nc.psum_tensor("mb_ps_b", [P, 2, CH], F32))
    ps_y = ctx.enter_context(nc.psum_tensor("mb_ps_y", [P, K, CH], F32))

    w_loaded, consts, a_exp, a_neg = sem("w_loaded"), sem("consts"), sem("a_exp"), sem("a_neg")
    u_loaded = [sem(f"u_loaded{j}") for j in range(2)]
    a_ready, a_free = sem("a_ready"), sem("a_free")
    bc_ready, bc_copied = sem("bc_ready"), sem("bc_copied")
    conv_step, conv_done, silu_done, soft_step, soft_done = (sem(n) for n in ("conv_step", "conv_done", "silu_done", "soft_step", "soft_done"))
    x_part1, x_res1, x_part2, x_split = (sem(n) for n in ("x_part1", "x_res1", "x_part2", "x_split"))
    dt_ready, dtx_ready = sem("dt_ready"), sem("dtx_ready")
    da_ready, dbx_ready, scanned, saved, hc_ready, summed = (sem(n) for n in ("da_ready", "dbx_ready", "scanned", "saved", "hc_ready", "summed"))
    kept, y_ready, gated, mo_stored, stood, out_copied = (sem(n) for n in ("kept", "y_ready", "gated", "mo_stored", "stood", "out_copied"))

    USES = 15

    AHEAD = 3
    N_CONSTS = 9

    class Step:
        def __init__(s, n, j, tail=True, front=True):
            s.n, s.j, s.tail, s.front = n, j, tail, front
            s.k = n * 2 + j
            s.use0, s.bank0 = s.k * USES + USES - 4, (j + 1) % 2
            s.nj, s.nn = 1 - j, n + j
            s.fronts = s.k + 1
            s.scanning = True

    def before():
        s = Step(0, 0)
        s.k, s.use0, s.bank0, s.nj, s.nn = -1, -2, 0, 0, 0
        s.scanning = False
        return s

    def after():
        s = Step(N, 0)
        s.use0, s.bank0 = s.use0 - (USES - 2), (s.bank0 + USES - 2) % 2
        s.fronts = s.k
        return s

    def run(eng, begin, step, end):
        begin(before())
        step(Step(0, 0, tail=False))
        step(Step(0, 1))
        with eng.Fori(1, N - 1) as n:
            for j in range(2):
                step(Step(n, j))
        step(Step(N - 1, 0))
        step(Step(N - 1, 1, front=False))
        end(after())

    def bank(s, idx):
        return (s.bank0 + idx) % 2

    with nc.Block() as block:
        @block.sync
        def _(sp):
            n = 0
            for dst, src in ((win[:, :, :, :], w["in_proj_w"].rearrange("j k p e -> p j k e")),
                             (wx[:, :, :, 0:BC], w["x_proj_w"][:, :, :, R:].rearrange("j k p e -> p j k e")),
                             (wx[:, :, :, BC:2 * BC], w["x_proj_w"][:, :, :, R:].rearrange("j k p e -> p j k e")),
                             (wx[:, :, :, 2 * BC:3 * BC], w["x_proj_w"][:, :, :, R:].rearrange("j k p e -> p j k e")),
                             (wx[:, :, :, 3 * BC:NX], w["x_proj_w"][:, :, :, 0:R].rearrange("j k p e -> p j k e")),
                             (wdt[3 * BC:NX, :, :], w["dt_proj_w"].rearrange("j r d -> r j d")),
                             (wout[:, :, :, :], w["out_proj_w"].rearrange("j k p e -> p j k e")),
                             (cw[:, :, :, :], w["conv_w"].rearrange("j (k p) t -> p j k t", p=P)),
                             (amat[:, :, :, :], w["A_log"].rearrange("j (k p) s -> p j k s", p=P))):
                for j in range(2):
                    sp.dma_start(dst[:, j], src[:, j]).then_inc(w_loaded, 16)
                    n += 1
            for dst, src in ((cb, "conv_b"), (dtb, "dt_proj_b"), (dskip, "Dp")):
                for j in range(2):
                    for k in range(K):
                        sp.dma_start(dst[:, j, k:k + 1], w[src][j, k * P:(k + 1) * P].unsqueeze(1)).then_inc(w_loaded, 16)
                        n += 1
            assert n == N_MAMBA_W

            def load(k, j, n):
                sp.dma_start(u[:, j, :, :].rearrange("p k l -> p (k l)"), u1[n if j == 0 else (N - 1) - n]).then_inc(u_loaded[j], 16)

            def store(k, j, n):
                sp.wait_ge(out_copied, (k + 1) * 2)
                stand(sp, stood)
                sp.dma_start(m_dirs[j, n], mo[:, :, :].rearrange("p t c -> p (t c)")).then_inc(mo_stored, 16)

            load(0, 0, 0)
            load(1, 1, 0)
            with sp.Fori(0, N - 1) as n:
                for j in range(2):
                    sp.wait_ge(dtx_ready, n * 2 + j + 1)
                    stand(sp, stood)
                    load(n * 2 + j + 2, j, n + 1)
                    store(n * 2 + j, j, n)
            store(2 * N - 2, 0, N - 1)
            store(2 * N - 1, 1, N - 1)
            sp.wait_ge(mo_stored, 32 * N)

        @block.tensor
        def _(pe):
            def fill(s, idx, mms):
                pe.wait_ge(a_free, s.use0 + idx + 1)
                for out, lhsT, rhs, start, stop in mms(ps_a[:, bank(s, idx), :]):
                    last = pe.matmul(out, lhsT, rhs, start=start, stop=stop)
                last.then_inc(a_ready, 1)

            def in_proj(s, e):
                if e == 0:
                    pe.wait_ge(u_loaded[s.nj], (s.nn + 1) * 16)
                fill(s, 2 + e, lambda ps: [(ps, win[:, s.nj, k, e * P:(e + 1) * P], u[:, s.nj, k, :], k == 0, k == 1)
                                           for k in range(2)])

            def x_proj(s):
                pe.wait_ge(silu_done, (s.k + 2) * 2 - 1)
                fill(s, 10, lambda ps: [(ps[0:NX], wx[:, s.nj, k, :], xs[:, s.nj, k, :], k == 0, k == K - 1)
                                        for k in range(K)])

            def dt_proj(s, k):
                if k == 0:
                    pe.wait_ge(a_free, s.use0 + 13)
                fill(s, 11 + k, lambda ps: [(ps, wdt[3 * BC:NX, s.nj, k * P:(k + 1) * P], xdt[3 * BC:NX, :], True, True)])

            def spread(s, i):
                if i == S:
                    pe.wait_ge(x_split, s.k + 2)
                for n in range(2):
                    pe.wait_ge(bc_copied, s.k * 2 * S + 2 * i + n + 1)
                    row = S * n + i % S
                    pe.matmul(ps_b[:, n, :], pick[:, row:row + 1].broadcast_to([3 * BC, P]),
                              xbc[:, s.j if i < S else s.nj, :], start=True, stop=True).then_inc(bc_ready, 1)

            def accumulate(s, i):
                pe.wait_ge(hc_ready, s.k * S + i + 5)
                if i == 0:
                    pe.wait_ge(y_ready, s.k * K)
                for k in range(K):
                    last = pe.matmul(ps_y[:, k, :], ident[:, :], hh[:, i % 4, k, :], start=(i == 0), stop=(i % S == S - 1))
                last.then_inc(summed, 1)

            def tail(s):
                pe.wait_ge(gated, s.k)
                for h in range(2):
                    fill(s, h, lambda ps: [(ps[:, t * C:(t + 1) * C], sp_tmp[:, k, (2 * h + t) * P:(2 * h + t + 1) * P],
                                            wout[:, s.nj, k, :], k == 0, k == K - 1) for t in range(2) for k in range(K)])

            def front(s, slot=None):
                for at, work in ((4, lambda: [in_proj(s, e) for e in (0, 1)]), (5, lambda: [in_proj(s, e) for e in (2, 3)]),
                                 (6, lambda: [in_proj(s, e) for e in (4, 5)]), (7, lambda: [in_proj(s, e) for e in (6, 7)]),
                                 (9, lambda: x_proj(s)), (10, lambda: [dt_proj(s, k) for k in (0, 1)]),
                                 (11, lambda: [dt_proj(s, k) for k in (2, 3)])):
                    if slot in (None, at):
                        work()

            def step(s):
                for i in range(S):
                    if i + AHEAD < S or s.front:
                        spread(s, i + AHEAD)
                    if i or s.tail:
                        accumulate(s, i - 1)
                    if i == 3 and s.tail:
                        tail(s)
                    if s.front:
                        front(s, i)

            def begin(s):
                front(s)
                for i in range(AHEAD):
                    spread(s, S + i)

            def end(s):
                accumulate(s, -1)
                tail(s)

            pe.wait_ge(consts, N_CONSTS)
            pe.wait_ge(w_loaded, 16 * N_MAMBA_W)
            run(pe, begin, step, end)

        @block.scalar
        def _(act):
            def data(j):
                return slice(3, W) if j == 0 else slice(0, CH)

            def in_copy(s, e):
                act.wait_ge(a_ready, s.use0 + 2 + e + 1)
                if e == 0:
                    act.wait_ge(conv_done, s.k + 1)
                dst = xpre[:, e, data(s.nj)] if e < K else zs[:, s.nj, e - K, :]
                act.activation(dst, ps_a[:, bank(s, 2 + e), :], ACT.Copy).then_inc(a_free, 1)

            def silus(s):
                act.wait_ge(conv_done, s.k + 2)
                act.activation(xs[:, s.nj], xs[:, s.nj], ACT.Silu).then_inc(silu_done, 1)
                act.wait_ge(a_free, s.use0 + 2 + 8 + 2)
                act.activation(zs[:, s.nj], zs[:, s.nj], ACT.Silu).then_inc(silu_done, 1)
                act.preload_act_table_set("natural_log_exp_and_others")

            def x_copy(s):
                act.wait_ge(a_ready, s.use0 + 11)
                act.activation(xbc[:, s.nj, :], ps_a[0:3 * BC, bank(s, 10), :], ACT.Copy).then_inc(x_part1, 1)
                act.activation(xdt[3 * BC:NX, :], ps_a[3 * BC:NX, bank(s, 10), :], ACT.Copy)
                act.wait_ge(x_res1, s.k + 2)
                for q in (1, 2):
                    rows = slice(q * BC, (q + 1) * BC)
                    last = act.activation(xbc[rows, s.nj, :], xres[rows, :], ACT.Copy)
                last.then_inc(x_part2, 1)
                act.wait_ge(x_part2, s.k + 2)
                act.sem_inc(a_free, 1)

            def dt_parts(s, k):
                act.wait_ge(a_ready, s.use0 + 12 + k)
                if k == 0:
                    if s.scanning:
                        act.wait_ge(da_ready, s.k * S * K)
                    act.wait_ge(dt_ready, s.k + 1)
                act.activation(dt[:, s.nj, k, :], ps_a[:, bank(s, 11 + k), :], ACT.Relu, bias=dtb[:, s.nj, k:k + 1])
                act.activation(sp_tmp[:, k, :], ps_a[:, bank(s, 11 + k), :], ACT.Abs, bias=dtb[:, s.nj, k:k + 1]).then_inc(a_free, 1)

            def soft(s):
                act.wait_ge(a_free, s.use0 + USES + 2)
                act.activation(sp_tmp[:], sp_tmp[:], ACT.Exp, scale=-1.0).then_inc(soft_step, 1)
                act.wait_ge(soft_step, s.k + 2)
                act.activation(sp_tmp[:], sp_tmp[:], ACT.Ln, bias=one[:, 0:1]).then_inc(soft_done, 1)

            def spread_copy(s, i):
                act.wait_ge(bc_ready, s.k * 2 * S + 2 * i + 1)
                act.wait_ge(dbx_ready, s.k * S + i + 1)
                act.activation(bb[:, i % 4, :], ps_b[:, 0, :], ACT.Copy).then_inc(bc_copied, 1)
                act.wait_ge(bc_ready, s.k * 2 * S + 2 * i + 2)
                act.wait_ge(hc_ready, s.k * S + i + 1)
                act.activation(cc[:, i % 4, :], ps_b[:, 1, :], ACT.Copy).then_inc(bc_copied, 1)

            def decays(s, i):
                act.wait_ge(scanned, s.k * S + i + 1)
                j = s.j if i < S else s.nj
                if i == S:
                    act.wait_ge(dt_ready, s.k + 2)
                for k in range(K):
                    act.activation(da[:, i % 2, k, :], dt[:, j, k, :], ACT.Exp,
                                   scale=amat[:, j, k, i % S:i % S + 1]).then_inc(da_ready, 1)

            def tail(s):
                act.wait_ge(mo_stored, s.k * 16 - 16)
                for h in range(2):
                    act.wait_ge(a_ready, s.use0 + h + 1)
                    act.activation(mo[:, 2 * h:2 * h + 2, :].rearrange("p t c -> p (t c)"), ps_a[:, bank(s, h), :],
                                   ACT.Copy).then_inc(a_free, 1)
                act.wait_ge(a_free, s.use0 + 2 + 2)
                act.sem_inc(out_copied, 2)

            def front(s, slot=None):
                for at, work in ((4, lambda: [in_copy(s, e) for e in (0, 1)]), (5, lambda: [in_copy(s, e) for e in (2, 3)]),
                                 (6, lambda: [in_copy(s, e) for e in (4, 5)]), (7, lambda: [in_copy(s, e) for e in (6, 7)]),
                                 (8, lambda: silus(s)), (9, lambda: x_copy(s)), (10, lambda: [dt_parts(s, k) for k in (0, 1)]),
                                 (11, lambda: [dt_parts(s, k) for k in (2, 3)]), (12, lambda: soft(s))):
                    if slot in (None, at):
                        work()

            def step(s):
                for i in range(S):
                    if i + 2 < S or s.front:
                        spread_copy(s, i + 2)
                    if i + 1 < S or s.front:
                        decays(s, i + 1)
                    if i == 3 and s.tail:
                        tail(s)
                    if s.front:
                        front(s, i)

            act.wait_ge(w_loaded, 16 * N_MAMBA_W)
            act.activation(amat[:], amat[:], ACT.Exp).then_inc(a_exp, 1)
            act.wait_ge(a_neg, 1)

            def begin(s):
                front(s)
                spread_copy(s, S)
                spread_copy(s, S + 1)
                decays(s, S)

            run(act, begin, step, tail)

        @block.gpsimd
        def _(pool):
            def inputs(s, i):
                if i == 0:
                    pool.wait_ge(dtx_ready, s.k + 1)
                pool.wait_ge(bc_copied, s.k * 2 * S + 2 * i + 3)
                pool.wait_ge(summed, s.k * S + i + 1)
                pool.tensor_tensor(hh[:, i % 4, :, :], dtx[:, s.j, :, :], bb[:, i % 4, :].unsqueeze(1).broadcast_to([P, K, CH]),
                                   ALU.mult).then_inc(dbx_ready, 1)

            def softplus(s):
                pool.wait_ge(soft_done, s.k + 2)
                pool.tensor_tensor(dt[:, s.nj], dt[:, s.nj], sp_tmp[:], ALU.add).then_inc(dt_ready, 1)
                pool.wait_ge(dt_ready, s.k + 2)
                if s.scanning:
                    pool.wait_ge(dbx_ready, s.k * S + 4)
                pool.tensor_tensor(dtx[:, s.nj], dt[:, s.nj], xs[:, s.nj], ALU.mult).then_inc(dtx_ready, 1)

            def tail(s):
                pool.wait_ge(y_ready, s.k * K)
                pool.wait_ge(dt_ready, s.fronts)
                dst = sp_tmp[:] if s.nj == 0 else sp_tmp[:, :, ::-1]
                pool.tensor_tensor(dst, xs[:, s.nj], zs[:, s.nj], ALU.mult).then_inc(gated, 1)

            def front(s, slot=None):
                if slot in (None, 12):
                    softplus(s)

            def step(s):
                for i in range(S):
                    inputs(s, i)
                    if i == 2 and s.tail:
                        tail(s)
                    if s.front:
                        front(s, i)

            pool.memset(keep[:, :], 1.0).then_inc(consts, 1)
            pool.wait_ge(consts, 1)
            pool.memset(keep[:, :].rearrange("p (b n) -> p b n", b=B)[:, :, 0:1], 0.0).then_inc(consts, 1)
            pool.memset(one[:, :], 1.0).then_inc(consts, 1)
            pool.memset(state[:], 0.0).then_inc(consts, 1)
            pool.memset(halo[:], 0.0).then_inc(consts, 1)
            pool.memset(pick[:, :], 0.0).then_inc(consts, 1)
            for q in range(3):
                pool.wait_ge(consts, 6 + q)
                pool.affine_select(out=pick[:, :], in_=pick[:, :], compare_op=ALU.not_equal, fill=1.0, base=-q * BC,
                                   pattern=[[-1, BC]], channel_multiplier=1).then_inc(consts, 1)
            pool.wait_ge(consts, N_CONSTS)
            run(pool, front, step, tail)

        @block.vector
        def _(dve):
            TAPS = 6

            def conv(s, part):
                j = s.nj
                edge, spot = (slice(CH, W), slice(0, 3)) if j == 0 else (slice(0, 3), slice(CH, W))
                base = (s.k + 1) * TAPS
                if part == 0:
                    dve.wait_ge(a_free, s.use0 + 2 + K + 2)
                    dve.wait_ge(conv_done, s.k + 1)
                    dve.wait_ge(a_ready, s.use0 + 2)
                    dve.tensor_scalar(xpre[:, :, spot], halo[:, j], keep[:, s.nn:s.nn + 1] if isinstance(s.nn, int) else keep[:, ds(s.nn, 1)],
                                      None, ALU.mult).then_inc(conv_step, 1)
                    dve.wait_ge(conv_step, base + 1)
                    dve.tensor_copy(halo[:, j], xpre[:, :, edge]).then_inc(conv_step, 1)
                for tap in ((3, 2) if part == 0 else (1, 0)):
                    at = tap if j == 0 else 3 - tap
                    for k in range(K):
                        src = xpre[:, k, at:at + CH]
                        if tap == 3:
                            last = dve.tensor_scalar(xs[:, j, k, :], src, cw[:, j, k, 3:4], cb[:, j, k:k + 1], ALU.mult, ALU.add)
                        else:
                            last = dve.scalar_tensor_tensor(xs[:, j, k, :], src, cw[:, j, k, tap:tap + 1], xs[:, j, k, :],
                                                            ALU.mult, ALU.add)
                    if tap:
                        last.then_inc(conv_step, 1)
                        dve.wait_ge(conv_step, base + 2 + 4 - tap)
                    else:
                        last.then_inc(conv_done, 1)
                if part == 1:
                    dve.sem_inc(conv_step, 1)

            def split(s):
                dve.wait_ge(x_part1, s.k + 2)
                for q in (1, 2):
                    rows = slice(q * BC, (q + 1) * BC)
                    last = dve.tensor_tensor(xres[rows, :], ps_a[rows, bank(s, 10), :], xbc[rows, s.nj, :], ALU.subtract)
                last.then_inc(x_res1, 1)
                dve.wait_ge(x_part2, s.k + 2)
                rows = slice(2 * BC, 3 * BC)
                dve.tensor_tensor(xbc[rows, s.nj, :], xres[rows, :], xbc[rows, s.nj, :], ALU.subtract).then_inc(x_split, 1)

            def scans(s, i):
                dve.wait_ge(dbx_ready, s.k * S + i + 5)
                if i == 0:
                    dve.wait_ge(kept, s.k + 1)
                for k in range(K):
                    dve.wait_ge(da_ready, (s.k * S + i) * K + k + 1)
                    h, a = hh[:, i % 4, k, :], da[:, i % 2, k, :]
                    if s.j:
                        h, a = h[:, ::-1], a[:, ::-1]
                    last = dve.tensor_tensor_scan(h, a, h, state[:, s.j, k, i:i + 1], ALU.mult, ALU.add)
                last.then_inc(scanned, 1)

            def save(s, i):
                dve.wait_ge(scanned, s.k * S + i + 3)
                j = s.j if i >= 0 else s.nj
                end = CH - 1 if j == 0 else 0
                dve.tensor_copy(state[:, j, :, i % S:i % S + 1], hh[:, i % 4, :, end:end + 1]).then_inc(saved, 1)

            def outputs(s, i):
                dve.wait_ge(saved, s.k * S + i + 1)
                dve.wait_ge(bc_copied, s.k * 2 * S + 2 * i + 4)
                dve.tensor_tensor(hh[:, i % 4], hh[:, i % 4], cc[:, i % 4, :].unsqueeze(1).broadcast_to([P, K, CH]),
                                  ALU.mult).then_inc(hc_ready, 1)

            def tail(s):
                dve.wait_ge(summed, s.k * S + 4)
                for k in range(K):
                    dve.scalar_tensor_tensor(xs[:, s.nj, k, :], xs[:, s.nj, k, :], dskip[:, s.nj, k:k + 1], ps_y[:, k, :],
                                             ALU.mult, ALU.add).then_inc(y_ready, 1)

            def front(s, slot=None):
                for at, work in ((6, lambda: conv(s, 0)), (7, lambda: conv(s, 1)), (9, lambda: split(s))):
                    if slot in (None, at):
                        work()

            def step(s):
                for i in range(S):
                    if i or s.tail:
                        save(s, i - 1)
                    if i == 0:
                        dve.wait_ge(saved, s.k * S)
                        dve.tensor_scalar(state[:, s.j], state[:, s.j], keep[:, s.n:s.n + 1] if isinstance(s.n, int) else keep[:, ds(s.n, 1)],
                                          None, ALU.mult).then_inc(kept, 1)
                    scans(s, i)
                    if i or s.tail:
                        outputs(s, i - 1)
                    if i == 1 and s.tail:
                        tail(s)
                    if s.front:
                        front(s, i)

            def end(s):
                save(s, -1)
                outputs(s, -1)
                tail(s)

            for t, v in ((a_free, 2), (bc_copied, 2), (dbx_ready, 4), (scanned, 2), (hc_ready, 4), (summed, 4)):
                dve.sem_inc(t, v)
            dve.wait_ge(a_exp, 1)
            dve.tensor_scalar(amat[:], amat[:], -1.0, None, ALU.mult).then_inc(a_neg, 1)
            dve.wait_ge(consts, N_CONSTS)
            run(dve, front, step, end)


def mlp_phase(nc, ctx, ident, w, t1, m_dirs, t2, xn, lg, xbuf):
    def sb(name, shape, dt=F32):
        return ctx.enter_context(nc.sbuf_tensor("ml_" + name, shape, dt))

    sem = phase_semaphores(nc, ctx, "ml_")

    N = B * NCH
    FB = 4
    w1, w2 = sb("w1", [P, 2, FB * P]), sb("w2", [P, FB, C])
    gw = sb("gw", [P, 2, EXPERTS])
    b1, lng, lnb = sb("b1", [P, FB]), sb("lng", [P, 2]), sb("lnb", [P, 2])
    b2, gb = sb("b2", [P, C]), sb("gb", [P, EXPERTS])
    eps, zero = sb("eps", [P, 1]), sb("zero", [P, 4 * C])
    min_, bin_, tin = sb("m", [P, 2, 4, C]), sb("back", [P, 2, 4, C]), sb("t1", [P, 2, 4, C])
    stats, mv = sb("stats", [P, 8, 6]), sb("mv", [P, 8, 2])
    std, rstd = sb("std", [P, 8]), sb("rstd", [P, 8])
    ht, xt = sb("ht", [P, 2, 2, CH]), sb("xt", [P, 2, CH])
    t2cur, xcur = sb("t2", [P, 2, 4, C]), sb("xn", [P, 2, 4, C])
    hid, pt = sb("hid", [P, 2, CH]), sb("pt", [P, FB, CH])
    ps_t = ctx.enter_context(nc.psum_tensor("ml_ps_t", [P, 2, CH], F32))
    ps_f = ctx.enter_context(nc.psum_tensor("ml_ps_f", [P, 2, CH], F32))
    ps_y = ctx.enter_context(nc.psum_tensor("ml_ps_y", [P, 2, CH], F32))
    ps_l = ctx.enter_context(nc.psum_tensor("ml_ps_l", [P, 4 * EXPERTS], F32))

    w_loaded, consts, zeroed = sem("w_loaded"), sem("consts"), sem("zeroed")
    m_loaded = [sem(f"m_loaded{j}") for j in range(2)]
    t_loaded = [sem(f"t_loaded{j}") for j in range(2)]
    t2_stored = [sem(f"t2_stored{j}") for j in range(2)]
    xn_stored = [sem(f"xn_stored{j}") for j in range(2)]
    m_ready, skip_step, skip_ready, bn_step, var_ready, std_ready, rstd_ready = (
        sem(n) for n in ("m_ready", "skip_step", "skip_ready", "bn_step", "var_ready", "std_ready", "rstd_ready"))
    h_normed, x_normed, turned, turned_copied = (sem(n) for n in ("h_normed", "x_normed", "turned", "turned_copied"))
    f_ready, hid_ready, act_ready, y_ready, t2_ready = (sem(n) for n in ("f_ready", "hid_ready", "act_ready", "y_ready", "t2_ready"))
    l_ready, lg_ready, stood, m_copied = sem("l_ready"), sem("lg_ready"), sem("stood"), sem("m_copied")

    def run(eng, step):
        step(-1, 1, None)
        step(0, 0, None)
        with eng.Fori(0, (N - 4) // 2) as h:
            step(h * 2 + 1, 1, h)
            step(h * 2 + 2, 0, h)
        step(N - 3, 1, None)
        step(N - 2, 0, None)
        step(N - 1, 1, None)
        step(N, 0, None)

    def has(i, what):
        if not isinstance(i, int):
            return True
        return {"load": i + 2 < N, "a": i + 1 < N, "b": 0 <= i < N, "c": i >= 1}[what]

    def loads(i, h):
        return h + 2 if h is not None else (i + 1) // 2 + 1

    def use(i, what):
        if isinstance(i, int) and i <= 0:
            return i + 1
        if isinstance(i, int) and i >= N - 1:
            return i + N - 1
        return i * 2 + (what == "c")

    with nc.Block() as block:
        @block.sync
        def _(sp):
            n = 0
            for dst, src in ((w1[:, :, :], w["attn_w1"].rearrange("k p e -> p k e")),
                             (w2[:, :, :], w["attn_w2"].rearrange("k p e -> p k e")),
                             (gw[:, :, :], w["ffn_gate_w"].rearrange("(k p) e -> p k e", p=P)),
                             (b2[:, :], w["attn_b2"].partition_broadcast(P)),
                             (gb[:, :], w["ffn_gate_b"].partition_broadcast(P))):
                sp.dma_start(dst, src).then_inc(w_loaded, 16)
                n += 1
            for dst, src, cut in ((b1, "attn_b1", FB), (lng, "attn_ln_g", 2), (lnb, "attn_ln_b", 2)):
                for k in range(cut):
                    sp.dma_start(dst[:, k:k + 1], w[src][k * P:(k + 1) * P].unsqueeze(1)).then_inc(w_loaded, 16)
                    n += 1
            assert n == N_MLP_W

            def flat(t):
                return t.rearrange("p t c -> p (t c)")

            def load_m(c, j):
                sp.dma_start(flat(bin_[:, j]), m_dirs[1, (c + NCH) % N]).then_inc(m_loaded[j], 16)
                sp.dma_start(flat(min_[:, j]), m_dirs[0, c]).then_inc(m_loaded[j], 16)

            def step(i, j, h):
                q = 1 - j
                if has(i, "a"):
                    sp.wait_ge(t2_ready, i * 2 + 4)
                    stand(sp, stood)
                    sp.dma_start(flat(tin[:, q]), t1[i + 1]).then_inc(t_loaded[q], 16)
                if has(i, "load") and not (isinstance(i, int) and i < 0):
                    sp.wait_ge(m_copied, i + 1)
                    sp.wait_ge(skip_ready, i + 1)
                    stand(sp, stood)
                    load_m(i + 2, j)
                if has(i, "c"):
                    sp.wait_ge(x_normed, i)
                    stand(sp, stood)
                    sp.dma_start(xn[i - 1], flat(xcur[:, q])).then_inc(xn_stored[q], 16)
                if has(i, "b"):
                    sp.wait_ge(t2_ready, i * 2 + 6)
                    stand(sp, stood)
                    sp.dma_start(t2[i], flat(t2cur[:, j])).then_inc(t2_stored[j], 16)

            load_m(0, 0)
            load_m(1, 1)
            run(sp, step)
            for j in range(2):
                sp.wait_ge(xn_stored[j], 8 * N)
                sp.wait_ge(t2_stored[j], 8 * N)
            sp.wait_ge(consts, 1)
            rows = xbuf[0:EXPERTS * CAP, :].rearrange("(n p t) c -> n p (t c)", p=P, t=4)
            for n in range(EXPERTS * CAP // (4 * P)):
                sp.dma_start(rows[n], zero[:, :]).then_inc(zeroed, 16)
            sp.wait_ge(zeroed, 16 * (EXPERTS * CAP // (4 * P)))

        @block.gpsimd
        def _(pool):
            pool.memset(zero[:, :], 0.0).then_inc(consts, 1)
            pool.memset(eps[:, :], GN_EPS).then_inc(consts, 1)
            pool.memset(mv[:, :, :], 1.0).then_inc(consts, 1)
            pool.wait_ge(w_loaded, 16 * N_MLP_W)

            def step(i, j, h):
                q = 1 - j
                if has(i, "a"):
                    pool.wait_ge(m_loaded[q], loads(i, h) * 32)
                    pool.tensor_tensor(min_[:, q], min_[:, q], bin_[:, q], ALU.add).then_inc(m_ready, 1)
                    pool.wait_ge(m_ready, i + 2)
                    pool.wait_ge(t_loaded[q], loads(i, h) * 16)
                    pool.tensor_tensor(tin[:, q], tin[:, q], min_[:, q], ALU.add).then_inc(skip_step, 1)
                    pool.wait_ge(skip_step, i + 2)
                    pool.tensor_tensor(tin[:, q], tin[:, q], b2[:, :].unsqueeze(1).broadcast_to([P, 4, C]), ALU.add).then_inc(skip_ready, 1)
            run(pool, step)

        @block.tensor
        def _(pe):
            def turn(i, what, src, count):
                pe.wait_ge(count, i + 2 if what == "a" else i)
                pe.wait_ge(turned_copied, use(i, what))
                for t in range(4):
                    for k in range(2):
                        last = pe.transpose(ps_t[:, k, t * P:(t + 1) * P], src(t, k), ident[:, :])
                last.then_inc(turned, 1)

            def step(i, j, h):
                q = 1 - j
                if has(i, "b"):
                    pe.wait_ge(m_copied, i + 1)
                    for f in range(FB):
                        pe.wait_ge(hid_ready, i * FB + f + 1)
                        for k in range(2):
                            last = pe.matmul(ps_f[:, f % 2, :], w1[:, k, f * P:(f + 1) * P], ht[:, j, k, :], start=(k == 0), stop=(k == 1))
                        last.then_inc(f_ready, 1)
                    pe.wait_ge(act_ready, (i + 1) * FB + 2)
                    pe.wait_ge(t2_ready, i * 2 + 4)
                    for t in range(4):
                        for f in range(FB):
                            last = pe.matmul(ps_y[:, t // 2, (t % 2) * C:(t % 2 + 1) * C], pt[:, f, t * P:(t + 1) * P], w2[:, f, :],
                                             start=(f == 0), stop=(f == FB - 1))
                    last.then_inc(y_ready, 1)
                if has(i, "a"):
                    turn(i, "a", lambda t, k: bin_[:, q, t, k * P:(k + 1) * P], h_normed)
                if has(i, "c"):
                    turn(i, "c", lambda t, k: xcur[:, q, t, k * P:(k + 1) * P], x_normed)
                    pe.wait_ge(turned_copied, use(i, "c") + 1)
                    pe.wait_ge(lg_ready, i - 1)
                    for t in range(4):
                        for k in range(2):
                            last = pe.matmul(ps_l[:, t * EXPERTS:(t + 1) * EXPERTS], xt[:, k, t * P:(t + 1) * P], gw[:, k, :],
                                             start=(k == 0), stop=(k == 1))
                    last.then_inc(l_ready, 1)

            pe.wait_ge(w_loaded, 16 * N_MLP_W)
            run(pe, step)

        @block.scalar
        def _(act):
            def step(i, j, h):
                q = 1 - j

                def biased(f):
                    act.wait_ge(f_ready, i * FB + f + 1)
                    act.wait_ge(act_ready, i * FB + f + 1)
                    act.activation(hid[:, f % 2, :], ps_f[:, f % 2, :], ACT.Identity, bias=b1[:, f:f + 1]).then_inc(hid_ready, 1)

                if has(i, "b"):
                    biased(0)
                    biased(1)
                act.wait_ge(var_ready, i + 2)
                act.activation(std[:, :], mv[:, :, 1], ACT.Sqrt, bias=eps[:, 0:1]).then_inc(std_ready, 1)
                if has(i, "b"):
                    biased(2)
                    biased(3)
                if has(i, "a"):
                    act.wait_ge(turned, use(i, "a") + 1)
                    for k in range(2):
                        last = act.activation(ht[:, q, k, :], ps_t[:, k, :], ACT.Identity, scale=lng[:, k:k + 1], bias=lnb[:, k:k + 1])
                    last.then_inc(turned_copied, 1)
                    act.wait_ge(turned_copied, use(i, "a") + 1)
                    act.sem_inc(m_copied, 1)
                if has(i, "c"):
                    act.wait_ge(turned, use(i, "c") + 1)
                    act.wait_ge(l_ready, i - 1)
                    act.activation(xt[:, :, :], ps_t[:, :, :], ACT.Copy).then_inc(turned_copied, 1)

            act.wait_ge(consts, 3)
            act.wait_ge(w_loaded, 16 * N_MLP_W)
            run(act, step)

        @block.vector
        def _(dve):
            def step(i, j, h):
                q = 1 - j
                if has(i, "a"):
                    dve.wait_ge(m_ready, i + 2)
                    for t in range(4):
                        last = dve.bn_stats(stats[:, t, :], min_[:, q, t, :])
                if has(i, "c"):
                    dve.wait_ge(t2_ready, i * 2 + 4)
                    for t in range(4):
                        last = dve.bn_stats(stats[:, 4 + t, :], t2cur[:, q, t, :])
                last.then_inc(bn_step, 1)
                dve.wait_ge(bn_step, i + 2)
                stand(dve, stood)
                for t in range(8):
                    if has(i, "a") if t < 4 else has(i, "c"):
                        last = dve.bn_aggr(mv[:, t, :], stats[:, t, :])
                last.then_inc(var_ready, 1)
                if has(i, "b"):
                    for f in range(FB):
                        dve.wait_ge(hid_ready, i * FB + f + 3)
                        if f == 0:
                            dve.wait_ge(y_ready, i)
                        dve.scalar_tensor_tensor(pt[:, f, :], hid[:, f % 2, :], 0.01, hid[:, f % 2, :], ALU.mult, ALU.max).then_inc(act_ready, 1)
                dve.wait_ge(std_ready, i + 2)
                dve.reciprocal(rstd[:, :], std[:, :]).then_inc(rstd_ready, 1)
                dve.wait_ge(rstd_ready, i + 2)
                if has(i, "a"):
                    for t in range(4):
                        last = dve.tensor_scalar(bin_[:, q, t, :], min_[:, q, t, :], mv[:, t, 0:1], rstd[:, t:t + 1], ALU.subtract, ALU.mult)
                    last.then_inc(h_normed, 1)
                if has(i, "c"):
                    dve.wait_ge(xn_stored[q], (h if h is not None else (i - 1) // 2) * 16)
                    for t in range(4):
                        last = dve.tensor_scalar(xcur[:, q, t, :], t2cur[:, q, t, :], mv[:, 4 + t, 0:1], rstd[:, 4 + t:5 + t], ALU.subtract, ALU.mult)
                    last.then_inc(x_normed, 1)
                if has(i, "b"):
                    dve.wait_ge(y_ready, i + 1)
                    dve.wait_ge(skip_ready, i + 1)
                    if has(i, "c"):
                        dve.wait_ge(x_normed, i - 1)
                        dve.wait_ge(t2_stored[j], (h + 1 - j if h is not None else i // 2) * 16)
                    for g in range(2):
                        dve.tensor_tensor(t2cur[:, j, 2 * g:2 * g + 2, :].rearrange("p t c -> p (t c)"), ps_y[:, g, :],
                                          tin[:, j, 2 * g:2 * g + 2, :].rearrange("p t c -> p (t c)"), ALU.add).then_inc(t2_ready, 1)
                if has(i, "c"):
                    dve.wait_ge(l_ready, i)
                    dst = lg[:, ds(i * 4 - 4, 4), :] if h is not None else lg[:, 4 * i - 4:4 * i, :]
                    dve.tensor_tensor(dst, ps_l[:, :].rearrange("p (t e) -> p t e", e=EXPERTS),
                                      gb[:, :].unsqueeze(1).broadcast_to([P, 4, EXPERTS]), ALU.add).then_inc(lg_ready, 1)

            for t, v in ((t2_ready, 4), (hid_ready, 2), (act_ready, 2)):
                dve.sem_inc(t, v)
            dve.wait_ge(consts, 3)
            dve.wait_ge(w_loaded, 16 * N_MLP_W)
            run(dve, step)


def routing_phase(nc, ctx, lg, tri, slot, scat, weight):
    def sb(name, shape, dt=F32):
        return ctx.enter_context(nc.sbuf_tensor("rt_" + name, shape, dt))

    sem = phase_semaphores(nc, ctx, "rt_")

    T, E = B * QT, EXPERTS
    mx, sh, ex, sm = sb("mx", [P, T]), sb("sh", [P, T, E]), sb("ex", [P, T, E]), sb("sm", [P, T])
    num, ones = sb("num", [P, E]), sb("ones", [P, P])
    cand, idx = sb("cand", [P, T, E]), sb("idx", [P, T])
    hot, tot, inc = sb("hot", [P, T, E]), sb("tot", [P, T, E]), sb("inc", [P, T, E])
    pos, kept, fslot, fscat = sb("pos", [P, T]), sb("kept", [P, T]), sb("fslot", [P, T]), sb("fscat", [P, T])
    ps_c = ctx.enter_context(nc.psum_tensor("rt_ps_c", [P, T * E], F32))
    ps_n = ctx.enter_context(nc.psum_tensor("rt_ps_n", [P, T * E], F32))
    consts, dve_step, sh_ready, ex_ready, hot_ready, counted, done = (
        sem(n) for n in ("consts", "dve_step", "sh_ready", "ex_ready", "hot_ready", "counted", "done"))
    wide = lambda t: t[:, :].unsqueeze(2).broadcast_to([P, T, E])
    flat = lambda t: t[:, :, :].rearrange("p t e -> p (t e)")

    with nc.Block() as block:
        @block.gpsimd
        def _(pool):
            pool.memset(tri[:, :], 1.0).then_inc(consts, 1)
            pool.memset(ones[:, :], 1.0).then_inc(consts, 1)
            pool.iota(num[:, :], pattern=[[1, E]], base=0, channel_multiplier=0,
                      allow_small_or_imprecise_dtypes=True).then_inc(consts, 1)
            pool.wait_ge(consts, 3)
            pool.affine_select(out=tri[:, :], in_=tri[:, :], compare_op=ALU.is_ge, fill=0.0, base=0,
                               pattern=[[1, P]], channel_multiplier=-1).then_inc(consts, 1)

        @block.scalar
        def _(act):
            act.wait_ge(sh_ready, 1)
            act.activation(ex[:, :, :], sh[:, :, :], ACT.Exp).then_inc(ex_ready, 1)

        @block.tensor
        def _(pe):
            pe.wait_ge(consts, 4)
            pe.wait_ge(hot_ready, 1)
            pe.matmul(ps_c[:, :], tri[:, :], flat(hot), start=True, stop=True)
            pe.matmul(ps_n[:, :], ones[:, :], flat(hot), start=True, stop=True).then_inc(counted, 1)

        @block.vector
        def _(dve):
            n = [0]

            def link(ins):
                n[0] += 1
                ins.then_inc(dve_step, 1)
                dve.wait_ge(dve_step, n[0])

            dve.wait_ge(consts, 4)
            link(dve.tensor_reduce(mx[:, :], lg[:, :, :], AX.X, ALU.max))
            dve.tensor_tensor(sh[:, :, :], lg[:, :, :], wide(mx), ALU.subtract).then_inc(sh_ready, 1)
            dve.wait_ge(sh_ready, 1)
            link(dve.tensor_scalar(cand[:, :, :], sh[:, :, :], 0.0, -float(E), ALU.is_equal, ALU.mult))
            link(dve.scalar_tensor_tensor(cand[:, :, :], cand[:, :, :], float(E), num[:, :].unsqueeze(1).broadcast_to([P, T, E]), ALU.add, ALU.add))
            link(dve.tensor_reduce(idx[:, :], cand[:, :, :], AX.X, ALU.min))
            dve.tensor_tensor(hot[:, :, :], num[:, :].unsqueeze(1).broadcast_to([P, T, E]), wide(idx), ALU.is_equal).then_inc(hot_ready, 1)
            dve.wait_ge(ex_ready, 1)
            link(dve.tensor_reduce(sm[:, :], ex[:, :, :], AX.X, ALU.add))
            link(dve.reciprocal(weight[:, :], sm[:, :]))
            dve.wait_ge(counted, 1)
            link(dve.tensor_copy(flat(tot), ps_n[:, :]))
            for e in range(E):
                last = dve.tensor_tensor_scan(inc[:, :, e], ones[:, 0:T], tot[:, :, e], 0.0, ALU.mult, ALU.add)
            link(last)
            link(dve.tensor_tensor(flat(inc), flat(inc), flat(tot), ALU.subtract))
            link(dve.tensor_tensor(flat(inc), ps_c[:, :], flat(inc), ALU.add))
            link(dve.tensor_tensor(inc[:, :, :], inc[:, :, :], hot[:, :, :], ALU.mult))
            link(dve.tensor_reduce(pos[:, :], inc[:, :, :], AX.X, ALU.add))
            link(dve.tensor_scalar(kept[:, :], pos[:, :], float(CAP), None, ALU.is_le))
            link(dve.tensor_scalar(fslot[:, :], pos[:, :], float(CAP), -1.0, ALU.min, ALU.add))
            link(dve.scalar_tensor_tensor(fslot[:, :], idx[:, :], float(CAP), fslot[:, :], ALU.mult, ALU.add))
            link(dve.tensor_tensor(weight[:, :], weight[:, :], kept[:, :], ALU.mult))
            link(dve.tensor_scalar(fscat[:, :], kept[:, :], -float(E * CAP), float(E * CAP), ALU.mult, ALU.add))
            link(dve.tensor_tensor(fscat[:, :], fscat[:, :], fslot[:, :], ALU.add))
            link(dve.tensor_copy(slot[:, :], fslot[:, :]))
            link(dve.tensor_copy(scat[:, :], fscat[:, :]))


def scatter_phase(nc, ctx, xn, scat, xbuf):
    rows = ctx.enter_context(nc.sbuf_tensor("sc_rows", [P, 4, 4, C], F32))
    sem = phase_semaphores(nc, ctx, "sc_")
    loaded = [sem(f"loaded{j}") for j in range(4)]
    scattered = [sem(f"scattered{j}") for j in range(4)]
    N = B * NCH

    with nc.Block() as block:
        @block.sync
        def _(sp):
            for n in range(N):
                j = n % 4
                if n >= 4:
                    sp.wait_ge(scattered[j], 64 * (n // 4))
                sp.dma_start(rows[:, j].rearrange("p t c -> p (t c)"), xn[n]).then_inc(loaded[j], 16)
            for j in range(4):
                sp.wait_ge(scattered[j], 64 * (N // 4))

        @block.gpsimd
        def _(pool):
            for n in range(N):
                j = n % 4
                pool.wait_ge(loaded[j], 16 * (n // 4 + 1))
                for t in range(4):
                    pool.indirect_dma_start(
                        out=xbuf, out_offset=bass.IndirectOffsetOnAxis(ap=scat[:, 4 * n + t:4 * n + t + 1], axis=0),
                        in_=rows[:, j, t, :], in_offset=None, bounds_check=EXPERTS * CAP - 1,
                        oob_is_err=False).then_inc(scattered[j], 16)


def experts_phase(nc, ctx, ident, w, xbuf, ybuf):
    def sb(name, shape, dt=F32):
        return ctx.enter_context(nc.sbuf_tensor("ex_" + name, shape, dt))

    sem = phase_semaphores(nc, ctx, "ex_")

    E, F = EXPERTS, 1024
    FB, RC = F // P, 256
    M = CAP // RC
    w1, w2 = sb("w1", [P, 2, 2, F]), sb("w2", [P, 2, FB, C])
    b1, b2 = sb("b1", [P, E, FB]), sb("b2", [P, E, C])
    xr, xt = sb("xr", [P, 2, 2, C]), sb("xt", [P, 2, 2, RC])
    hid = sb("hid", [P, 2, FB, RC])
    yr = sb("yr", [P, 2, 2, C])
    ps_x = ctx.enter_context(nc.psum_tensor("ex_ps_x", [P, 2, CH], F32))
    ps_h = ctx.enter_context(nc.psum_tensor("ex_ps_h", [P, 4, CH], F32))
    ps_y = ctx.enter_context(nc.psum_tensor("ex_ps_y", [P, 2, CH], F32))
    b1c, b2c = sb("b1c", [P, 2, FB]), sb("b2c", [P, 2, C])
    b_loaded, bias_ready = sem("b_loaded"), sem("bias_ready")
    w_loaded = [sem(f"w_loaded{j}") for j in range(2)]
    x_loaded = [sem(f"x_loaded{j}") for j in range(2)]
    turned, x_copied, h_ready, relued, y_ready, y_added, stood = (
        sem(n) for n in ("turned", "x_copied", "h_ready", "relued", "y_ready", "y_added", "stood"))
    y_stored = [sem(f"y_stored{j}") for j in range(2)]
    TURN = 2 * M

    def loop(eng, chunk):
        with eng.Fori(0, E // 2) as r:
            for m in range(TURN):
                chunk(r * TURN + m, m, r)

    with nc.Block() as block:
        @block.sync
        def _(sp):
            sp.dma_start(b1[:, :, :], w["b1"]).then_inc(b_loaded, 16)
            sp.dma_start(b2[:, :, :].rearrange("p e c -> p (e c)"), w["b2"].rearrange("e c -> (e c)").partition_broadcast(P)).then_inc(b_loaded, 16)

            def load_w(e, j):
                sp.dma_start(w1[:, j], w["w1"][e].rearrange("(k p) f -> p k f", p=P)).then_inc(w_loaded[j], 16)
                sp.dma_start(w2[:, j], w["w2"][e].rearrange("(f p) c -> p f c", p=P)).then_inc(w_loaded[j], 16)

            def load_x(n, j):
                sp.dma_start(xr[:, j], xbuf[ds(n * RC, RC), :].rearrange("(t p) c -> p t c", p=P)).then_inc(x_loaded[j], 16)

            load_w(0, 0)
            load_w(1, 1)
            load_x(0, 0)
            load_x(1, 1)

            def chunk(n, m, r, last=False):
                if not (last and m >= TURN - 2):
                    sp.wait_ge(turned, n + 1)
                    stand(sp, stood)
                    load_x(n + 2, m % 2)
                if not last and m in (M, TURN - 1):
                    j = 0 if m == M else 1
                    sp.wait_ge(y_ready, n if m == M else n + 1)
                    stand(sp, stood)
                    load_w(r * 2 + 2 + j, j)
                sp.wait_ge(y_added, (n + 1) * 2)
                stand(sp, stood)
                sp.dma_start(ybuf[ds(n * RC, RC), :].rearrange("(t p) c -> p t c", p=P), yr[:, m % 2]).then_inc(y_stored[m % 2], 16)

            with sp.Fori(0, E // 2 - 1) as r:
                for m in range(TURN):
                    chunk(r * TURN + m, m, r)
            for m in range(TURN):
                chunk((E // 2 - 1) * TURN + m, m, None, last=True)
            for j in range(2):
                sp.wait_ge(y_stored[j], 16 * E * M // 2)

        @block.tensor
        def _(pe):
            def turn(n, q, loads):
                pe.wait_ge(x_loaded[q], loads)
                pe.wait_ge(x_copied, n)
                for t in range(2):
                    for k in range(2):
                        last = pe.transpose(ps_x[:, q, k * RC + t * P:k * RC + (t + 1) * P], xr[:, q, t, k * P:(k + 1) * P], ident[:, :])
                last.then_inc(turned, 1)

            def chunk(n, m, r, last=False):
                j, q = m // M, m % 2
                if m % M == 0:
                    pe.wait_ge(w_loaded[j], (r + 1) * 32)
                pe.wait_ge(x_copied, n + 2)
                for f in range(FB):
                    pe.wait_ge(relued, n * FB + f + 1)
                    for k in range(2):
                        ins = pe.matmul(ps_h[:, f % 4, 0:RC], w1[:, j, k, f * P:(f + 1) * P], xt[:, q, k, :], start=(k == 0), stop=(k == 1))
                    ins.then_inc(h_ready, 1)
                if not (last and m == TURN - 1):
                    turn(n + 1, 1 - q, (r * (TURN // 2) + (m + 1) // 2 + 1) * 16)
                pe.wait_ge(relued, (n + 1) * FB + 4)
                pe.wait_ge(y_added, n * 2)
                for t in range(2):
                    for f in range(FB):
                        ins = pe.matmul(ps_y[:, t, 0:C], hid[:, q, f, t * P:(t + 1) * P], w2[:, j, f, :], start=(f == 0), stop=(f == FB - 1))
                ins.then_inc(y_ready, 1)

            turn(0, 0, 16)
            with pe.Fori(0, E // 2 - 1) as r:
                for m in range(TURN):
                    chunk(r * TURN + m, m, r)
            for m in range(TURN):
                chunk((E // 2 - 1) * TURN + m, m, E // 2 - 1, last=True)

        @block.scalar
        def _(act):
            def chunk(n, m, r):
                q = m % 2
                if m % M == 0:
                    act.wait_ge(bias_ready, r * 2 + m // M + 1)
                for f in range(FB):
                    act.wait_ge(h_ready, n * FB + f + 1)
                    act.activation(hid[:, q, f, :], ps_h[:, f % 4, 0:RC], ACT.Relu, bias=b1c[:, m // M, f:f + 1]).then_inc(relued, 1)
            loop(act, chunk)

        @block.vector
        def _(dve):
            def copy(n, q):
                dve.wait_ge(turned, n + 1)
                dve.tensor_copy(xt[:, q], ps_x[:, q, :].rearrange("p (k r) -> p k r", k=2)).then_inc(x_copied, 1)

            def chunk(n, m, r, last=False):
                q = m % 2
                if m % M == 0:
                    dve.wait_ge(y_ready, n)
                    dve.tensor_copy(b2c[:, m // M, :], b2[:, ds(r * 2 + m // M, 1), :].rearrange("p a c -> p (a c)"))
                    dve.tensor_copy(b1c[:, m // M, :], b1[:, ds(r * 2 + m // M, 1), :].rearrange("p a f -> p (a f)")).then_inc(bias_ready, 1)
                    dve.wait_ge(bias_ready, r * 2 + m // M + 1)
                if not (last and m == TURN - 1):
                    copy(n + 1, 1 - q)
                dve.wait_ge(y_ready, n + 1)
                dve.wait_ge(y_stored[q], r * (TURN // 2) * 16 + m // 2 * 16)
                for t in range(2):
                    dve.tensor_tensor(yr[:, q, t, :], ps_y[:, t, 0:C], b2c[:, m // M, :], ALU.add).then_inc(y_added, 1)

            dve.wait_ge(b_loaded, 32)
            dve.sem_inc(x_copied, 1)
            dve.sem_inc(relued, 4)
            copy(0, 0)
            with dve.Fori(0, E // 2 - 1) as r:
                for m in range(TURN):
                    chunk(r * TURN + m, m, r)
            for m in range(TURN):
                chunk((E // 2 - 1) * TURN + m, m, E // 2 - 1, last=True)


def gather_phase(nc, ctx, ident, ybuf, slot, weight, t2, out):
    def sb(name, shape, dt=F32):
        return ctx.enter_context(nc.sbuf_tensor("ga_" + name, shape, dt))

    sem = phase_semaphores(nc, ctx, "ga_")

    N = B * NCH
    D = 4
    yg, tin = sb("yg", [P, D, 4, C]), sb("t2", [P, D, 4, C])
    safe, fin, same = sb("safe", [P, 2, 4, C]), sb("fin", [P, 2, 4 * C], I32), sb("same", [P, 2, 4 * C], I32)
    bounded, fin_ready = sem("bounded"), sem("fin_ready")
    bound = sb("bound", [P, 2, 4, C])
    lim = sb("lim", [P, 2, 4, C])
    ot = sb("ot", [P, 2, 2, CH])
    ps_o = ctx.enter_context(nc.psum_tensor("ga_ps_o", [P, 2, 2, CH], F32))
    t_loaded = [sem(f"t_loaded{j}") for j in range(D)]
    y_loaded = [sem(f"y_loaded{j}") for j in range(D)]
    zeroed, weighed, masked, chosen, kept_step, added, turned, copied = (
        sem(n) for n in ("zeroed", "weighed", "masked", "chosen", "kept_step", "added", "turned", "copied"))
    stored = [sem(f"stored{j}") for j in range(2)]
    flat = lambda t: t.rearrange("p t c -> p (t c)")

    with nc.Block() as block:
        @block.gpsimd
        def _(pool):
            for n in range(N):
                j = n % D
                if n >= D:
                    pool.wait_ge(added, n - D + 1)
                for t in range(4):
                    pool.indirect_dma_start(
                        out=yg[:, j, t, :], out_offset=None, in_=ybuf,
                        in_offset=bass.IndirectOffsetOnAxis(ap=slot[:, 4 * n + t:4 * n + t + 1], axis=0),
                        bounds_check=EXPERTS * CAP - 1, oob_is_err=False).then_inc(y_loaded[j], 16)

        @block.sync
        def _(sp):
            for n in range(N):
                j = n % D
                if n >= D:
                    sp.wait_ge(turned, n - D + 1)
                sp.dma_start(flat(tin[:, j]), t2[n]).then_inc(t_loaded[j], 16)

        @block.vector
        def _(dve):
            dve.memset(safe[:, :, :, :], 0.0).then_inc(zeroed, 1)
            dve.wait_ge(zeroed, 1)
            for n in range(N):
                j, q = n % D, n % 2
                y = yg[:, j]
                dve.wait_ge(y_loaded[j], 64 * (n // D + 1))
                if n >= 2:
                    dve.wait_ge(added, n - 1)
                for t in range(4):
                    last = dve.tensor_scalar(yg[:, j, t, :], yg[:, j, t, :], weight[:, 4 * n + t:4 * n + t + 1], None, ALU.mult)
                last.then_inc(weighed, 1)
                dve.wait_ge(weighed, n + 1)
                dve.tensor_tensor(same[:, q, :], flat(y), flat(y), ALU.is_equal)
                dve.tensor_scalar(flat(bound[:, q]), flat(y), FLT_MAX, -FLT_MAX, ALU.min, ALU.max).then_inc(bounded, 1)
                dve.tensor_scalar(flat(lim[:, q]), flat(y), 1e4, -1e4, ALU.min, ALU.max).then_inc(masked, 1)
                dve.wait_ge(bounded, n + 1)
                dve.tensor_tensor(fin[:, q, :], flat(bound[:, q]), flat(y), ALU.is_equal).then_inc(fin_ready, 1)
                dve.wait_ge(masked, n + 1)
                dve.copy_predicated(flat(safe[:, q]), same[:, q, :], flat(lim[:, q])).then_inc(chosen, 1)
                dve.wait_ge(chosen, n + 1)
                dve.wait_ge(fin_ready, n + 1)
                dve.copy_predicated(flat(safe[:, q]), fin[:, q, :], flat(y)).then_inc(kept_step, 1)
                dve.wait_ge(kept_step, n + 1)
                dve.wait_ge(t_loaded[j], 16 * (n // D + 1))
                dve.tensor_tensor(tin[:, j], tin[:, j], safe[:, q], ALU.add).then_inc(added, 1)

        @block.tensor
        def _(pe):
            for n in range(N):
                j, q = n % D, n % 2
                pe.wait_ge(added, n + 1)
                if n >= 2:
                    pe.wait_ge(copied, n - 1)
                for t in range(4):
                    for k in range(2):
                        last = pe.transpose(ps_o[:, q, k, t * P:(t + 1) * P], tin[:, j, t, k * P:(k + 1) * P], ident[:, :])
                last.then_inc(turned, 1)

        @block.scalar
        def _(act):
            for n in range(N):
                q = n % 2
                act.wait_ge(turned, n + 1)
                if n >= 2:
                    act.wait_ge(stored[q], 16 * (n // 2))
                act.activation(ot[:, q], ps_o[:, q], ACT.Copy).then_inc(copied, 1)
                act.wait_ge(copied, n + 1)
                b, c = divmod(n, NCH)
                act.dma_start(out[b * C:(b + 1) * C, c * CH:(c + 1) * CH].rearrange("(k p) l -> p k l", p=P), ot[:, q]).then_inc(stored[q], 16)
            for j in range(2):
                act.wait_ge(stored[j], 8 * N)


N_CONV_W = 3 * 8 + 2 * 4
N_MAMBA_W = 9 * 2 + 3 * 2 * 4
N_MLP_W = 5 + 8


def hybrid_kernel(nc, a, out):
    x = a["x"].rearrange("b c h w -> (b c) (h w)")
    q_split = scratch(nc, "q_split", (3, C * B, L), BF16)
    k_split = scratch(nc, "k_split", (3, C * B, L), BF16)
    v_split = scratch(nc, "v_split", (HEADS, P, QT * P), BF16)
    attn_out = scratch(nc, "attn_out", (HEADS, P, QT * DH))
    with ExitStack() as whole:
        ident = whole.enter_context(nc.sbuf_tensor("ident", [P, P], F32))
        ident_ready = whole.enter_context(nc.semaphore("ident_ready"))
        with nc.Block() as block:
            @block.gpsimd
            def _(pool):
                pool.memset(ident[:, :], 0.0).then_inc(ident_ready, 1)
                pool.wait_ge(ident_ready, 1)
                pool.affine_select(out=ident[:, :], in_=ident[:, :], compare_op=ALU.not_equal, fill=1.0, base=0,
                                   pattern=[[-1, P]], channel_multiplier=1).then_inc(ident_ready, 1)
                pool.wait_ge(ident_ready, 2)
        with ExitStack() as ctx:
            conv_phase(nc, ctx, ident, x, a["L0_conv_qw"], a["L0_conv_kw"], a["L0_conv_vw"], a["L0_conv_c1w"],
                       a["L0_conv_c1b"], a["L0_conv_gnw"], a["L0_conv_gnb"], q_split, k_split, v_split)
        with ExitStack() as ctx:
            attention_phase(nc, ctx, ident, q_split, k_split, v_split, attn_out)
        t1 = scratch(nc, "t1", (B * NCH, P, 4 * C))
        u1 = scratch(nc, "u1", (B * NCH, P, 2 * CH))
        m_dirs = scratch(nc, "m_dirs", (2, B * NCH, P, 4 * C))
        with ExitStack() as ctx:
            tokens_phase(nc, ctx, ident, x, attn_out, t1, u1)
        with ExitStack() as ctx:
            mamba_phase(nc, ctx, ident, {k[8:]: v for k, v in a.items() if k.startswith("L1_attn_")}, u1, m_dirs)
        t2 = scratch(nc, "t2", (B * NCH, P, 4 * C))
        xn = scratch(nc, "xn", (B * NCH, P, 4 * C))
        xbuf = scratch(nc, "xbuf", (EXPERTS * CAP, C))
        ybuf = scratch(nc, "ybuf", (EXPERTS * CAP, C))
        lg, weight = (whole.enter_context(nc.sbuf_tensor(*v, F32)) for v in (("lg", [P, B * QT, EXPERTS]), ("weight", [P, B * QT])))
        slot, scat = (whole.enter_context(nc.sbuf_tensor(n, [P, B * QT], U32)) for n in ("slot", "scat"))
        tri = whole.enter_context(nc.sbuf_tensor("tri", [P, P], F32))
        w = {k[3:]: v for k, v in a.items() if k.startswith("L1_")}
        with ExitStack() as ctx:
            mlp_phase(nc, ctx, ident, w, t1, m_dirs, t2, xn, lg, xbuf)
        with ExitStack() as ctx:
            routing_phase(nc, ctx, lg, tri, slot, scat, weight)
        with ExitStack() as ctx:
            scatter_phase(nc, ctx, xn, scat, xbuf)
        with ExitStack() as ctx:
            experts_phase(nc, ctx, ident, {k[4:]: v for k, v in w.items() if k.startswith("ffn_")}, xbuf, ybuf)
        with ExitStack() as ctx:
            gather_phase(nc, ctx, ident, ybuf, slot, weight, t2, out.rearrange("b c h w -> (b c) (h w)"))

def _layout(inputs, np):
    w = {k: np.ascontiguousarray(v) for k, v in inputs.items()}
    for n in ("qw", "kw", "vw"):
        t = w[f"L0_conv_{n}"].reshape(4, 16, 16, 9)
        w[f"L0_conv_{n}"] = t.transpose(0, 2, 3, 1)
    for n, cut in (("in_proj_w", 2), ("x_proj_w", 4), ("out_proj_w", 4)):
        t = w[f"L1_attn_{n}"].transpose(0, 2, 1)
        w[f"L1_attn_{n}"] = t.reshape(2, cut, P, t.shape[2])
    for n, cut in (("w1", 2), ("w2", 4)):
        t = w[f"L1_attn_{n}"].T
        w[f"L1_attn_{n}"] = t.reshape(cut, P, t.shape[1])
    w["L1_ffn_b1"] = w["L1_ffn_b1"].reshape(EXPERTS, -1, P).transpose(2, 0, 1)
    w["L1_attn_dt_proj_w"] = w["L1_attn_dt_proj_w"].transpose(0, 2, 1)
    w["L0_conv_c1w"] = w["L0_conv_c1w"][:, :, 0, 0].T
    return {k: np.ascontiguousarray(v) for k, v in w.items()}


def kernel(**inputs):
    import numpy as _np
    import concourse.bacc as _bacc
    from concourse.bass_utils import run_bass_kernel_spmd as _run

    nc = _bacc.Bacc("TRN2", target_bir_lowering=False, num_devices=1)
    arrays, args = {}, {}
    for name, a in _layout(inputs, _np).items():
        arrays[f"in_{name}"] = a
        args[name] = nc.dram_tensor(f"in_{name}", a.shape, mybir.dt.from_np(a.dtype), kind="ExternalInput").ap()
    out = nc.dram_tensor("out_x", (B, C, IMG, IMG), F32, kind="ExternalOutput").ap()
    hybrid_kernel(nc, args, out)
    r = _run(nc, [arrays], core_ids=[0])
    return r.results[0]["out_x"]
```

```python
import concourse.bass as bass
from concourse import mybir
from contextlib import ExitStack

F32 = mybir.dt.float32
BF16 = mybir.dt.bfloat16
U32 = mybir.dt.uint32
I32 = mybir.dt.int32
ALU = mybir.AluOpType
ACT = mybir.ActivationFunctionType
AX = mybir.AxisListType
ds = bass.ds

P = 128
B, C, IMG = 2, 256, 64
L = IMG * IMG
HEADS = 8
DH = 64
PAIRS = HEADS // 2
PAD = IMG + 2
CH = 512
NCH = L // CH
QT = L // P
EXPERTS = 8
CAP = 1280
GN_EPS = 1e-5
FLT_MAX = 3.4028234663852886e38
ONE = 1


def scratch(nc, name, shape, dt=F32):
    return nc.dram_tensor(name, shape, dt, kind="Internal").ap()


def stand(eng, sem):
    eng.sem_inc(sem, 1)


def phase_semaphores(nc, ctx, prefix):
    taken = []

    def sem(name):
        taken.append(nc.alloc_semaphore(prefix + name))
        return taken[-1]

    def start():
        with nc.Block() as block:
            @block.gpsimd
            def _(pool):
                for s in taken:
                    pool.sem_inc(s, ONE)

    def put_back():
        with nc.Block() as block:
            @block.gpsimd
            def _(pool):
                for s in taken:
                    pool.sem_clear(s)
        for s in taken:
            nc.release_semaphore(s)

    ctx.callback(put_back)
    return sem, start


def conv_phase(nc, ctx, ident, x, qw, kw, vw, c1w, c1b, gnw, gnb, q_split, k_split, v_split):
    def sb(name, shape, dt=F32):
        return ctx.enter_context(nc.sbuf_tensor(name, shape, dt))

    sem, start_semaphores = phase_semaphores(nc, ctx, "")

    wq, wk, wv = sb("wq", [P, 9, P]), sb("wk", [P, 9, P]), sb("wv", [P, 9, P])
    wc1 = sb("wc1", [P, P])
    vecs = sb("conv_vecs", [P, 3])
    group8 = sb("group8", [P, P])
    eps = sb("conv_eps", [P, 1])
    ximg = sb("ximg", [P, L])
    xpad = sb("xpad", [P, PAD, PAD])
    gated = sb("gated", [P, L])
    resid = sb("resid", [P, L])
    qp = [sb(f"q_part{n}", [P, L], BF16) for n in range(3)]
    kp = [sb(f"k_part{n}", [P, L], BF16) for n in range(3)]
    vparts = sb("v_parts", [P, 2, QT, 2 * DH], BF16)
    vc = sb("v_chunk", [P, 2, CH])
    kres = sb("k_resid", [P, 2, CH])
    stats = sb("conv_stats", [P, NCH, 6])
    mv = sb("conv_mv", [P, 2])
    chan = sb("chan", [P, 2])
    grp = sb("grp", [P, 2])
    col = sb("conv_cols", [P, 8])
    colsum = sb("colsum", [P, 3, PAD])
    rowsum = sb("rowsum", [P, 3, PAD])
    cat = sb("cat", [P, 2 * IMG])
    gates = sb("gates", [P, 2 * IMG])
    ps_g = ctx.enter_context(nc.psum_tensor("ps_g", [P, 2], F32))
    ps_k = ctx.enter_context(nc.psum_tensor("ps_k", [P, 2, CH], F32))
    ps_q = ctx.enter_context(nc.psum_tensor("ps_q", [P, 2 * IMG], F32))
    ps_c = ctx.enter_context(nc.psum_tensor("ps_c", [P, 2 * IMG], F32))
    ps_v = ctx.enter_context(nc.psum_tensor("ps_v", [P, 2, CH], F32))

    w_ready = sem("conv_w_ready")
    zeroed = sem("conv_zeroed")
    stood = sem("conv_stood")
    x_loaded = sem("x_loaded")
    stored = sem("conv_stored")
    dve_step = sem("conv_dve_step")
    chan_ready, grp_summed, var_ready, std_ready = (sem(n) for n in ("chan_ready", "grp_summed", "var_ready", "std_ready"))
    affine_ready, xn_ready, sums_ready, q_summed = (sem(n) for n in ("affine_ready", "xn_ready", "sums_ready", "q_summed"))
    cat_ready, c1_done, gates_ready = sem("cat_ready"), sem("c1_done"), sem("gates_ready")
    var2_ready, std2_ready, qaff_ready = sem("var2_ready"), sem("std2_ready"), sem("qaff_ready")
    vc_ready, v_turned = sem("vc_ready"), sem("v_turned")
    k_summed, k1_ready, kres_ready, k2_ready, k3_ready = (sem(n) for n in ("k_summed", "k1_ready", "kres_ready", "k2_ready", "k3_ready"))
    v_summed, v1_ready, v2_ready = sem("v_summed"), sem("v1_ready"), sem("v2_ready")
    q_ready, q1_ready, qres_ready, q2_ready, q3_ready = (sem(n) for n in ("q_ready", "q1_ready", "qres_ready", "q2_ready", "q3_ready"))

    inner = xpad[:, 1:IMG + 1, 1:IMG + 1]
    image = lambda t: t[:, :].rearrange("p (h w) -> p h w", w=IMG)
    STORES = 7
    TILE_GROUPS = QT // 4

    start_semaphores()
    with nc.Block() as block:
        @block.gpsimd
        def _(pool):
            for t in (wq[:, :, :], wk[:, :, :], wv[:, :, :], wc1[:, :], xpad[:, :, :], colsum[:, :, :], rowsum[:, :, :]):
                pool.memset(t, 0.0).then_inc(zeroed, 1)
            pool.memset(eps[:, :], GN_EPS).then_inc(zeroed, 1)
            pool.memset(group8[:, :], 0.125).then_inc(zeroed, 1)
            pool.wait_ge(zeroed, ONE + 9)
            blocks = group8[:, :].rearrange("p (a b) -> p a b", b=8)
            pool.affine_select(out=blocks, in_=blocks, compare_op=ALU.is_ge, fill=0.0, base=0,
                               pattern=[[-8, 16], [0, 8]], channel_multiplier=1).then_inc(zeroed, 1)
            pool.wait_ge(zeroed, ONE + 10)
            pool.affine_select(out=blocks, in_=blocks, compare_op=ALU.is_ge, fill=0.0, base=7,
                               pattern=[[8, 16], [0, 8]], channel_multiplier=-1).then_inc(zeroed, 1)

        @block.sync
        def _(sp):
            sp.wait_ge(zeroed, ONE + 9)
            n = 0
            for dst, src in ((wk, kw), (wv, vw), (wq, qw)):
                for j in range(8):
                    sp.dma_start(dst[16 * j:16 * j + 16, :, 16 * j:16 * j + 16], src[j % 4]).then_inc(w_ready, 16)
                    n += 1
            for h in range(2):
                rows = slice(DH * h, DH * h + DH)
                sp.dma_start(wc1[rows, rows], c1w).then_inc(w_ready, 16)
                for j, v in enumerate((c1b, gnw, gnb)):
                    sp.dma_start(vecs[rows, j:j + 1], v.unsqueeze(1)).then_inc(w_ready, 16)
                n += 4
            assert n == N_CONV_W
            with sp.Fori(0, PAIRS) as i:
                sp.wait_ge(gates_ready, ONE + i)
                sp.wait_ge(xn_ready, ONE + i)
                stand(sp, stood)
                sp.dma_start(ximg[:, :], x[ds(i * P, P), :]).then_inc(x_loaded, 16)
                sp.wait_ge(k3_ready, ONE + (i + 1) * NCH)
                sp.wait_ge(k2_ready, ONE + (i + 1) * NCH)
                stand(sp, stood)
                for n in range(3):
                    sp.dma_start(k_split[n, ds(i * P, P), :], kp[n][:, :]).then_inc(stored, 16)
                sp.wait_ge(v2_ready, ONE + (i + 1) * TILE_GROUPS + 2)
                stand(sp, stood)
                sp.dma_start(v_split[ds(i * 2, 2)].rearrange("h p n -> p h n"),
                             vparts[:, :, :, :].rearrange("p h t c -> p h (t c)")).then_inc(stored, 16)
                sp.wait_ge(q3_ready, ONE + i + 1)
                stand(sp, stood)
                for n in range(3):
                    sp.dma_start(q_split[n, ds(i * P, P), :], qp[n][:, :]).then_inc(stored, 16)
            sp.wait_ge(stored, ONE + 16 * STORES * PAIRS)

        @block.tensor
        def _(pe):
            pe.wait_ge(w_ready, ONE + 16 * N_CONV_W)
            pe.wait_ge(zeroed, ONE + 11)
            with pe.Fori(0, PAIRS) as i:
                pe.wait_ge(chan_ready, ONE + i + 1)
                pe.matmul(ps_g[:, :], group8[:, :], chan[:, :], start=True, stop=True).then_inc(grp_summed, 1)
                pe.wait_ge(xn_ready, ONE + i + 1)
                for c in range(NCH):
                    if c < 2:
                        pe.wait_ge(vc_ready, ONE + i * NCH)
                    else:
                        pe.wait_ge(kres_ready, ONE + i * NCH + c - 1)
                    for t in range(9):
                        dy, dx = divmod(t, 3)
                        last = pe.matmul(ps_k[:, c % 2, :], wk[:, t, :],
                                         xpad[:, 8 * c + dy:8 * c + dy + 8, dx:dx + IMG],
                                         start=(t == 0), stop=(t == 8))
                    last.then_inc(k_summed, 1)
                pe.wait_ge(sums_ready, ONE + 2 * (i + 1))
                for t in range(9):
                    dy, dx = divmod(t, 3)
                    pe.matmul(ps_q[:, 0:IMG], wq[:, t, :], colsum[:, dy, dx:dx + IMG], start=(t == 0), stop=(t == 8))
                for t in range(9):
                    dy, dx = divmod(t, 3)
                    last = pe.matmul(ps_q[:, IMG:2 * IMG], wq[:, t, :], rowsum[:, dx, dy:dy + IMG],
                                     start=(t == 0), stop=(t == 8))
                last.then_inc(q_summed, 1)
                for c in range(NCH + 1):
                    if c == 2:
                        pe.wait_ge(cat_ready, ONE + i + 1)
                        pe.matmul(ps_c[:, :], wc1[:, :], cat[:, :], start=True, stop=True).then_inc(c1_done, 1)
                    if c < NCH:
                        if c < 2:
                            pe.wait_ge(kres_ready, ONE + i * NCH + NCH - 1 + c)
                        else:
                            pe.wait_ge(vc_ready, ONE + i * NCH + c - 1)
                        for t in range(9):
                            dy, dx = divmod(t, 3)
                            last = pe.matmul(ps_k[:, c % 2, :], wv[:, t, :],
                                             xpad[:, 8 * c + dy:8 * c + dy + 8, dx:dx + IMG],
                                             start=(t == 0), stop=(t == 8))
                        last.then_inc(v_summed, 1)
                    if c:
                        pe.wait_ge(vc_ready, ONE + i * NCH + c)
                        pe.wait_ge(v2_ready, ONE + i * NCH + c)
                        for k in range(4):
                            last = pe.transpose(ps_v[:, (c - 1) % 2, k * P:(k + 1) * P],
                                                vc[:, (c - 1) % 2, k * P:(k + 1) * P], ident[:, :])
                        last.then_inc(v_turned, 1)

        @block.scalar
        def _(act):
            act.wait_ge(zeroed, ONE + 11)
            act.wait_ge(w_ready, ONE + 16 * N_CONV_W)
            with act.Fori(0, PAIRS) as i:
                act.wait_ge(var_ready, ONE + i + 1)
                act.activation(col[:, 0:1], grp[:, 1:2], ACT.Sqrt, scale=-1.0, bias=eps[:, 0:1]).then_inc(std_ready, 1)
                act.wait_ge(affine_ready, ONE + i + 1)
                act.wait_ge(v_summed, ONE + i * TILE_GROUPS)
                act.activation(inner, image(ximg), ACT.Identity, scale=col[:, 1:2], bias=col[:, 2:3]).then_inc(xn_ready, 1)
                act.wait_ge(stored, ONE + i * 16 * STORES)
                for c in range(NCH):
                    cs = slice(c * CH, (c + 1) * CH)
                    act.wait_ge(k_summed, ONE + i * NCH + c + 1)
                    act.activation(kp[0][:, cs], ps_k[:, c % 2, :], ACT.Copy).then_inc(k1_ready, 1)
                    act.wait_ge(kres_ready, ONE + i * NCH + c + 1)
                    act.activation(kp[1][:, cs], kres[:, c % 2, :], ACT.Copy).then_inc(k2_ready, 1)
                act.wait_ge(q_summed, ONE + i + 1)
                act.activation(cat[:, :], ps_q[:, :], ACT.Copy, scale=1.0 / IMG).then_inc(cat_ready, 1)
                for c in range(NCH + 1):
                    if c < NCH:
                        act.wait_ge(v_summed, ONE + i * NCH + c + 1)
                        act.wait_ge(v_turned, ONE + i * NCH + c + 1)
                        act.activation(vc[:, c % 2, :], ps_k[:, c % 2, :], ACT.Copy).then_inc(vc_ready, 1)
                    if c:
                        g = c - 1
                        act.wait_ge(v_turned, ONE + i * NCH + c + 2)
                        act.activation(vparts[:, :, 4 * g:4 * g + 4, 0:DH],
                                       ps_v[:, g % 2, :].rearrange("p (t h c) -> p h t c", t=4, h=2),
                                       ACT.Copy).then_inc(v1_ready, 1)
                    if c == 3:
                        act.wait_ge(c1_done, ONE + i + 1)
                        act.activation(gates[:, :], ps_c[:, :], ACT.Sigmoid, bias=vecs[:, 0:1]).then_inc(gates_ready, 1)
                act.wait_ge(var2_ready, ONE + i + 1)
                act.activation(col[:, 3:4], mv[:, 1:2], ACT.Sqrt, bias=eps[:, 0:1]).then_inc(std2_ready, 1)
                act.wait_ge(qaff_ready, ONE + i + 1)
                act.activation(gated[:, :], gated[:, :], ACT.Identity, scale=col[:, 5:6], bias=col[:, 6:7]).then_inc(q_ready, 1)
                act.wait_ge(q_ready, ONE + i + 1)
                act.activation(qp[0][:, :], gated[:, :], ACT.Copy).then_inc(q1_ready, 1)
                act.wait_ge(qres_ready, ONE + i + 1)
                act.activation(qp[1][:, :], resid[:, :], ACT.Copy).then_inc(q2_ready, 1)

        @block.vector
        def _(dve):
            STEPS = 16
            dve.sem_inc(v_turned, 2)
            dve.sem_inc(v2_ready, 2)
            dve.wait_ge(zeroed, ONE + 11)
            dve.wait_ge(w_ready, ONE + 16 * N_CONV_W)
            with dve.Fori(0, PAIRS) as i:
                n = [0]

                def link(ins):
                    n[0] += 1
                    ins.then_inc(dve_step, 1)
                    dve.wait_ge(dve_step, ONE + i * STEPS + n[0])

                def channel_stats(t):
                    for c in range(NCH):
                        last = dve.bn_stats(stats[:, c, :], t[:, c * CH:(c + 1) * CH])
                    link(last)

                dve.wait_ge(x_loaded, ONE + (i + 1) * 16)
                channel_stats(ximg)
                stand(dve, stood)
                link(dve.bn_aggr(mv[:, :], stats[:, :, :].rearrange("p a b -> p (a b)")))
                dve.tensor_copy(chan[:, 0:1], mv[:, 0:1])
                dve.scalar_tensor_tensor(chan[:, 1:2], mv[:, 0:1], mv[:, 0:1], mv[:, 1:2],
                                         ALU.mult, ALU.add).then_inc(chan_ready, 1)
                dve.wait_ge(grp_summed, ONE + i + 1)
                link(dve.tensor_copy(grp[:, :], ps_g[:, :]))
                link(dve.tensor_tensor(col[:, 7:8], grp[:, 0:1], grp[:, 0:1], ALU.mult))
                dve.tensor_tensor(grp[:, 1:2], col[:, 7:8], grp[:, 1:2], ALU.subtract).then_inc(var_ready, 1)
                dve.wait_ge(std_ready, ONE + i + 1)
                link(dve.reciprocal(col[:, 1:2], col[:, 0:1]))
                dve.tensor_scalar(col[:, 2:3], grp[:, 0:1], -1.0, col[:, 1:2], ALU.mult, ALU.mult).then_inc(affine_ready, 1)
                dve.wait_ge(xn_ready, ONE + i + 1)
                dve.tensor_reduce(colsum[:, 1, 1:IMG + 1], inner.rearrange("p h w -> p w h"), AX.X, ALU.add)
                link(dve.tensor_reduce(rowsum[:, 1, 1:IMG + 1], inner, AX.X, ALU.add))
                for d, edge in ((0, IMG), (2, 1)):
                    dve.tensor_tensor(colsum[:, d, 1:IMG + 1], colsum[:, 1, 1:IMG + 1], xpad[:, edge, 1:IMG + 1], ALU.subtract)
                    dve.tensor_tensor(rowsum[:, d, 1:IMG + 1], rowsum[:, 1, 1:IMG + 1], xpad[:, 1:IMG + 1, edge],
                                      ALU.subtract).then_inc(sums_ready, 1)
                dve.wait_ge(stored, ONE + i * 16 * STORES)
                for c in range(NCH + 1):
                    if c < NCH:
                        dve.wait_ge(k1_ready, ONE + i * NCH + c + 1)
                        if c > 1:
                            dve.wait_ge(k3_ready, ONE + i * NCH + c - 1)
                        dve.tensor_tensor(kres[:, c % 2, :], ps_k[:, c % 2, :], kp[0][:, c * CH:(c + 1) * CH],
                                          ALU.subtract).then_inc(kres_ready, 1)
                    if c:
                        dve.wait_ge(k2_ready, ONE + i * NCH + c)
                        cs = slice((c - 1) * CH, c * CH)
                        dve.tensor_tensor(kp[2][:, cs], kres[:, (c - 1) % 2, :], kp[1][:, cs],
                                          ALU.subtract).then_inc(k3_ready, 1)
                for g in range(TILE_GROUPS):
                    dve.wait_ge(v1_ready, ONE + i * TILE_GROUPS + g + 1)
                    dve.tensor_tensor(vparts[:, :, 4 * g:4 * g + 4, DH:2 * DH],
                                      ps_v[:, g % 2, :].rearrange("p (t h c) -> p h t c", t=4, h=2),
                                      vparts[:, :, 4 * g:4 * g + 4, 0:DH], ALU.subtract).then_inc(v2_ready, 1)
                dve.wait_ge(gates_ready, ONE + i + 1)
                link(dve.tensor_tensor(image(gated), inner, gates[:, 0:IMG].unsqueeze(1).broadcast_to([P, IMG, IMG]), ALU.mult))
                link(dve.tensor_tensor(image(gated), image(gated),
                                       gates[:, IMG:2 * IMG].unsqueeze(2).broadcast_to([P, IMG, IMG]), ALU.mult))
                channel_stats(gated)
                stand(dve, stood)
                dve.bn_aggr(mv[:, :], stats[:, :, :].rearrange("p a b -> p (a b)")).then_inc(var2_ready, 1)
                dve.wait_ge(std2_ready, ONE + i + 1)
                link(dve.reciprocal(col[:, 4:5], col[:, 3:4]))
                link(dve.tensor_tensor(col[:, 5:6], col[:, 4:5], vecs[:, 1:2], ALU.mult))
                link(dve.tensor_tensor(col[:, 7:8], mv[:, 0:1], col[:, 5:6], ALU.mult))
                dve.tensor_tensor(col[:, 6:7], vecs[:, 2:3], col[:, 7:8], ALU.subtract).then_inc(qaff_ready, 1)
                dve.wait_ge(q1_ready, ONE + i + 1)
                dve.tensor_tensor(resid[:, :], gated[:, :], qp[0][:, :], ALU.subtract).then_inc(qres_ready, 1)
                dve.wait_ge(q2_ready, ONE + i + 1)
                link(dve.tensor_tensor(qp[2][:, :], resid[:, :], qp[1][:, :], ALU.subtract))
                dve.sem_inc(q3_ready, 1)
                for _ in range(STEPS - n[0]):
                    dve.sem_inc(dve_step, 1)
                assert n[0] <= STEPS


def attention_phase(nc, ctx, ident, q_split, k_split, v_split, attn_out):
    def sb(name, shape, dt=F32):
        return ctx.enter_context(nc.sbuf_tensor(name, shape, dt))

    sem, start_semaphores = phase_semaphores(nc, ctx, "")

    qa, qb, ka, kb, kc = ([sb(f"{n}{j}", [P, L], BF16) for j in range(2)] for n in ("q12_", "q13_", "k11_", "k22_", "k31_"))
    vv = [sb(f"v12_{j}", [P, QT, P], BF16) for j in range(2)]
    prob = [sb(f"prob{j}", [P, L]) for j in range(2)]
    hi, lo = sb("p_hi", [P, 2, CH], BF16), sb("p_lo", [P, 2, CH], BF16)
    mx, nmx = sb("mx", [P, 2, 4]), sb("nmx", [P, 2])
    rs, rsum, rinv = sb("rs", [P, 2, 4]), sb("rsum", [P, 2]), sb("rinv", [P, 2])
    otmp = sb("otmp", [P, DH])
    oh = sb("o_head", [P, 2, QT, DH])
    ps_s = ctx.enter_context(nc.psum_tensor("ps_s", [P, 2, 2 * CH], F32))
    ps_t = ctx.enter_context(nc.psum_tensor("ps_t", [P, 2, CH], F32))
    ps_o = ctx.enter_context(nc.psum_tensor("ps_o", [P, 2, CH], F32))

    loaded = [sem(f"head_loaded{j}") for j in range(2)]
    s_ready, s_copied, max_ready, exp_ready = sem("s_ready"), sem("s_copied"), sem("max_ready"), sem("exp_ready")
    t_ready, hi_ready, lo_ready, pv_done = sem("t_ready"), sem("hi_ready"), sem("lo_ready"), sem("pv_done")
    o_ready, o_stored, fin_step = sem("o_ready"), sem("o_stored"), sem("fin_step")

    LOADS = 11
    SC = L // (2 * CH)
    TG = L // CH
    scale = 1.0 / 16.0

    SCORES_AT = (0, 1, 3, 5)
    EXPS_AT = (0, 2, 4, 6)
    FINISH_AT = 2

    def tiles(eng, head, step):
        step(head * QT, 0, 0, False, True)
        with eng.Fori(0, QT // 2 - 1) as it:
            for u in (1, 0):
                step(head * QT + it * 2 + 2 - u, it * 2 + 2 - u, u, True, True)
        step(head * QT + QT - 1, QT - 1, 1, True, False)

    def heads(eng, body):
        with eng.Fori(0, HEADS // 2) as hp:
            for j in range(2):
                body(hp * 2 + j, j, hp)

    start_semaphores()
    with nc.Block() as block:
        @block.sync
        def _(sp):
            def load(h, j):
                rows = ds(h * DH, DH)
                top, bottom = slice(0, DH), slice(DH, P)
                for dst, part, src in ((qa[j][top], 0, q_split), (qa[j][bottom], 1, q_split),
                                       (ka[j][top], 0, k_split), (ka[j][bottom], 0, k_split),
                                       (kb[j][top], 1, k_split), (kb[j][bottom], 1, k_split),
                                       (qb[j][top], 0, q_split), (qb[j][bottom], 2, q_split),
                                       (kc[j][top], 2, k_split), (kc[j][bottom], 0, k_split)):
                    sp.dma_start(dst, src[part, rows, :]).then_inc(loaded[j], 16)
                sp.dma_start(vv[j][:, :, :].rearrange("p t c -> p (t c)"), v_split[h]).then_inc(loaded[j], 16)

            def store(h, j):
                sp.wait_ge(o_ready, ONE + (h + 1) * QT + 1)
                sp.dma_start(attn_out[h], oh[:, j, :, :].rearrange("p t c -> p (t c)")).then_inc(o_stored, 16)

            load(0, 0)
            load(1, 1)
            with sp.Fori(1, HEADS // 2) as hp:
                for j in range(2):
                    store(hp * 2 + j - 2, j)
                    load(hp * 2 + j, j)
            store(HEADS - 2, 0)
            store(HEADS - 1, 1)
            sp.wait_ge(o_stored, ONE + 16 * HEADS)

        @block.tensor
        def _(pe):
            def head(h, j, hp):
                def scores(g, t, u, c):
                    pe.wait_ge(s_copied, ONE + g * SC + c + 1)
                    for half in range(2):
                        keys = slice((2 * c + half) * CH, (2 * c + half + 1) * CH)
                        for n, (a, b) in enumerate(((qa, ka), (qa, kb), (qb, kc))):
                            last = pe.matmul(ps_s[:, c % 2, half * CH:(half + 1) * CH], a[j][:, ds(t * P, P)],
                                             b[j][:, keys], start=(n == 0), stop=(n == 2))
                    last.then_inc(s_ready, 1)

                def transposes(g, t, u, k):
                    pe.wait_ge(exp_ready, ONE + g * SC + k // 2 + 1)
                    pe.wait_ge(lo_ready, ONE + g * TG + k + 1)
                    for m in range(4):
                        last = pe.transpose(ps_t[:, k % 2, m * P:(m + 1) * P],
                                            prob[u][:, (4 * k + m) * P:(4 * k + m + 1) * P], ident[:, :])
                    last.then_inc(t_ready, 1)

                def values(g, t, u, k):
                    pe.wait_ge(lo_ready, ONE + g * TG + k + 3)
                    if k == 0:
                        pe.wait_ge(o_ready, ONE + g)
                    for m in range(4):
                        for n, part in enumerate((hi, lo)):
                            last = pe.matmul(ps_o[:, u, 0:P], part[:, k % 2, m * P:(m + 1) * P], vv[j][:, 4 * k + m, :],
                                             start=(k == 0 and m == 0 and n == 0), stop=(k == TG - 1 and m == 3 and n == 1))
                    last.then_inc(pv_done, 1)

                def step(g, t, u, before, after):
                    for k in range(TG):
                        if after and k in SCORES_AT:
                            scores(g + 1, t + 1, 1 - u, SCORES_AT.index(k))
                        if k >= 2:
                            values(g, t, u, k - 2)
                        elif before:
                            values(g - 1, t - 1, 1 - u, TG - 2 + k)
                        transposes(g, t, u, k)
                    if not after:
                        values(g, t, u, TG - 2)
                        values(g, t, u, TG - 1)

                pe.wait_ge(loaded[j], ONE + (hp + 1) * 16 * LOADS)
                for c in range(SC):
                    scores(h * QT, 0, 0, c)
                tiles(pe, h, step)

            heads(pe, head)

        @block.scalar
        def _(act):
            def exps(g, u, c):
                if c == 0:
                    act.wait_ge(max_ready, ONE + g + 1)
                cs = slice(c * 2 * CH, (c + 1) * 2 * CH)
                act.activation(prob[u][:, cs], prob[u][:, cs], ACT.Exp, bias=nmx[:, u:u + 1],
                               accum_out=rs[:, u, c:c + 1]).then_inc(exp_ready, 1)

            def his(g, k):
                act.wait_ge(t_ready, ONE + g * TG + k + 1)
                act.wait_ge(pv_done, ONE + g * TG + k + 1)
                act.activation(hi[:, k % 2, :], ps_t[:, k % 2, :], ACT.Copy).then_inc(hi_ready, 1)

            def step(g, t, u, before, after):
                if not before:
                    exps(g, u, 0)
                for k in range(TG):
                    his(g, k)
                    if k in EXPS_AT:
                        c = EXPS_AT.index(k) + 1
                        if c < SC:
                            exps(g, u, c)
                        elif after:
                            exps(g + 1, 1 - u, 0)

            act.preload_act_table(ACT.Exp)
            heads(act, lambda h, j, hp: tiles(act, h, step))

        @block.vector
        def _(dve):
            def head(h, j, hp):
                def copies(g, u, c):
                    dve.wait_ge(s_ready, ONE + g * SC + c + 1)
                    dve.tensor_scalar(prob[u][:, c * 2 * CH:(c + 1) * 2 * CH], ps_s[:, c % 2, :], scale, -FLT_MAX,
                                      ALU.mult, ALU.max, accum_out=mx[:, u, c:c + 1]).then_inc(s_copied, 1)

                def maximum(g, u):
                    dve.wait_ge(s_copied, ONE + g * SC + SC + 2)
                    dve.tensor_reduce(nmx[:, u:u + 1], mx[:, u, :], AX.X, ALU.max, negate=True).then_inc(max_ready, 1)

                def los(g, u, k):
                    dve.wait_ge(hi_ready, ONE + g * TG + k + 1)
                    dve.tensor_tensor(lo[:, k % 2, :], ps_t[:, k % 2, :], hi[:, k % 2, :], ALU.subtract).then_inc(lo_ready, 1)

                def finish(g, t, u):
                    dve.tensor_reduce(rsum[:, u:u + 1], rs[:, u, :], AX.X, ALU.add).then_inc(fin_step, 1)
                    dve.wait_ge(fin_step, ONE + g * 3 + 1)
                    dve.reciprocal(rinv[:, u:u + 1], rsum[:, u:u + 1]).then_inc(fin_step, 1)
                    dve.wait_ge(fin_step, ONE + g * 3 + 2)
                    dve.wait_ge(pv_done, ONE + (g + 1) * TG + 2)
                    dve.tensor_scalar(otmp[:, :], ps_o[:, u, DH:P], rinv[:, u:u + 1], None, ALU.mult).then_inc(fin_step, 1)
                    dve.wait_ge(fin_step, ONE + g * 3 + 3)
                    dve.scalar_tensor_tensor(oh[:, j, ds(t, 1), :].rearrange("p a c -> p (a c)"), ps_o[:, u, 0:DH],
                                             rinv[:, u:u + 1], otmp[:, :], ALU.mult, ALU.add).then_inc(o_ready, 1)

                def step(g, t, u, before, after):
                    for k in range(TG):
                        if after and k in SCORES_AT:
                            copies(g + 1, 1 - u, SCORES_AT.index(k))
                        if after and k == SCORES_AT[-1]:
                            maximum(g + 1, 1 - u)
                        los(g, u, k)
                        if before and k == FINISH_AT:
                            finish(g - 1, t - 1, 1 - u)
                    if not after:
                        finish(g, t, u)

                if j == 0:
                    dve.wait_ge(o_stored, ONE + hp * 32)
                for c in range(SC):
                    copies(h * QT, 0, c)
                maximum(h * QT, 0)
                tiles(dve, h, step)

            dve.sem_inc(s_copied, 2)
            dve.sem_inc(lo_ready, 2)
            dve.sem_inc(pv_done, 2)
            dve.sem_inc(o_ready, 1)
            heads(dve, head)


def tokens_phase(nc, ctx, ident, x, attn_out, t1, u1):
    def sb(name, shape, dt=F32):
        return ctx.enter_context(nc.sbuf_tensor(name, shape, dt))

    sem, start_semaphores = phase_semaphores(nc, ctx, "")

    xin = sb("tk_x", [P, 2, 2, CH])
    oin = sb("tk_o", [P, 2, 4, 4 * DH])
    tt = sb("tk_t", [P, 2, 4, C])
    nt = sb("tk_n", [P, 2, 4, C])
    ut = sb("tk_u", [P, 2, 2, CH])
    stats, mv = sb("tk_stats", [P, 4, 6]), sb("tk_mv", [P, 4, 2])
    std, rstd, eps = sb("tk_std", [P, 4]), sb("tk_rstd", [P, 4]), sb("tk_eps", [P, 1])
    ps_x = ctx.enter_context(nc.psum_tensor("tk_ps_x", [P, 2, 2, CH], F32))
    ps_u = ctx.enter_context(nc.psum_tensor("tk_ps_u", [P, 2, 2, CH], F32))
    eps_ready = sem("tk_eps_ready")
    in_loaded = [sem(f"tk_in_loaded{j}") for j in range(2)]
    x_turned, t_ready, stats_step, var_ready, std_ready = (sem(f"tk_{n}") for n in ("x_turned", "t_ready", "stats_step", "var_ready", "std_ready"))
    n_ready, u_turned, u_ready, stored, stood = (sem(f"tk_{n}") for n in ("n_ready", "u_turned", "u_ready", "stored", "stood"))
    N = B * NCH

    def chunks(eng, body):
        with eng.Fori(0, B) as b:
            with eng.Fori(0, NCH // 2) as h:
                for j in range(2):
                    body(b * NCH + h * 2 + j, j, b, h * 2 + j)

    start_semaphores()
    with nc.Block() as block:
        @block.sync
        def _(sp):
            def body(n, j, b, c):
                sp.wait_ge(t_ready, ONE + n * 2)
                stand(sp, stood)
                sp.dma_start(xin[:, j, :, :], x[ds(b * C, C), ds(c * CH, CH)].rearrange("(k p) l -> p k l", p=P)).then_inc(in_loaded[j], 16)
                sp.dma_start(oin[:, j, :, :], attn_out[ds(b * 4, 4), :, ds(c * 4 * DH, 4 * DH)].rearrange("g p n -> p g n")).then_inc(in_loaded[j], 16)
                sp.wait_ge(t_ready, ONE + n * 2 + 6)
                stand(sp, stood)
                sp.dma_start(t1[n], tt[:, j, :, :].rearrange("p t c -> p (t c)")).then_inc(stored, 16)
                sp.wait_ge(u_ready, ONE + n + 1)
                stand(sp, stood)
                sp.dma_start(u1[n], ut[:, j, :, :].rearrange("p k l -> p (k l)")).then_inc(stored, 16)
            chunks(sp, body)
            sp.wait_ge(stored, ONE + 32 * N)

        @block.tensor
        def _(pe):
            def body(n, j, b, c):
                pe.wait_ge(in_loaded[j], ONE + b * (16 * NCH) + (c - j) * 16 + 32)
                pe.wait_ge(t_ready, ONE + n * 2)
                for t in range(4):
                    for k in range(2):
                        last = pe.transpose(ps_x[:, j, t // 2, (t % 2) * C + k * P:(t % 2) * C + (k + 1) * P],
                                            xin[:, j, k, t * P:(t + 1) * P], ident[:, :])
                last.then_inc(x_turned, 1)
                pe.wait_ge(n_ready, ONE + n + 1)
                pe.wait_ge(u_ready, ONE + n)
                for t in range(4):
                    for k in range(2):
                        last = pe.transpose(ps_u[:, j, k, t * P:(t + 1) * P], nt[:, j, t, k * P:(k + 1) * P], ident[:, :])
                last.then_inc(u_turned, 1)
            chunks(pe, body)

        @block.scalar
        def _(act):
            def body(n, j, b, c):
                act.wait_ge(var_ready, ONE + n + 1)
                act.activation(std[:, :], mv[:, :, 1], ACT.Sqrt, bias=eps[:, 0:1]).then_inc(std_ready, 1)
                act.wait_ge(u_turned, ONE + n + 1)
                act.wait_ge(stored, ONE + n * 32)
                act.activation(ut[:, j, :, :], ps_u[:, j, :, :], ACT.Copy).then_inc(u_ready, 1)
            act.wait_ge(eps_ready, ONE + 1)
            chunks(act, body)

        @block.vector
        def _(dve):
            def body(n, j, b, c):
                dve.wait_ge(x_turned, ONE + n + 1)
                dve.wait_ge(stored, ONE + n * 32)
                for h in range(2):
                    o = oin[:, j, :, :].rearrange("p g (t c) -> p t g c", t=4)[:, 2 * h:2 * h + 2]
                    dve.tensor_tensor(tt[:, j, 2 * h:2 * h + 2, :].rearrange("p t (g c) -> p t g c", g=4),
                                      ps_x[:, j, h, :].rearrange("p (t g c) -> p t g c", t=2, g=4), o, ALU.add).then_inc(t_ready, 1)
                dve.wait_ge(t_ready, ONE + n * 2 + 6)
                for t in range(4):
                    last = dve.bn_stats(stats[:, t, :], tt[:, j, t, :])
                last.then_inc(stats_step, 1)
                dve.wait_ge(stats_step, ONE + n * 2 + 1)
                stand(dve, stood)
                for t in range(4):
                    last = dve.bn_aggr(mv[:, t, :], stats[:, t, :])
                last.then_inc(var_ready, 1)
                dve.wait_ge(std_ready, ONE + n + 1)
                dve.reciprocal(rstd[:, :], std[:, :]).then_inc(stats_step, 1)
                dve.wait_ge(stats_step, ONE + n * 2 + 2)
                dve.wait_ge(u_turned, ONE + n)
                for t in range(4):
                    last = dve.tensor_scalar(nt[:, j, t, :], tt[:, j, t, :], mv[:, t, 0:1], rstd[:, t:t + 1],
                                             ALU.subtract, ALU.mult)
                last.then_inc(n_ready, 1)
            dve.memset(eps[:, :], GN_EPS).then_inc(eps_ready, 1)
            dve.sem_inc(t_ready, 4)
            chunks(dve, body)


def mamba_phase(nc, ctx, ident, w, u1, m_dirs):
    def sb(name, shape, dt=F32):
        return ctx.enter_context(nc.sbuf_tensor(name, shape, dt))

    sem, start_semaphores = phase_semaphores(nc, ctx, "mb_")

    N = B * NCH
    K = 4
    S = 16
    R = 16
    BC = 2 * S
    NX = 3 * BC + R
    W = CH + 3

    win = sb("win", [P, 2, 2, 8 * P])
    wx = sb("wx", [P, 2, K, NX])
    wdt = sb("wdt", [NX, 2, K * P])
    wout = sb("wout", [P, 2, K, C])
    cw, cb = sb("cw", [P, 2, K, 4]), sb("cb", [P, 2, K])
    dtb, dskip = sb("dtb", [P, 2, K]), sb("dskip", [P, 2, K])
    amat = sb("amat", [P, 2, K, S])
    keep = sb("keep", [P, N])
    one = sb("one", [P, 1])
    u = sb("mb_u", [P, 2, 2, CH])
    xpre = sb("xpre", [P, K, W])
    halo = sb("halo", [P, 2, K, 3])
    xs = sb("xs", [P, 2, K, CH])
    zs = sb("zs", [P, 2, K, CH])
    dt = sb("dt", [P, 2, K, CH])
    dtx = sb("dtx", [P, 2, K, CH])
    sp_tmp = sb("sp_tmp", [P, K, CH])
    xdt = sb("xdt", [NX, CH])
    xbc = sb("xbc", [3 * BC, 2, CH], BF16)
    xres = sb("xres", [3 * BC, CH])
    pick = sb("pick", [3 * BC, BC], BF16)
    bb, cc = sb("bb", [P, 4, CH]), sb("cc", [P, 4, CH])
    da = sb("da", [P, 2, K, CH])
    hh = sb("hh", [P, 4, K, CH])
    state = sb("state", [P, 2, K, S])
    mo = sb("mo", [P, 4, C])
    ps_a = ctx.enter_context(nc.psum_tensor("mb_ps_a", [P, 2, CH], F32))
    ps_b = ctx.enter_context(nc.psum_tensor("mb_ps_b", [P, 2, CH], F32))
    ps_y = ctx.enter_context(nc.psum_tensor("mb_ps_y", [P, K, CH], F32))

    w_loaded, consts, a_exp, a_neg = sem("w_loaded"), sem("consts"), sem("a_exp"), sem("a_neg")
    u_loaded = [sem(f"u_loaded{j}") for j in range(2)]
    a_ready, a_free = sem("a_ready"), sem("a_free")
    bc_ready, bc_copied = sem("bc_ready"), sem("bc_copied")
    conv_step, conv_done, silu_done, soft_step, soft_done = (sem(n) for n in ("conv_step", "conv_done", "silu_done", "soft_step", "soft_done"))
    x_part1, x_res1, x_part2, x_split = (sem(n) for n in ("x_part1", "x_res1", "x_part2", "x_split"))
    dt_ready, dtx_ready = sem("dt_ready"), sem("dtx_ready")
    da_ready, dbx_ready, scanned, saved, hc_ready, summed = (sem(n) for n in ("da_ready", "dbx_ready", "scanned", "saved", "hc_ready", "summed"))
    kept, y_ready, gated, mo_stored, stood, out_copied = (sem(n) for n in ("kept", "y_ready", "gated", "mo_stored", "stood", "out_copied"))

    USES = 15

    PE_IN, PE_OUT, PE_X, PE_DT = (1, 2, 6, 7), (3, 4), 9, (11, 12)
    ACT_IN, ACT_OUT, ACT_SILU, ACT_X, ACT_DT, ACT_SOFT = (2, 3, 7, 8), (5, 6), 9, 10, (12, 13), 13
    DVE_SKIP, DVE_CONV, DVE_SPLIT, DVE_WEIGH = 1, (5, 7), 10, 15
    POOL_GATE, POOL_SOFT = 4, 15
    AHEAD = 4
    N_CONSTS = 9

    class Step:
        def __init__(s, n, j, tail=True, front=True):
            s.n, s.j, s.tail, s.front = n, j, tail, front
            s.k = n * 2 + j
            s.use0, s.bank0 = s.k * USES + USES - 4, (j + 1) % 2
            s.nj, s.nn = 1 - j, n + j
            s.fronts = s.k + 1
            s.scanning = True
            s.x_use, s.out_use = (0 if tail else 2), (K if front else 0)

    def before():
        s = Step(0, 0, tail=False)
        s.k, s.use0, s.bank0, s.nj, s.nn = -1, -2, 0, 0, 0
        s.scanning = False
        return s

    def after():
        s = Step(N, 0, front=False)
        s.use0, s.bank0 = s.use0 - (USES - 2), (s.bank0 + USES - 2) % 2
        s.fronts = s.k
        return s

    def run(eng, begin, step, end):
        begin(before())
        step(Step(0, 0, tail=False))
        step(Step(0, 1))
        with eng.Fori(1, N - 1) as n:
            for j in range(2):
                step(Step(n, j))
        step(Step(N - 1, 0))
        step(Step(N - 1, 1, front=False))
        end(after())

    def in_use(s, e):
        return s.x_use + e if e < K else 2 + e

    def bank(s, idx):
        return (s.bank0 + idx) % 2

    start_semaphores()
    with nc.Block() as block:
        @block.sync
        def _(sp):
            n = 0
            for dst, src in ((win[:, :, :, :], w["in_proj_w"].rearrange("j k p e -> p j k e")),
                             (wx[:, :, :, 0:BC], w["x_proj_w"][:, :, :, R:].rearrange("j k p e -> p j k e")),
                             (wx[:, :, :, BC:2 * BC], w["x_proj_w"][:, :, :, R:].rearrange("j k p e -> p j k e")),
                             (wx[:, :, :, 2 * BC:3 * BC], w["x_proj_w"][:, :, :, R:].rearrange("j k p e -> p j k e")),
                             (wx[:, :, :, 3 * BC:NX], w["x_proj_w"][:, :, :, 0:R].rearrange("j k p e -> p j k e")),
                             (wdt[3 * BC:NX, :, :], w["dt_proj_w"].rearrange("j r d -> r j d")),
                             (wout[:, :, :, :], w["out_proj_w"].rearrange("j k p e -> p j k e")),
                             (cw[:, :, :, :], w["conv_w"].rearrange("j (k p) t -> p j k t", p=P)),
                             (amat[:, :, :, :], w["A_log"].rearrange("j (k p) s -> p j k s", p=P))):
                for j in range(2):
                    sp.dma_start(dst[:, j], src[:, j]).then_inc(w_loaded, 16)
                    n += 1
            for dst, src in ((cb, "conv_b"), (dtb, "dt_proj_b"), (dskip, "Dp")):
                for j in range(2):
                    for k in range(K):
                        sp.dma_start(dst[:, j, k:k + 1], w[src][j, k * P:(k + 1) * P].unsqueeze(1)).then_inc(w_loaded, 16)
                        n += 1
            assert n == N_MAMBA_W

            def load(k, j, n):
                sp.dma_start(u[:, j, :, :].rearrange("p k l -> p (k l)"), u1[n if j == 0 else (N - 1) - n]).then_inc(u_loaded[j], 16)

            def store(k, j, n):
                sp.wait_ge(out_copied, ONE + (k + 1) * 2)
                stand(sp, stood)
                sp.dma_start(m_dirs[j, n], mo[:, :, :].rearrange("p t c -> p (t c)")).then_inc(mo_stored, 16)

            load(0, 0, 0)
            load(1, 1, 0)
            with sp.Fori(0, N - 1) as n:
                for j in range(2):
                    sp.wait_ge(dtx_ready, ONE + n * 2 + j + 1)
                    stand(sp, stood)
                    load(n * 2 + j + 2, j, n + 1)
                    store(n * 2 + j, j, n)
            store(2 * N - 2, 0, N - 1)
            store(2 * N - 1, 1, N - 1)
            sp.wait_ge(mo_stored, ONE + 32 * N)

        @block.tensor
        def _(pe):
            def fill(s, idx, mms):
                pe.wait_ge(a_free, ONE + s.use0 + idx + 1)
                for out, lhsT, rhs, start, stop in mms(ps_a[:, bank(s, idx), :]):
                    last = pe.matmul(out, lhsT, rhs, start=start, stop=stop)
                last.then_inc(a_ready, 1)

            def in_proj(s, e):
                if e == 0:
                    pe.wait_ge(u_loaded[s.nj], ONE + (s.nn + 1) * 16)
                fill(s, in_use(s, e), lambda ps: [(ps, win[:, s.nj, k, e * P:(e + 1) * P], u[:, s.nj, k, :], k == 0, k == 1)
                                           for k in range(2)])

            def x_proj(s):
                pe.wait_ge(silu_done, ONE + (s.k + 2) * 2 - 1)
                fill(s, 10, lambda ps: [(ps[0:NX], wx[:, s.nj, k, :], xs[:, s.nj, k, :], k == 0, k == K - 1)
                                        for k in range(K)])

            def dt_proj(s, k):
                if k == 0:
                    pe.wait_ge(a_free, ONE + s.use0 + 13)
                fill(s, 11 + k, lambda ps: [(ps, wdt[3 * BC:NX, s.nj, k * P:(k + 1) * P], xdt[3 * BC:NX, :], True, True)])

            def spread(s, i):
                if i == S:
                    pe.wait_ge(x_split, ONE + s.k + 2)
                for n in range(2):
                    pe.wait_ge(bc_copied, ONE + s.k * 2 * S + 2 * i + n + 1)
                    row = S * n + i % S
                    pe.matmul(ps_b[:, n, :], pick[:, row:row + 1].broadcast_to([3 * BC, P]),
                              xbc[:, s.j if i < S else s.nj, :], start=True, stop=True).then_inc(bc_ready, 1)

            def accumulate(s, i):
                pe.wait_ge(hc_ready, ONE + s.k * S + i + 5)
                if i == 0:
                    pe.wait_ge(y_ready, ONE + s.k * K)
                for k in range(K):
                    last = pe.matmul(ps_y[:, k, :], ident[:, :], hh[:, i % 4, k, :], start=(i == 0), stop=(i % S == S - 1))
                last.then_inc(summed, 1)

            def tail(s, h):
                if h == 0:
                    pe.wait_ge(gated, ONE + s.k)
                if True:
                    fill(s, s.out_use + h, lambda ps: [(ps[:, t * C:(t + 1) * C], sp_tmp[:, k, (2 * h + t) * P:(2 * h + t + 1) * P],
                                            wout[:, s.nj, k, :], k == 0, k == K - 1) for t in range(2) for k in range(K)])

            def front(s, slot=None):
                for at, work in ([(at, lambda q=q: [in_proj(s, e) for e in (2 * q, 2 * q + 1)]) for q, at in enumerate(PE_IN)] +
                                 [(PE_X, lambda: x_proj(s))] +
                                 [(at, lambda q=q: [dt_proj(s, k) for k in (2 * q, 2 * q + 1)]) for q, at in enumerate(PE_DT)]):
                    if slot in (None, at):
                        work()

            def step(s):
                for i in range(S):
                    if s.front:
                        front(s, i)
                    if i + AHEAD < S or s.front:
                        spread(s, i + AHEAD)
                    if i or s.tail:
                        accumulate(s, i - 1)
                    if i in PE_OUT and s.tail:
                        tail(s, PE_OUT.index(i))

            def begin(s):
                front(s)
                for i in range(AHEAD):
                    spread(s, S + i)

            def end(s):
                accumulate(s, -1)
                tail(s, 0)
                tail(s, 1)

            pe.wait_ge(consts, ONE + N_CONSTS)
            pe.wait_ge(w_loaded, ONE + 16 * N_MAMBA_W)
            run(pe, begin, step, end)

        @block.scalar
        def _(act):
            def data(j):
                return slice(3, W) if j == 0 else slice(0, CH)

            def in_copy(s, e):
                act.wait_ge(a_ready, ONE + s.use0 + in_use(s, e) + 1)
                if e == 0:
                    act.wait_ge(conv_done, ONE + s.k + 1)
                if e == K and s.tail:
                    act.wait_ge(gated, ONE + s.k)
                dst = xpre[:, e, data(s.nj)] if e < K else zs[:, s.nj, e - K, :]
                act.activation(dst, ps_a[:, bank(s, in_use(s, e)), :], ACT.Copy).then_inc(a_free, 1)

            def silus(s):
                act.wait_ge(conv_done, ONE + s.k + 2)
                act.activation(xs[:, s.nj], xs[:, s.nj], ACT.Silu).then_inc(silu_done, 1)
                act.wait_ge(a_free, ONE + s.use0 + 2 + 8 + 2)
                act.activation(zs[:, s.nj], zs[:, s.nj], ACT.Silu).then_inc(silu_done, 1)
                act.preload_act_table_set("natural_log_exp_and_others")

            def x_copy(s):
                act.wait_ge(a_ready, ONE + s.use0 + 11)
                act.activation(xbc[:, s.nj, :], ps_a[0:3 * BC, bank(s, 10), :], ACT.Copy).then_inc(x_part1, 1)
                act.activation(xdt[3 * BC:NX, :], ps_a[3 * BC:NX, bank(s, 10), :], ACT.Copy)
                act.wait_ge(x_res1, ONE + s.k + 2)
                for q in (1, 2):
                    rows = slice(q * BC, (q + 1) * BC)
                    last = act.activation(xbc[rows, s.nj, :], xres[rows, :], ACT.Copy)
                last.then_inc(x_part2, 1)
                act.wait_ge(x_part2, ONE + s.k + 2)
                act.sem_inc(a_free, 1)

            def dt_parts(s, k):
                act.wait_ge(a_ready, ONE + s.use0 + 12 + k)
                if k == 0:
                    if s.scanning:
                        act.wait_ge(da_ready, ONE + s.k * S * K)
                    act.wait_ge(dt_ready, ONE + s.k + 1)
                act.activation(dt[:, s.nj, k, :], ps_a[:, bank(s, 11 + k), :], ACT.Relu, bias=dtb[:, s.nj, k:k + 1])
                act.activation(sp_tmp[:, k, :], ps_a[:, bank(s, 11 + k), :], ACT.Abs, bias=dtb[:, s.nj, k:k + 1]).then_inc(a_free, 1)

            def soft(s):
                act.wait_ge(a_free, ONE + s.use0 + USES + 2)
                act.activation(sp_tmp[:], sp_tmp[:], ACT.Exp, scale=-1.0).then_inc(soft_step, 1)
                act.wait_ge(soft_step, ONE + s.k + 2)
                act.activation(sp_tmp[:], sp_tmp[:], ACT.Ln, bias=one[:, 0:1]).then_inc(soft_done, 1)

            def spread_copy(s, i):
                act.wait_ge(bc_ready, ONE + s.k * 2 * S + 2 * i + 1)
                act.wait_ge(dbx_ready, ONE + s.k * S + i + 1)
                act.activation(bb[:, i % 4, :], ps_b[:, 0, :], ACT.Copy).then_inc(bc_copied, 1)
                act.wait_ge(bc_ready, ONE + s.k * 2 * S + 2 * i + 2)
                act.wait_ge(hc_ready, ONE + s.k * S + i + 1)
                act.activation(cc[:, i % 4, :], ps_b[:, 1, :], ACT.Copy).then_inc(bc_copied, 1)

            def decays(s, i):
                act.wait_ge(scanned, ONE + s.k * S + i + 1)
                j = s.j if i < S else s.nj
                if i == S:
                    act.wait_ge(dt_ready, ONE + s.k + 2)
                for k in range(K):
                    act.activation(da[:, i % 2, k, :], dt[:, j, k, :], ACT.Exp,
                                   scale=amat[:, j, k, i % S:i % S + 1]).then_inc(da_ready, 1)

            def tail(s, h):
                if h == 0:
                    act.wait_ge(mo_stored, ONE + s.k * 16 - 16)
                if True:
                    act.wait_ge(a_ready, ONE + s.use0 + s.out_use + h + 1)
                    act.activation(mo[:, 2 * h:2 * h + 2, :].rearrange("p t c -> p (t c)"), ps_a[:, bank(s, s.out_use + h), :],
                                   ACT.Copy).then_inc(a_free, 1)
                if h == 1:
                    act.wait_ge(a_free, ONE + s.use0 + s.out_use + 2 + 2)
                    act.sem_inc(out_copied, 2)

            def front(s, slot=None):
                for at, work in ([(at, lambda q=q: [in_copy(s, e) for e in (2 * q, 2 * q + 1)]) for q, at in enumerate(ACT_IN)] +
                                 [(ACT_SILU, lambda: silus(s)), (ACT_X, lambda: x_copy(s))] +
                                 [(at, lambda q=q: [dt_parts(s, k) for k in (2 * q, 2 * q + 1)]) for q, at in enumerate(ACT_DT)] +
                                 [(ACT_SOFT, lambda: soft(s))]):
                    if slot in (None, at):
                        work()

            def step(s):
                for i in range(S):
                    if i + 2 < S or s.front:
                        spread_copy(s, i + 2)
                    if i + 1 < S or s.front:
                        decays(s, i + 1)
                    if i in ACT_OUT and s.tail:
                        tail(s, ACT_OUT.index(i))
                    if s.front:
                        front(s, i)

            act.wait_ge(w_loaded, ONE + 16 * N_MAMBA_W)
            act.activation(amat[:], amat[:], ACT.Exp).then_inc(a_exp, 1)
            act.wait_ge(a_neg, ONE + 1)

            def begin(s):
                front(s)
                spread_copy(s, S)
                spread_copy(s, S + 1)
                decays(s, S)

            run(act, begin, step, lambda s: [tail(s, h) for h in range(2)])

        @block.gpsimd
        def _(pool):
            def inputs(s, i):
                if i == 0:
                    pool.wait_ge(dtx_ready, ONE + s.k + 1)
                pool.wait_ge(bc_copied, ONE + s.k * 2 * S + 2 * i + 3)
                pool.wait_ge(summed, ONE + s.k * S + i + 1)
                pool.tensor_tensor(hh[:, i % 4, :, :], dtx[:, s.j, :, :], bb[:, i % 4, :].unsqueeze(1).broadcast_to([P, K, CH]),
                                   ALU.mult).then_inc(dbx_ready, 1)

            def softplus(s):
                pool.wait_ge(soft_done, ONE + s.k + 2)
                pool.tensor_tensor(dt[:, s.nj], dt[:, s.nj], sp_tmp[:], ALU.add).then_inc(dt_ready, 1)

            def tail(s):
                pool.wait_ge(y_ready, ONE + s.k * K)
                pool.wait_ge(dt_ready, ONE + s.fronts)
                dst = sp_tmp[:] if s.nj == 0 else sp_tmp[:, :, ::-1]
                pool.tensor_tensor(dst, xs[:, s.nj], zs[:, s.nj], ALU.mult).then_inc(gated, 1)

            def front(s, slot=None):
                if slot in (None, POOL_SOFT):
                    softplus(s)

            def step(s):
                for i in range(S):
                    inputs(s, i)
                    if i == POOL_GATE and s.tail:
                        tail(s)
                    if s.front:
                        front(s, i)

            pool.memset(keep[:, :], 1.0).then_inc(consts, 1)
            pool.wait_ge(consts, ONE + 1)
            pool.memset(keep[:, :].rearrange("p (b n) -> p b n", b=B)[:, :, 0:1], 0.0).then_inc(consts, 1)
            pool.memset(one[:, :], 1.0).then_inc(consts, 1)
            pool.memset(state[:], 0.0).then_inc(consts, 1)
            pool.memset(halo[:], 0.0).then_inc(consts, 1)
            pool.memset(pick[:, :], 0.0).then_inc(consts, 1)
            for q in range(3):
                pool.wait_ge(consts, ONE + 6 + q)
                pool.affine_select(out=pick[:, :], in_=pick[:, :], compare_op=ALU.not_equal, fill=1.0, base=-q * BC,
                                   pattern=[[-1, BC]], channel_multiplier=1).then_inc(consts, 1)
            pool.wait_ge(consts, ONE + N_CONSTS)
            run(pool, front, step, tail)

        @block.vector
        def _(dve):
            TAPS = 6

            def conv(s, part):
                j = s.nj
                edge, spot = (slice(CH, W), slice(0, 3)) if j == 0 else (slice(0, 3), slice(CH, W))
                base = (s.k + 1) * TAPS
                if part == 0:
                    dve.wait_ge(a_free, ONE + s.use0 + s.x_use + K + 2)
                    dve.wait_ge(conv_done, ONE + s.k + 1)
                    if s.tail:
                        dve.wait_ge(gated, ONE + s.k)
                    dve.tensor_scalar(xpre[:, :, spot], halo[:, j], keep[:, s.nn:s.nn + 1] if isinstance(s.nn, int) else keep[:, ds(s.nn, 1)],
                                      None, ALU.mult).then_inc(conv_step, 1)
                    dve.wait_ge(conv_step, ONE + base + 1)
                    dve.tensor_copy(halo[:, j], xpre[:, :, edge]).then_inc(conv_step, 1)
                for tap in ((3, 2) if part == 0 else (1, 0)):
                    at = tap if j == 0 else 3 - tap
                    for k in range(K):
                        src = xpre[:, k, at:at + CH]
                        if tap == 3:
                            last = dve.tensor_scalar(xs[:, j, k, :], src, cw[:, j, k, 3:4], cb[:, j, k:k + 1], ALU.mult, ALU.add)
                        else:
                            last = dve.scalar_tensor_tensor(xs[:, j, k, :], src, cw[:, j, k, tap:tap + 1], xs[:, j, k, :],
                                                            ALU.mult, ALU.add)
                    if tap:
                        last.then_inc(conv_step, 1)
                        dve.wait_ge(conv_step, ONE + base + 2 + 4 - tap)
                    else:
                        last.then_inc(conv_done, 1)
                if part == 1:
                    dve.sem_inc(conv_step, 1)

            def split(s):
                dve.wait_ge(x_part1, ONE + s.k + 2)
                for q in (1, 2):
                    rows = slice(q * BC, (q + 1) * BC)
                    last = dve.tensor_tensor(xres[rows, :], ps_a[rows, bank(s, 10), :], xbc[rows, s.nj, :], ALU.subtract)
                last.then_inc(x_res1, 1)
                dve.wait_ge(x_part2, ONE + s.k + 2)
                rows = slice(2 * BC, 3 * BC)
                dve.tensor_tensor(xbc[rows, s.nj, :], xres[rows, :], xbc[rows, s.nj, :], ALU.subtract).then_inc(x_split, 1)

            def scans(s, i):
                dve.wait_ge(dbx_ready, ONE + s.k * S + i + 5)
                if i == 0:
                    dve.wait_ge(kept, ONE + s.k + 1)
                for k in range(K):
                    dve.wait_ge(da_ready, ONE + (s.k * S + i) * K + k + 1)
                    h, a = hh[:, i % 4, k, :], da[:, i % 2, k, :]
                    if s.j:
                        h, a = h[:, ::-1], a[:, ::-1]
                    last = dve.tensor_tensor_scan(h, a, h, state[:, s.j, k, i:i + 1], ALU.mult, ALU.add)
                last.then_inc(scanned, 1)

            def save(s, i):
                dve.wait_ge(scanned, ONE + s.k * S + i + 3)
                j = s.j if i >= 0 else s.nj
                end = CH - 1 if j == 0 else 0
                dve.tensor_copy(state[:, j, :, i % S:i % S + 1], hh[:, i % 4, :, end:end + 1]).then_inc(saved, 1)

            def weigh(s):
                dve.wait_ge(dt_ready, ONE + s.k + 2)
                if s.scanning:
                    dve.wait_ge(dbx_ready, ONE + s.k * S + 4)
                dve.tensor_tensor(dtx[:, s.nj], dt[:, s.nj], xs[:, s.nj], ALU.mult).then_inc(dtx_ready, 1)

            def outputs(s, i):
                dve.wait_ge(saved, ONE + s.k * S + i + 1)
                dve.wait_ge(bc_copied, ONE + s.k * 2 * S + 2 * i + 4)
                dve.tensor_tensor(hh[:, i % 4], hh[:, i % 4], cc[:, i % 4, :].unsqueeze(1).broadcast_to([P, K, CH]),
                                  ALU.mult).then_inc(hc_ready, 1)

            def tail(s):
                dve.wait_ge(summed, ONE + s.k * S + 4)
                for k in range(K):
                    dve.scalar_tensor_tensor(xs[:, s.nj, k, :], xs[:, s.nj, k, :], dskip[:, s.nj, k:k + 1], ps_y[:, k, :],
                                             ALU.mult, ALU.add).then_inc(y_ready, 1)

            def front(s, slot=None):
                for at, work in ((DVE_CONV[0], lambda: conv(s, 0)), (DVE_CONV[1], lambda: conv(s, 1)), (DVE_SPLIT, lambda: split(s)), (DVE_WEIGH, lambda: weigh(s))):
                    if slot in (None, at):
                        work()

            def step(s):
                for i in range(S):
                    if i or s.tail:
                        save(s, i - 1)
                    if i == 0:
                        dve.wait_ge(saved, ONE + s.k * S)
                        dve.tensor_scalar(state[:, s.j], state[:, s.j], keep[:, s.n:s.n + 1] if isinstance(s.n, int) else keep[:, ds(s.n, 1)],
                                          None, ALU.mult).then_inc(kept, 1)
                    scans(s, i)
                    if i or s.tail:
                        outputs(s, i - 1)
                    if i == DVE_SKIP and s.tail:
                        tail(s)
                    if s.front:
                        front(s, i)

            def end(s):
                save(s, -1)
                outputs(s, -1)
                tail(s)

            for t, v in ((a_free, 2), (bc_copied, 2), (dbx_ready, 4), (scanned, 2), (hc_ready, 4), (summed, 4)):
                dve.sem_inc(t, v)
            dve.wait_ge(a_exp, ONE + 1)
            dve.tensor_scalar(amat[:], amat[:], -1.0, None, ALU.mult).then_inc(a_neg, 1)
            dve.wait_ge(consts, ONE + N_CONSTS)
            run(dve, front, step, end)


def mlp_phase(nc, ctx, ident, w, t1, m_dirs, t2, xn, lg, xbuf):
    def sb(name, shape, dt=F32):
        return ctx.enter_context(nc.sbuf_tensor("ml_" + name, shape, dt))

    sem, start_semaphores = phase_semaphores(nc, ctx, "ml_")

    N = B * NCH
    FB = 4
    w1, w2 = sb("w1", [P, 2, FB * P]), sb("w2", [P, FB, C])
    gw = sb("gw", [P, 2, EXPERTS])
    b1, lng, lnb = sb("b1", [P, FB]), sb("lng", [P, 2]), sb("lnb", [P, 2])
    b2, gb = sb("b2", [P, C]), sb("gb", [P, EXPERTS])
    eps, zero = sb("eps", [P, 1]), sb("zero", [P, 4 * C])
    min_, bin_, tin = sb("m", [P, 2, 4, C]), sb("back", [P, 2, 4, C]), sb("t1", [P, 2, 4, C])
    stats, mv = sb("stats", [P, 8, 6]), sb("mv", [P, 8, 2])
    std, rstd = sb("std", [P, 8]), sb("rstd", [P, 8])
    ht, xt = sb("ht", [P, 2, 2, CH]), sb("xt", [P, 2, CH])
    t2cur, xcur = sb("t2", [P, 2, 4, C]), sb("xn", [P, 2, 4, C])
    hid, pt = sb("hid", [P, 2, CH]), sb("pt", [P, FB, CH])
    ps_t = ctx.enter_context(nc.psum_tensor("ml_ps_t", [P, 2, CH], F32))
    ps_f = ctx.enter_context(nc.psum_tensor("ml_ps_f", [P, 2, CH], F32))
    ps_y = ctx.enter_context(nc.psum_tensor("ml_ps_y", [P, 2, CH], F32))
    ps_l = ctx.enter_context(nc.psum_tensor("ml_ps_l", [P, 4 * EXPERTS], F32))

    w_loaded, consts, zeroed = sem("w_loaded"), sem("consts"), sem("zeroed")
    m_loaded = [sem(f"m_loaded{j}") for j in range(2)]
    t_loaded = [sem(f"t_loaded{j}") for j in range(2)]
    t2_stored = [sem(f"t2_stored{j}") for j in range(2)]
    xn_stored = [sem(f"xn_stored{j}") for j in range(2)]
    m_ready, skip_step, skip_ready, bn_step, var_ready, std_ready, rstd_ready = (
        sem(n) for n in ("m_ready", "skip_step", "skip_ready", "bn_step", "var_ready", "std_ready", "rstd_ready"))
    h_normed, x_normed, turned, turned_copied = (sem(n) for n in ("h_normed", "x_normed", "turned", "turned_copied"))
    f_ready, hid_ready, act_ready, y_ready, t2_ready = (sem(n) for n in ("f_ready", "hid_ready", "act_ready", "y_ready", "t2_ready"))
    l_ready, lg_ready, stood, m_copied = sem("l_ready"), sem("lg_ready"), sem("stood"), sem("m_copied")

    def run(eng, step):
        step(-1, 1, None)
        step(0, 0, None)
        with eng.Fori(0, (N - 4) // 2) as h:
            step(h * 2 + 1, 1, h)
            step(h * 2 + 2, 0, h)
        step(N - 3, 1, None)
        step(N - 2, 0, None)
        step(N - 1, 1, None)
        step(N, 0, None)

    def has(i, what):
        if not isinstance(i, int):
            return True
        return {"load": i + 2 < N, "a": i + 1 < N, "b": 0 <= i < N, "c": i >= 1}[what]

    def loads(i, h):
        return h + 2 if h is not None else (i + 1) // 2 + 1

    def use(i, what):
        if isinstance(i, int) and i <= 0:
            return i + 1
        if isinstance(i, int) and i >= N - 1:
            return i + N - 1
        return i * 2 + (what == "c")

    start_semaphores()
    with nc.Block() as block:
        @block.sync
        def _(sp):
            n = 0
            for dst, src in ((w1[:, :, :], w["attn_w1"].rearrange("k p e -> p k e")),
                             (w2[:, :, :], w["attn_w2"].rearrange("k p e -> p k e")),
                             (gw[:, :, :], w["ffn_gate_w"].rearrange("(k p) e -> p k e", p=P)),
                             (b2[:, :], w["attn_b2"].partition_broadcast(P)),
                             (gb[:, :], w["ffn_gate_b"].partition_broadcast(P))):
                sp.dma_start(dst, src).then_inc(w_loaded, 16)
                n += 1
            for dst, src, cut in ((b1, "attn_b1", FB), (lng, "attn_ln_g", 2), (lnb, "attn_ln_b", 2)):
                for k in range(cut):
                    sp.dma_start(dst[:, k:k + 1], w[src][k * P:(k + 1) * P].unsqueeze(1)).then_inc(w_loaded, 16)
                    n += 1
            assert n == N_MLP_W

            def flat(t):
                return t.rearrange("p t c -> p (t c)")

            def load_m(c, j):
                sp.dma_start(flat(bin_[:, j]), m_dirs[1, (c + NCH) % N]).then_inc(m_loaded[j], 16)
                sp.dma_start(flat(min_[:, j]), m_dirs[0, c]).then_inc(m_loaded[j], 16)

            def step(i, j, h):
                q = 1 - j
                if has(i, "a"):
                    sp.wait_ge(t2_ready, ONE + i * 2 + 4)
                    stand(sp, stood)
                    sp.dma_start(flat(tin[:, q]), t1[i + 1]).then_inc(t_loaded[q], 16)
                if has(i, "load") and not (isinstance(i, int) and i < 0):
                    sp.wait_ge(m_copied, ONE + i + 1)
                    sp.wait_ge(skip_ready, ONE + i + 1)
                    stand(sp, stood)
                    load_m(i + 2, j)
                if has(i, "c"):
                    sp.wait_ge(x_normed, ONE + i)
                    stand(sp, stood)
                    sp.dma_start(xn[i - 1], flat(xcur[:, q])).then_inc(xn_stored[q], 16)
                if has(i, "b"):
                    sp.wait_ge(t2_ready, ONE + i * 2 + 6)
                    stand(sp, stood)
                    sp.dma_start(t2[i], flat(t2cur[:, j])).then_inc(t2_stored[j], 16)

            load_m(0, 0)
            load_m(1, 1)
            run(sp, step)
            for j in range(2):
                sp.wait_ge(xn_stored[j], ONE + 8 * N)
                sp.wait_ge(t2_stored[j], ONE + 8 * N)
            sp.wait_ge(consts, ONE + 1)
            rows = xbuf[0:EXPERTS * CAP, :].rearrange("(n p t) c -> n p (t c)", p=P, t=4)
            for n in range(EXPERTS * CAP // (4 * P)):
                sp.dma_start(rows[n], zero[:, :]).then_inc(zeroed, 16)
            sp.wait_ge(zeroed, ONE + 16 * (EXPERTS * CAP // (4 * P)))

        @block.gpsimd
        def _(pool):
            pool.memset(zero[:, :], 0.0).then_inc(consts, 1)
            pool.memset(eps[:, :], GN_EPS).then_inc(consts, 1)
            pool.memset(mv[:, :, :], 1.0).then_inc(consts, 1)
            pool.wait_ge(w_loaded, ONE + 16 * N_MLP_W)

            def step(i, j, h):
                q = 1 - j
                if has(i, "a"):
                    pool.wait_ge(m_loaded[q], ONE + loads(i, h) * 32)
                    pool.tensor_tensor(min_[:, q], min_[:, q], bin_[:, q], ALU.add).then_inc(m_ready, 1)
                    pool.wait_ge(m_ready, ONE + i + 2)
                    pool.wait_ge(t_loaded[q], ONE + loads(i, h) * 16)
                    pool.tensor_tensor(tin[:, q], tin[:, q], min_[:, q], ALU.add).then_inc(skip_step, 1)
                    pool.wait_ge(skip_step, ONE + i + 2)
                    pool.tensor_tensor(tin[:, q], tin[:, q], b2[:, :].unsqueeze(1).broadcast_to([P, 4, C]), ALU.add).then_inc(skip_ready, 1)
            run(pool, step)

        @block.tensor
        def _(pe):
            def turn(i, what, src, count):
                pe.wait_ge(count, ONE + (i + 2 if what == "a" else i))
                pe.wait_ge(turned_copied, ONE + use(i, what))
                for t in range(4):
                    for k in range(2):
                        last = pe.transpose(ps_t[:, k, t * P:(t + 1) * P], src(t, k), ident[:, :])
                last.then_inc(turned, 1)

            def step(i, j, h):
                q = 1 - j
                if has(i, "b"):
                    pe.wait_ge(m_copied, ONE + i + 1)
                    for f in range(FB):
                        pe.wait_ge(hid_ready, ONE + i * FB + f + 1)
                        for k in range(2):
                            last = pe.matmul(ps_f[:, f % 2, :], w1[:, k, f * P:(f + 1) * P], ht[:, j, k, :], start=(k == 0), stop=(k == 1))
                        last.then_inc(f_ready, 1)
                    pe.wait_ge(act_ready, ONE + (i + 1) * FB + 2)
                    pe.wait_ge(t2_ready, ONE + i * 2 + 4)
                    for t in range(4):
                        for f in range(FB):
                            last = pe.matmul(ps_y[:, t // 2, (t % 2) * C:(t % 2 + 1) * C], pt[:, f, t * P:(t + 1) * P], w2[:, f, :],
                                             start=(f == 0), stop=(f == FB - 1))
                    last.then_inc(y_ready, 1)
                if has(i, "a"):
                    turn(i, "a", lambda t, k: bin_[:, q, t, k * P:(k + 1) * P], h_normed)
                if has(i, "c"):
                    turn(i, "c", lambda t, k: xcur[:, q, t, k * P:(k + 1) * P], x_normed)
                    pe.wait_ge(turned_copied, ONE + use(i, "c") + 1)
                    pe.wait_ge(lg_ready, ONE + i - 1)
                    for t in range(4):
                        for k in range(2):
                            last = pe.matmul(ps_l[:, t * EXPERTS:(t + 1) * EXPERTS], xt[:, k, t * P:(t + 1) * P], gw[:, k, :],
                                             start=(k == 0), stop=(k == 1))
                    last.then_inc(l_ready, 1)

            pe.wait_ge(w_loaded, ONE + 16 * N_MLP_W)
            run(pe, step)

        @block.scalar
        def _(act):
            def step(i, j, h):
                q = 1 - j

                def biased(f):
                    act.wait_ge(f_ready, ONE + i * FB + f + 1)
                    act.wait_ge(act_ready, ONE + i * FB + f + 1)
                    act.activation(hid[:, f % 2, :], ps_f[:, f % 2, :], ACT.Identity, bias=b1[:, f:f + 1]).then_inc(hid_ready, 1)

                if has(i, "b"):
                    biased(0)
                    biased(1)
                act.wait_ge(var_ready, ONE + i + 2)
                act.activation(std[:, :], mv[:, :, 1], ACT.Sqrt, bias=eps[:, 0:1]).then_inc(std_ready, 1)
                if has(i, "b"):
                    biased(2)
                    biased(3)
                if has(i, "a"):
                    act.wait_ge(turned, ONE + use(i, "a") + 1)
                    for k in range(2):
                        last = act.activation(ht[:, q, k, :], ps_t[:, k, :], ACT.Identity, scale=lng[:, k:k + 1], bias=lnb[:, k:k + 1])
                    last.then_inc(turned_copied, 1)
                    act.wait_ge(turned_copied, ONE + use(i, "a") + 1)
                    act.sem_inc(m_copied, 1)
                if has(i, "c"):
                    act.wait_ge(turned, ONE + use(i, "c") + 1)
                    act.wait_ge(l_ready, ONE + i - 1)
                    act.activation(xt[:, :, :], ps_t[:, :, :], ACT.Copy).then_inc(turned_copied, 1)

            act.wait_ge(consts, ONE + 3)
            act.wait_ge(w_loaded, ONE + 16 * N_MLP_W)
            run(act, step)

        @block.vector
        def _(dve):
            def step(i, j, h):
                q = 1 - j
                if has(i, "a"):
                    dve.wait_ge(m_ready, ONE + i + 2)
                    for t in range(4):
                        last = dve.bn_stats(stats[:, t, :], min_[:, q, t, :])
                if has(i, "c"):
                    dve.wait_ge(t2_ready, ONE + i * 2 + 4)
                    for t in range(4):
                        last = dve.bn_stats(stats[:, 4 + t, :], t2cur[:, q, t, :])
                last.then_inc(bn_step, 1)
                dve.wait_ge(bn_step, ONE + i + 2)
                stand(dve, stood)
                for t in range(8):
                    if has(i, "a") if t < 4 else has(i, "c"):
                        last = dve.bn_aggr(mv[:, t, :], stats[:, t, :])
                last.then_inc(var_ready, 1)
                if has(i, "b"):
                    for f in range(FB):
                        dve.wait_ge(hid_ready, ONE + i * FB + f + 3)
                        if f == 0:
                            dve.wait_ge(y_ready, ONE + i)
                        dve.scalar_tensor_tensor(pt[:, f, :], hid[:, f % 2, :], 0.01, hid[:, f % 2, :], ALU.mult, ALU.max).then_inc(act_ready, 1)
                dve.wait_ge(std_ready, ONE + i + 2)
                dve.reciprocal(rstd[:, :], std[:, :]).then_inc(rstd_ready, 1)
                dve.wait_ge(rstd_ready, ONE + i + 2)
                if has(i, "a"):
                    for t in range(4):
                        last = dve.tensor_scalar(bin_[:, q, t, :], min_[:, q, t, :], mv[:, t, 0:1], rstd[:, t:t + 1], ALU.subtract, ALU.mult)
                    last.then_inc(h_normed, 1)
                if has(i, "c"):
                    dve.wait_ge(xn_stored[q], ONE + (h if h is not None else (i - 1) // 2) * 16)
                    for t in range(4):
                        last = dve.tensor_scalar(xcur[:, q, t, :], t2cur[:, q, t, :], mv[:, 4 + t, 0:1], rstd[:, 4 + t:5 + t], ALU.subtract, ALU.mult)
                    last.then_inc(x_normed, 1)
                if has(i, "b"):
                    dve.wait_ge(y_ready, ONE + i + 1)
                    dve.wait_ge(skip_ready, ONE + i + 1)
                    if has(i, "c"):
                        dve.wait_ge(x_normed, ONE + i - 1)
                        dve.wait_ge(t2_stored[j], ONE + (h + 1 - j if h is not None else i // 2) * 16)
                    for g in range(2):
                        dve.tensor_tensor(t2cur[:, j, 2 * g:2 * g + 2, :].rearrange("p t c -> p (t c)"), ps_y[:, g, :],
                                          tin[:, j, 2 * g:2 * g + 2, :].rearrange("p t c -> p (t c)"), ALU.add).then_inc(t2_ready, 1)
                if has(i, "c"):
                    dve.wait_ge(l_ready, ONE + i)
                    dst = lg[:, ds(i * 4 - 4, 4), :] if h is not None else lg[:, 4 * i - 4:4 * i, :]
                    dve.tensor_tensor(dst, ps_l[:, :].rearrange("p (t e) -> p t e", e=EXPERTS),
                                      gb[:, :].unsqueeze(1).broadcast_to([P, 4, EXPERTS]), ALU.add).then_inc(lg_ready, 1)

            for t, v in ((t2_ready, 4), (hid_ready, 2), (act_ready, 2)):
                dve.sem_inc(t, v)
            dve.wait_ge(consts, ONE + 3)
            dve.wait_ge(w_loaded, ONE + 16 * N_MLP_W)
            run(dve, step)


def routing_phase(nc, ctx, lg, tri, slot, scat, weight):
    def sb(name, shape, dt=F32):
        return ctx.enter_context(nc.sbuf_tensor("rt_" + name, shape, dt))

    sem, start_semaphores = phase_semaphores(nc, ctx, "rt_")

    T, E = B * QT, EXPERTS
    mx, sh, ex, sm = sb("mx", [P, T]), sb("sh", [P, T, E]), sb("ex", [P, T, E]), sb("sm", [P, T])
    num, ones = sb("num", [P, E]), sb("ones", [P, P])
    cand, idx = sb("cand", [P, T, E]), sb("idx", [P, T])
    hot, tot, inc = sb("hot", [P, T, E]), sb("tot", [P, T, E]), sb("inc", [P, T, E])
    pos, kept, fslot, fscat = sb("pos", [P, T]), sb("kept", [P, T]), sb("fslot", [P, T]), sb("fscat", [P, T])
    ps_c = ctx.enter_context(nc.psum_tensor("rt_ps_c", [P, T * E], F32))
    ps_n = ctx.enter_context(nc.psum_tensor("rt_ps_n", [P, T * E], F32))
    consts, dve_step, sh_ready, ex_ready, hot_ready, counted, done = (
        sem(n) for n in ("consts", "dve_step", "sh_ready", "ex_ready", "hot_ready", "counted", "done"))
    wide = lambda t: t[:, :].unsqueeze(2).broadcast_to([P, T, E])
    flat = lambda t: t[:, :, :].rearrange("p t e -> p (t e)")

    start_semaphores()
    with nc.Block() as block:
        @block.gpsimd
        def _(pool):
            pool.memset(tri[:, :], 1.0).then_inc(consts, 1)
            pool.memset(ones[:, :], 1.0).then_inc(consts, 1)
            pool.iota(num[:, :], pattern=[[1, E]], base=0, channel_multiplier=0,
                      allow_small_or_imprecise_dtypes=True).then_inc(consts, 1)
            pool.wait_ge(consts, ONE + 3)
            pool.affine_select(out=tri[:, :], in_=tri[:, :], compare_op=ALU.is_ge, fill=0.0, base=0,
                               pattern=[[1, P]], channel_multiplier=-1).then_inc(consts, 1)

        @block.scalar
        def _(act):
            act.wait_ge(sh_ready, ONE + 1)
            act.activation(ex[:, :, :], sh[:, :, :], ACT.Exp).then_inc(ex_ready, 1)

        @block.tensor
        def _(pe):
            pe.wait_ge(consts, ONE + 4)
            pe.wait_ge(hot_ready, ONE + 1)
            pe.matmul(ps_c[:, :], tri[:, :], flat(hot), start=True, stop=True)
            pe.matmul(ps_n[:, :], ones[:, :], flat(hot), start=True, stop=True).then_inc(counted, 1)

        @block.vector
        def _(dve):
            n = [0]

            def link(ins):
                n[0] += 1
                ins.then_inc(dve_step, 1)
                dve.wait_ge(dve_step, ONE + n[0])

            dve.wait_ge(consts, ONE + 4)
            link(dve.tensor_reduce(mx[:, :], lg[:, :, :], AX.X, ALU.max))
            dve.tensor_tensor(sh[:, :, :], lg[:, :, :], wide(mx), ALU.subtract).then_inc(sh_ready, 1)
            dve.wait_ge(sh_ready, ONE + 1)
            link(dve.tensor_scalar(cand[:, :, :], sh[:, :, :], 0.0, -float(E), ALU.is_equal, ALU.mult))
            link(dve.scalar_tensor_tensor(cand[:, :, :], cand[:, :, :], float(E), num[:, :].unsqueeze(1).broadcast_to([P, T, E]), ALU.add, ALU.add))
            link(dve.tensor_reduce(idx[:, :], cand[:, :, :], AX.X, ALU.min))
            dve.tensor_tensor(hot[:, :, :], num[:, :].unsqueeze(1).broadcast_to([P, T, E]), wide(idx), ALU.is_equal).then_inc(hot_ready, 1)
            dve.wait_ge(ex_ready, ONE + 1)
            link(dve.tensor_reduce(sm[:, :], ex[:, :, :], AX.X, ALU.add))
            link(dve.reciprocal(weight[:, :], sm[:, :]))
            dve.wait_ge(counted, ONE + 1)
            link(dve.tensor_copy(flat(tot), ps_n[:, :]))
            for e in range(E):
                last = dve.tensor_tensor_scan(inc[:, :, e], ones[:, 0:T], tot[:, :, e], 0.0, ALU.mult, ALU.add)
            link(last)
            link(dve.tensor_tensor(flat(inc), flat(inc), flat(tot), ALU.subtract))
            link(dve.tensor_tensor(flat(inc), ps_c[:, :], flat(inc), ALU.add))
            link(dve.tensor_tensor(inc[:, :, :], inc[:, :, :], hot[:, :, :], ALU.mult))
            link(dve.tensor_reduce(pos[:, :], inc[:, :, :], AX.X, ALU.add))
            link(dve.tensor_scalar(kept[:, :], pos[:, :], float(CAP), None, ALU.is_le))
            link(dve.tensor_scalar(fslot[:, :], pos[:, :], float(CAP), -1.0, ALU.min, ALU.add))
            link(dve.scalar_tensor_tensor(fslot[:, :], idx[:, :], float(CAP), fslot[:, :], ALU.mult, ALU.add))
            link(dve.tensor_tensor(weight[:, :], weight[:, :], kept[:, :], ALU.mult))
            link(dve.tensor_scalar(fscat[:, :], kept[:, :], -float(E * CAP), float(E * CAP), ALU.mult, ALU.add))
            link(dve.tensor_tensor(fscat[:, :], fscat[:, :], fslot[:, :], ALU.add))
            link(dve.tensor_copy(slot[:, :], fslot[:, :]))
            link(dve.tensor_copy(scat[:, :], fscat[:, :]))


def scatter_phase(nc, ctx, xn, scat, xbuf):
    rows = ctx.enter_context(nc.sbuf_tensor("sc_rows", [P, 4, 4, C], F32))
    sem, _ = phase_semaphores(nc, ctx, "sc_")
    loaded = [sem(f"loaded{j}") for j in range(4)]
    scattered = [sem(f"scattered{j}") for j in range(4)]
    N = B * NCH

    with nc.Block() as block:
        @block.sync
        def _(sp):
            for n in range(N):
                j = n % 4
                if n >= 4:
                    sp.wait_ge(scattered[j], 64 * (n // 4))
                sp.dma_start(rows[:, j].rearrange("p t c -> p (t c)"), xn[n]).then_inc(loaded[j], 16)
            for j in range(4):
                sp.wait_ge(scattered[j], 64 * (N // 4))

        @block.gpsimd
        def _(pool):
            for n in range(N):
                j = n % 4
                pool.wait_ge(loaded[j], 16 * (n // 4 + 1))
                for t in range(4):
                    pool.indirect_dma_start(
                        out=xbuf, out_offset=bass.IndirectOffsetOnAxis(ap=scat[:, 4 * n + t:4 * n + t + 1], axis=0),
                        in_=rows[:, j, t, :], in_offset=None, bounds_check=EXPERTS * CAP - 1,
                        oob_is_err=False).then_inc(scattered[j], 16)


def experts_phase(nc, ctx, ident, w, xbuf, ybuf):
    def sb(name, shape, dt=F32):
        return ctx.enter_context(nc.sbuf_tensor("ex_" + name, shape, dt))

    sem, start_semaphores = phase_semaphores(nc, ctx, "ex_")

    E, F = EXPERTS, 1024
    FB, RC = F // P, 256
    M = CAP // RC
    w1, w2 = sb("w1", [P, 2, 2, F]), sb("w2", [P, 2, FB, C])
    b1, b2 = sb("b1", [P, E, FB]), sb("b2", [P, E, C])
    xr, xt = sb("xr", [P, 2, 2, C]), sb("xt", [P, 2, 2, RC])
    hid = sb("hid", [P, 2, FB, RC])
    yr = sb("yr", [P, 2, 2, C])
    ps_x = ctx.enter_context(nc.psum_tensor("ex_ps_x", [P, 2, CH], F32))
    ps_h = ctx.enter_context(nc.psum_tensor("ex_ps_h", [P, 4, CH], F32))
    ps_y = ctx.enter_context(nc.psum_tensor("ex_ps_y", [P, 2, CH], F32))
    b1c, b2c = sb("b1c", [P, 2, FB]), sb("b2c", [P, 2, C])
    b_loaded, bias_ready = sem("b_loaded"), sem("bias_ready")
    w_loaded = [sem(f"w_loaded{j}") for j in range(2)]
    x_loaded = [sem(f"x_loaded{j}") for j in range(2)]
    turned, x_copied, h_ready, relued, y_ready, y_added, stood = (
        sem(n) for n in ("turned", "x_copied", "h_ready", "relued", "y_ready", "y_added", "stood"))
    y_stored = [sem(f"y_stored{j}") for j in range(2)]
    TURN = 2 * M

    def loop(eng, chunk):
        with eng.Fori(0, E // 2) as r:
            for m in range(TURN):
                chunk(r * TURN + m, m, r)

    start_semaphores()
    with nc.Block() as block:
        @block.sync
        def _(sp):
            sp.dma_start(b1[:, :, :], w["b1"]).then_inc(b_loaded, 16)
            sp.dma_start(b2[:, :, :].rearrange("p e c -> p (e c)"), w["b2"].rearrange("e c -> (e c)").partition_broadcast(P)).then_inc(b_loaded, 16)

            def load_w(e, j):
                sp.dma_start(w1[:, j], w["w1"][e].rearrange("(k p) f -> p k f", p=P)).then_inc(w_loaded[j], 16)
                sp.dma_start(w2[:, j], w["w2"][e].rearrange("(f p) c -> p f c", p=P)).then_inc(w_loaded[j], 16)

            def load_x(n, j):
                sp.dma_start(xr[:, j], xbuf[ds(n * RC, RC), :].rearrange("(t p) c -> p t c", p=P)).then_inc(x_loaded[j], 16)

            load_w(0, 0)
            load_w(1, 1)
            load_x(0, 0)
            load_x(1, 1)

            def chunk(n, m, r, last=False):
                if not (last and m >= TURN - 2):
                    sp.wait_ge(turned, ONE + n + 1)
                    stand(sp, stood)
                    load_x(n + 2, m % 2)
                if not last and m in (M, TURN - 1):
                    j = 0 if m == M else 1
                    sp.wait_ge(y_ready, ONE + (n if m == M else n + 1))
                    stand(sp, stood)
                    load_w(r * 2 + 2 + j, j)
                sp.wait_ge(y_added, ONE + (n + 1) * 2)
                stand(sp, stood)
                sp.dma_start(ybuf[ds(n * RC, RC), :].rearrange("(t p) c -> p t c", p=P), yr[:, m % 2]).then_inc(y_stored[m % 2], 16)

            with sp.Fori(0, E // 2 - 1) as r:
                for m in range(TURN):
                    chunk(r * TURN + m, m, r)
            for m in range(TURN):
                chunk((E // 2 - 1) * TURN + m, m, None, last=True)
            for j in range(2):
                sp.wait_ge(y_stored[j], ONE + 16 * E * M // 2)

        @block.tensor
        def _(pe):
            def turn(n, q, loads):
                pe.wait_ge(x_loaded[q], ONE + loads)
                pe.wait_ge(x_copied, ONE + n)
                for t in range(2):
                    for k in range(2):
                        last = pe.transpose(ps_x[:, q, k * RC + t * P:k * RC + (t + 1) * P], xr[:, q, t, k * P:(k + 1) * P], ident[:, :])
                last.then_inc(turned, 1)

            def chunk(n, m, r, last=False):
                j, q = m // M, m % 2
                if m % M == 0:
                    pe.wait_ge(w_loaded[j], ONE + (r + 1) * 32)
                pe.wait_ge(x_copied, ONE + n + 2)
                for f in range(FB):
                    pe.wait_ge(relued, ONE + n * FB + f + 1)
                    for k in range(2):
                        ins = pe.matmul(ps_h[:, f % 4, 0:RC], w1[:, j, k, f * P:(f + 1) * P], xt[:, q, k, :], start=(k == 0), stop=(k == 1))
                    ins.then_inc(h_ready, 1)
                if not (last and m == TURN - 1):
                    turn(n + 1, 1 - q, (r * (TURN // 2) + (m + 1) // 2 + 1) * 16)
                pe.wait_ge(relued, ONE + (n + 1) * FB + 4)
                pe.wait_ge(y_added, ONE + n * 2)
                for t in range(2):
                    for f in range(FB):
                        ins = pe.matmul(ps_y[:, t, 0:C], hid[:, q, f, t * P:(t + 1) * P], w2[:, j, f, :], start=(f == 0), stop=(f == FB - 1))
                ins.then_inc(y_ready, 1)

            turn(0, 0, 16)
            with pe.Fori(0, E // 2 - 1) as r:
                for m in range(TURN):
                    chunk(r * TURN + m, m, r)
            for m in range(TURN):
                chunk((E // 2 - 1) * TURN + m, m, E // 2 - 1, last=True)

        @block.scalar
        def _(act):
            def chunk(n, m, r):
                q = m % 2
                if m % M == 0:
                    act.wait_ge(bias_ready, ONE + r * 2 + m // M + 1)
                for f in range(FB):
                    act.wait_ge(h_ready, ONE + n * FB + f + 1)
                    act.activation(hid[:, q, f, :], ps_h[:, f % 4, 0:RC], ACT.Relu, bias=b1c[:, m // M, f:f + 1]).then_inc(relued, 1)
            loop(act, chunk)

        @block.vector
        def _(dve):
            def copy(n, q):
                dve.wait_ge(turned, ONE + n + 1)
                dve.tensor_copy(xt[:, q], ps_x[:, q, :].rearrange("p (k r) -> p k r", k=2)).then_inc(x_copied, 1)

            def chunk(n, m, r, last=False):
                q = m % 2
                if m % M == 0:
                    dve.wait_ge(y_ready, ONE + n)
                    dve.tensor_copy(b2c[:, m // M, :], b2[:, ds(r * 2 + m // M, 1), :].rearrange("p a c -> p (a c)"))
                    dve.tensor_copy(b1c[:, m // M, :], b1[:, ds(r * 2 + m // M, 1), :].rearrange("p a f -> p (a f)")).then_inc(bias_ready, 1)
                    dve.wait_ge(bias_ready, ONE + r * 2 + m // M + 1)
                if not (last and m == TURN - 1):
                    copy(n + 1, 1 - q)
                dve.wait_ge(y_ready, ONE + n + 1)
                dve.wait_ge(y_stored[q], ONE + r * (TURN // 2) * 16 + m // 2 * 16)
                for t in range(2):
                    dve.tensor_tensor(yr[:, q, t, :], ps_y[:, t, 0:C], b2c[:, m // M, :], ALU.add).then_inc(y_added, 1)

            dve.wait_ge(b_loaded, ONE + 32)
            dve.sem_inc(x_copied, 1)
            dve.sem_inc(relued, 4)
            copy(0, 0)
            with dve.Fori(0, E // 2 - 1) as r:
                for m in range(TURN):
                    chunk(r * TURN + m, m, r)
            for m in range(TURN):
                chunk((E // 2 - 1) * TURN + m, m, E // 2 - 1, last=True)


def gather_phase(nc, ctx, ident, ybuf, slot, weight, t2, out):
    def sb(name, shape, dt=F32):
        return ctx.enter_context(nc.sbuf_tensor("ga_" + name, shape, dt))

    sem, _ = phase_semaphores(nc, ctx, "ga_")

    N = B * NCH
    D = 4
    yg, tin = sb("yg", [P, D, 4, C]), sb("t2", [P, D, 4, C])
    safe, fin, same = sb("safe", [P, 2, 4, C]), sb("fin", [P, 2, 4 * C], I32), sb("same", [P, 2, 4 * C], I32)
    bounded, fin_ready = sem("bounded"), sem("fin_ready")
    bound = sb("bound", [P, 2, 4, C])
    lim = sb("lim", [P, 2, 4, C])
    ot = sb("ot", [P, 2, 2, CH])
    ps_o = ctx.enter_context(nc.psum_tensor("ga_ps_o", [P, 2, 2, CH], F32))
    t_loaded = [sem(f"t_loaded{j}") for j in range(D)]
    y_loaded = [sem(f"y_loaded{j}") for j in range(D)]
    zeroed, weighed, masked, chosen, kept_step, added, turned, copied = (
        sem(n) for n in ("zeroed", "weighed", "masked", "chosen", "kept_step", "added", "turned", "copied"))
    stored = [sem(f"stored{j}") for j in range(2)]
    flat = lambda t: t.rearrange("p t c -> p (t c)")

    with nc.Block() as block:
        @block.gpsimd
        def _(pool):
            for n in range(N):
                j = n % D
                if n >= D:
                    pool.wait_ge(added, n - D + 1)
                for t in range(4):
                    pool.indirect_dma_start(
                        out=yg[:, j, t, :], out_offset=None, in_=ybuf,
                        in_offset=bass.IndirectOffsetOnAxis(ap=slot[:, 4 * n + t:4 * n + t + 1], axis=0),
                        bounds_check=EXPERTS * CAP - 1, oob_is_err=False).then_inc(y_loaded[j], 16)

        @block.sync
        def _(sp):
            for n in range(N):
                j = n % D
                if n >= D:
                    sp.wait_ge(turned, n - D + 1)
                sp.dma_start(flat(tin[:, j]), t2[n]).then_inc(t_loaded[j], 16)

        @block.vector
        def _(dve):
            dve.memset(safe[:, :, :, :], 0.0).then_inc(zeroed, 1)
            dve.wait_ge(zeroed, 1)
            for n in range(N):
                j, q = n % D, n % 2
                y = yg[:, j]
                dve.wait_ge(y_loaded[j], 64 * (n // D + 1))
                if n >= 2:
                    dve.wait_ge(added, n - 1)
                for t in range(4):
                    last = dve.tensor_scalar(yg[:, j, t, :], yg[:, j, t, :], weight[:, 4 * n + t:4 * n + t + 1], None, ALU.mult)
                last.then_inc(weighed, 1)
                dve.wait_ge(weighed, n + 1)
                dve.tensor_tensor(same[:, q, :], flat(y), flat(y), ALU.is_equal)
                dve.tensor_scalar(flat(bound[:, q]), flat(y), FLT_MAX, -FLT_MAX, ALU.min, ALU.max).then_inc(bounded, 1)
                dve.tensor_scalar(flat(lim[:, q]), flat(y), 1e4, -1e4, ALU.min, ALU.max).then_inc(masked, 1)
                dve.wait_ge(bounded, n + 1)
                dve.tensor_tensor(fin[:, q, :], flat(bound[:, q]), flat(y), ALU.is_equal).then_inc(fin_ready, 1)
                dve.wait_ge(masked, n + 1)
                dve.copy_predicated(flat(safe[:, q]), same[:, q, :], flat(lim[:, q])).then_inc(chosen, 1)
                dve.wait_ge(chosen, n + 1)
                dve.wait_ge(fin_ready, n + 1)
                dve.copy_predicated(flat(safe[:, q]), fin[:, q, :], flat(y)).then_inc(kept_step, 1)
                dve.wait_ge(kept_step, n + 1)
                dve.wait_ge(t_loaded[j], 16 * (n // D + 1))
                dve.tensor_tensor(tin[:, j], tin[:, j], safe[:, q], ALU.add).then_inc(added, 1)

        @block.tensor
        def _(pe):
            for n in range(N):
                j, q = n % D, n % 2
                pe.wait_ge(added, n + 1)
                if n >= 2:
                    pe.wait_ge(copied, n - 1)
                for t in range(4):
                    for k in range(2):
                        last = pe.transpose(ps_o[:, q, k, t * P:(t + 1) * P], tin[:, j, t, k * P:(k + 1) * P], ident[:, :])
                last.then_inc(turned, 1)

        @block.scalar
        def _(act):
            for n in range(N):
                q = n % 2
                act.wait_ge(turned, n + 1)
                if n >= 2:
                    act.wait_ge(stored[q], 16 * (n // 2))
                act.activation(ot[:, q], ps_o[:, q], ACT.Copy).then_inc(copied, 1)
                act.wait_ge(copied, n + 1)
                b, c = divmod(n, NCH)
                act.dma_start(out[b * C:(b + 1) * C, c * CH:(c + 1) * CH].rearrange("(k p) l -> p k l", p=P), ot[:, q]).then_inc(stored[q], 16)
            for j in range(2):
                act.wait_ge(stored[j], 8 * N)


N_CONV_W = 3 * 8 + 2 * 4
N_MAMBA_W = 9 * 2 + 3 * 2 * 4
N_MLP_W = 5 + 8


def hybrid_kernel(nc, a, out):
    x = a["x"].rearrange("b c h w -> (b c) (h w)")
    q_split = scratch(nc, "q_split", (3, C * B, L), BF16)
    k_split = scratch(nc, "k_split", (3, C * B, L), BF16)
    v_split = scratch(nc, "v_split", (HEADS, P, QT * P), BF16)
    attn_out = scratch(nc, "attn_out", (HEADS, P, QT * DH))
    with ExitStack() as whole:
        ident = whole.enter_context(nc.sbuf_tensor("ident", [P, P], F32))
        ident_ready = whole.enter_context(nc.semaphore("ident_ready"))
        with nc.Block() as block:
            @block.gpsimd
            def _(pool):
                pool.memset(ident[:, :], 0.0).then_inc(ident_ready, 1)
                pool.wait_ge(ident_ready, 1)
                pool.affine_select(out=ident[:, :], in_=ident[:, :], compare_op=ALU.not_equal, fill=1.0, base=0,
                                   pattern=[[-1, P]], channel_multiplier=1).then_inc(ident_ready, 1)
                pool.wait_ge(ident_ready, 2)
        with ExitStack() as ctx:
            conv_phase(nc, ctx, ident, x, a["L0_conv_qw"], a["L0_conv_kw"], a["L0_conv_vw"], a["L0_conv_c1w"],
                       a["L0_conv_c1b"], a["L0_conv_gnw"], a["L0_conv_gnb"], q_split, k_split, v_split)
        with ExitStack() as ctx:
            attention_phase(nc, ctx, ident, q_split, k_split, v_split, attn_out)
        t1 = scratch(nc, "t1", (B * NCH, P, 4 * C))
        u1 = scratch(nc, "u1", (B * NCH, P, 2 * CH))
        m_dirs = scratch(nc, "m_dirs", (2, B * NCH, P, 4 * C))
        with ExitStack() as ctx:
            tokens_phase(nc, ctx, ident, x, attn_out, t1, u1)
        with ExitStack() as ctx:
            mamba_phase(nc, ctx, ident, {k[8:]: v for k, v in a.items() if k.startswith("L1_attn_")}, u1, m_dirs)
        t2 = scratch(nc, "t2", (B * NCH, P, 4 * C))
        xn = scratch(nc, "xn", (B * NCH, P, 4 * C))
        xbuf = scratch(nc, "xbuf", (EXPERTS * CAP, C))
        ybuf = scratch(nc, "ybuf", (EXPERTS * CAP, C))
        lg, weight = (whole.enter_context(nc.sbuf_tensor(*v, F32)) for v in (("lg", [P, B * QT, EXPERTS]), ("weight", [P, B * QT])))
        slot, scat = (whole.enter_context(nc.sbuf_tensor(n, [P, B * QT], U32)) for n in ("slot", "scat"))
        tri = whole.enter_context(nc.sbuf_tensor("tri", [P, P], F32))
        w = {k[3:]: v for k, v in a.items() if k.startswith("L1_")}
        with ExitStack() as ctx:
            mlp_phase(nc, ctx, ident, w, t1, m_dirs, t2, xn, lg, xbuf)
        with ExitStack() as ctx:
            routing_phase(nc, ctx, lg, tri, slot, scat, weight)
        with ExitStack() as ctx:
            scatter_phase(nc, ctx, xn, scat, xbuf)
        with ExitStack() as ctx:
            experts_phase(nc, ctx, ident, {k[4:]: v for k, v in w.items() if k.startswith("ffn_")}, xbuf, ybuf)
        with ExitStack() as ctx:
            gather_phase(nc, ctx, ident, ybuf, slot, weight, t2, out.rearrange("b c h w -> (b c) (h w)"))

def _layout(inputs, np):
    w = {k: np.ascontiguousarray(v) for k, v in inputs.items()}
    for n in ("qw", "kw", "vw"):
        t = w[f"L0_conv_{n}"].reshape(4, 16, 16, 9)
        w[f"L0_conv_{n}"] = t.transpose(0, 2, 3, 1)
    for n, cut in (("in_proj_w", 2), ("x_proj_w", 4), ("out_proj_w", 4)):
        t = w[f"L1_attn_{n}"].transpose(0, 2, 1)
        w[f"L1_attn_{n}"] = t.reshape(2, cut, P, t.shape[2])
    for n, cut in (("w1", 2), ("w2", 4)):
        t = w[f"L1_attn_{n}"].T
        w[f"L1_attn_{n}"] = t.reshape(cut, P, t.shape[1])
    w["L1_ffn_b1"] = w["L1_ffn_b1"].reshape(EXPERTS, -1, P).transpose(2, 0, 1)
    w["L1_attn_dt_proj_w"] = w["L1_attn_dt_proj_w"].transpose(0, 2, 1)
    w["L0_conv_c1w"] = w["L0_conv_c1w"][:, :, 0, 0].T
    return {k: np.ascontiguousarray(v) for k, v in w.items()}


def kernel(**inputs):
    import numpy as _np
    import concourse.bacc as _bacc
    from concourse.bass_utils import run_bass_kernel_spmd as _run

    nc = _bacc.Bacc("TRN2", target_bir_lowering=False, num_devices=1)
    arrays, args = {}, {}
    for name, a in _layout(inputs, _np).items():
        arrays[f"in_{name}"] = a
        args[name] = nc.dram_tensor(f"in_{name}", a.shape, mybir.dt.from_np(a.dtype), kind="ExternalInput").ap()
    out = nc.dram_tensor("out_x", (B, C, IMG, IMG), F32, kind="ExternalOutput").ap()
    hybrid_kernel(nc, args, out)
    r = _run(nc, [arrays], core_ids=[0])
    return r.results[0]["out_x"]
```

```python
import concourse.bass as bass
from concourse import mybir
from contextlib import ExitStack

F32 = mybir.dt.float32
BF16 = mybir.dt.bfloat16
U32 = mybir.dt.uint32
I32 = mybir.dt.int32
ALU = mybir.AluOpType
ACT = mybir.ActivationFunctionType
AX = mybir.AxisListType
ds = bass.ds

P = 128
B, C, IMG = 2, 256, 64
L = IMG * IMG
HEADS = 8
DH = 64
PAIRS = HEADS // 2
PAD = IMG + 2
CH = 512
NCH = L // CH
QT = L // P
EXPERTS = 8
CAP = 1280
GN_EPS = 1e-5
FLT_MAX = 3.4028234663852886e38
ONE = 1


def scratch(nc, name, shape, dt=F32):
    return nc.dram_tensor(name, shape, dt, kind="Internal").ap()


def stand(eng, sem):
    eng.sem_inc(sem, 1)


def phase_semaphores(nc, ctx, prefix):
    taken, counted_from_one = [], []

    def sem(name, first=ONE):
        taken.append(nc.alloc_semaphore(prefix + name))
        if first:
            counted_from_one.append(taken[-1])
        return taken[-1]

    def start():
        with nc.Block() as block:
            @block.gpsimd
            def _(pool):
                for s in counted_from_one:
                    pool.sem_inc(s, ONE)

    def put_back():
        with nc.Block() as block:
            @block.gpsimd
            def _(pool):
                for s in taken:
                    pool.sem_clear(s)
        for s in taken:
            nc.release_semaphore(s)

    ctx.callback(put_back)
    return sem, start


def conv_phase(nc, ctx, ident, x, qw, kw, vw, c1w, c1b, gnw, gnb, q_split, k_split, v_split):
    def sb(name, shape, dt=F32):
        return ctx.enter_context(nc.sbuf_tensor(name, shape, dt))

    sem, start_semaphores = phase_semaphores(nc, ctx, "")

    wq, wk, wv = sb("wq", [P, 9, P]), sb("wk", [P, 9, P]), sb("wv", [P, 9, P])
    wc1 = sb("wc1", [P, P])
    vecs = sb("conv_vecs", [P, 3])
    group8 = sb("group8", [P, P])
    eps = sb("conv_eps", [P, 1])
    ximg = sb("ximg", [P, L])
    xpads = [sb(f"xpad{j}", [P, PAD, PAD]) for j in range(2)]
    gated = sb("gated", [P, L])
    resid = sb("resid", [P, L])
    qp = [sb(f"q_part{n}", [P, L], BF16) for n in range(3)]
    kp = [sb(f"k_part{n}", [P, L], BF16) for n in range(3)]
    vparts = sb("v_parts", [P, 2, QT, 2 * DH], BF16)
    vc = sb("v_chunk", [P, 2, CH])
    kres = sb("k_resid", [P, 2, CH])
    stats = sb("conv_stats", [P, NCH, 6])
    mv = sb("conv_mv", [P, 2])
    chan = sb("chan", [P, 2])
    grp = sb("grp", [P, 2])
    col = sb("conv_cols", [P, 8])
    colsum = sb("colsum", [P, 3, PAD])
    rowsum = sb("rowsum", [P, 3, PAD])
    cat = sb("cat", [P, 2 * IMG])
    gates = sb("gates", [P, 2 * IMG])
    ps_g = ctx.enter_context(nc.psum_tensor("ps_g", [P, 2], F32))
    ps_k = ctx.enter_context(nc.psum_tensor("ps_k", [P, 2, CH], F32))
    ps_q = ctx.enter_context(nc.psum_tensor("ps_q", [P, 2 * IMG], F32))
    ps_c = ctx.enter_context(nc.psum_tensor("ps_c", [P, 2 * IMG], F32))
    ps_v = ctx.enter_context(nc.psum_tensor("ps_v", [P, 2, CH], F32))

    w_ready = sem("conv_w_ready")
    zeroed = sem("conv_zeroed")
    stood = sem("conv_stood")
    x_loaded = sem("x_loaded")
    k_stored, v_stored, q_stored = sem("k_stored"), sem("v_stored"), sem("q_stored")
    dve_step = sem("conv_dve_step")
    chan_ready, grp_summed, var_ready, std_ready = (sem(n) for n in ("chan_ready", "grp_summed", "var_ready", "std_ready"))
    affine_ready, xn_ready, sums_ready, q_summed = (sem(n) for n in ("affine_ready", "xn_ready", "sums_ready", "q_summed"))
    cat_ready, c1_done, gates_ready = sem("cat_ready"), sem("c1_done"), sem("gates_ready")
    var2_ready, std2_ready, qaff_ready = sem("var2_ready"), sem("std2_ready"), sem("qaff_ready")
    vc_ready, v_turned = sem("vc_ready"), sem("v_turned")
    k_summed, k1_ready, kres_ready, k2_ready, k3_ready = (sem(n) for n in ("k_summed", "k1_ready", "kres_ready", "k2_ready", "k3_ready"))
    v_summed, v1_ready, v2_ready = sem("v_summed"), sem("v1_ready"), sem("v2_ready")
    q_ready, q1_ready, qres_ready, q2_ready, q3_ready = (sem(n) for n in ("q_ready", "q1_ready", "qres_ready", "q2_ready", "q3_ready"))

    inner = [t[:, 1:IMG + 1, 1:IMG + 1] for t in xpads]
    image = lambda t: t[:, :].rearrange("p (h w) -> p h w", w=IMG)
    TILE_GROUPS = QT // 4
    ZEROED = 12

    def pairs(eng, step):
        with eng.Fori(0, PAIRS // 2 - 1) as h:
            for b in range(2):
                step(h * 2 + b, b, False)
        step(PAIRS - 2, 0, False)
        step(PAIRS - 1, 1, True)

    start_semaphores()
    with nc.Block() as block:
        @block.gpsimd
        def _(pool):
            for t in (wq[:, :, :], wk[:, :, :], wv[:, :, :], wc1[:, :], xpads[0][:, :, :], xpads[1][:, :, :], colsum[:, :, :], rowsum[:, :, :]):
                pool.memset(t, 0.0).then_inc(zeroed, 1)
            pool.memset(eps[:, :], GN_EPS).then_inc(zeroed, 1)
            pool.memset(group8[:, :], 0.125).then_inc(zeroed, 1)
            pool.wait_ge(zeroed, ONE + ZEROED - 2)
            blocks = group8[:, :].rearrange("p (a b) -> p a b", b=8)
            pool.affine_select(out=blocks, in_=blocks, compare_op=ALU.is_ge, fill=0.0, base=0,
                               pattern=[[-8, 16], [0, 8]], channel_multiplier=1).then_inc(zeroed, 1)
            pool.wait_ge(zeroed, ONE + ZEROED - 1)
            pool.affine_select(out=blocks, in_=blocks, compare_op=ALU.is_ge, fill=0.0, base=7,
                               pattern=[[8, 16], [0, 8]], channel_multiplier=-1).then_inc(zeroed, 1)

            def step(i, b, last_pair):
                if not last_pair:
                    pool.wait_ge(qres_ready, ONE + i + 1)
                    pool.wait_ge(q_stored, ONE + i * 48)
                    pool.tensor_copy(qp[1][:, :], resid[:, :]).then_inc(q2_ready, 1)
                    pool.wait_ge(q2_ready, ONE + i + 1)
                    pool.tensor_tensor(qp[2][:, :], resid[:, :], qp[1][:, :], ALU.subtract).then_inc(q3_ready, 1)
            pairs(pool, step)

        @block.sync
        def _(sp):
            def load(i):
                sp.dma_start(ximg[:, :], x[ds(i * P, P), :]).then_inc(x_loaded, 16)

            load(0)
            sp.wait_ge(zeroed, ONE + ZEROED - 2)
            n = 0
            for dst, src in ((wk, kw), (wv, vw), (wq, qw)):
                for j in range(8):
                    sp.dma_start(dst[16 * j:16 * j + 16, :, 16 * j:16 * j + 16], src[j % 4]).then_inc(w_ready, 16)
                    n += 1
            for h in range(2):
                rows = slice(DH * h, DH * h + DH)
                sp.dma_start(wc1[rows, rows], c1w).then_inc(w_ready, 16)
                for j, v in enumerate((c1b, gnw, gnb)):
                    sp.dma_start(vecs[rows, j:j + 1], v.unsqueeze(1)).then_inc(w_ready, 16)
                n += 4
            assert n == N_CONV_W

            def step(i, b, last):
                if not last:
                    sp.wait_ge(xn_ready, ONE + i + 1)
                    stand(sp, stood)
                    load(i + 1)
                sp.wait_ge(k3_ready, ONE + (i + 1) * NCH)
                sp.wait_ge(k2_ready, ONE + (i + 1) * NCH)
                stand(sp, stood)
                for n in range(3):
                    sp.dma_start(k_split[n, ds(i * P, P), :], kp[n][:, :]).then_inc(k_stored, 16)
                sp.wait_ge(v2_ready, ONE + (i + 1) * TILE_GROUPS + 2)
                stand(sp, stood)
                sp.dma_start(v_split[ds(i * 2, 2)].rearrange("h p n -> p h n"),
                             vparts[:, :, :, :].rearrange("p h t c -> p h (t c)")).then_inc(v_stored, 16)
                sp.wait_ge(q3_ready, ONE + i + 1)
                stand(sp, stood)
                for n in range(3):
                    sp.dma_start(q_split[n, ds(i * P, P), :], qp[n][:, :]).then_inc(q_stored, 16)

            pairs(sp, step)
            sp.wait_ge(k_stored, ONE + 48 * PAIRS)
            sp.wait_ge(v_stored, ONE + 16 * PAIRS)
            sp.wait_ge(q_stored, ONE + 48 * PAIRS)

        @block.tensor
        def _(pe):
            pe.wait_ge(zeroed, ONE + ZEROED)
            def group_means(i):
                pe.wait_ge(chan_ready, ONE + i + 1)
                pe.matmul(ps_g[:, :], group8[:, :], chan[:, :], start=True, stop=True).then_inc(grp_summed, 1)

            def step(i, b, last_pair):
                xpad = xpads[b]
                pe.wait_ge(xn_ready, ONE + i + 1)
                for c in range(NCH):
                    if c < 2:
                        pe.wait_ge(vc_ready, ONE + i * NCH)
                    else:
                        pe.wait_ge(kres_ready, ONE + i * NCH + c - 1)
                    for t in range(9):
                        dy, dx = divmod(t, 3)
                        last = pe.matmul(ps_k[:, c % 2, :], wk[:, t, :],
                                         xpad[:, 8 * c + dy:8 * c + dy + 8, dx:dx + IMG],
                                         start=(t == 0), stop=(t == 8))
                    last.then_inc(k_summed, 1)
                pe.wait_ge(sums_ready, ONE + 2 * (i + 1))
                for t in range(9):
                    dy, dx = divmod(t, 3)
                    pe.matmul(ps_q[:, 0:IMG], wq[:, t, :], colsum[:, dy, dx:dx + IMG], start=(t == 0), stop=(t == 8))
                for t in range(9):
                    dy, dx = divmod(t, 3)
                    last = pe.matmul(ps_q[:, IMG:2 * IMG], wq[:, t, :], rowsum[:, dx, dy:dy + IMG],
                                     start=(t == 0), stop=(t == 8))
                last.then_inc(q_summed, 1)
                for c in range(NCH + 1):
                    if c == 1 and not last_pair:
                        group_means(i + 1)
                    if c == 2:
                        pe.wait_ge(cat_ready, ONE + i + 1)
                        pe.matmul(ps_c[:, :], wc1[:, :], cat[:, :], start=True, stop=True).then_inc(c1_done, 1)
                    if c < NCH:
                        if c < 2:
                            pe.wait_ge(kres_ready, ONE + i * NCH + NCH - 1 + c)
                        else:
                            pe.wait_ge(vc_ready, ONE + i * NCH + c - 1)
                        for t in range(9):
                            dy, dx = divmod(t, 3)
                            last = pe.matmul(ps_k[:, c % 2, :], wv[:, t, :],
                                             xpad[:, 8 * c + dy:8 * c + dy + 8, dx:dx + IMG],
                                             start=(t == 0), stop=(t == 8))
                        last.then_inc(v_summed, 1)
                    if c:
                        pe.wait_ge(vc_ready, ONE + i * NCH + c)
                        pe.wait_ge(v2_ready, ONE + i * NCH + c)
                        for k in range(4):
                            last = pe.transpose(ps_v[:, (c - 1) % 2, k * P:(k + 1) * P],
                                                vc[:, (c - 1) % 2, k * P:(k + 1) * P], ident[:, :])
                        last.then_inc(v_turned, 1)

            group_means(0)
            pe.wait_ge(w_ready, ONE + 16 * N_CONV_W)
            pairs(pe, step)

        @block.scalar
        def _(act):
            act.wait_ge(zeroed, ONE + ZEROED)

            def normalize(i, b, first=False):
                act.wait_ge(var_ready, ONE + i + 1)
                act.activation(col[:, 0:1], grp[:, 1:2], ACT.Sqrt, scale=-1.0, bias=eps[:, 0:1]).then_inc(std_ready, 1)
                act.wait_ge(affine_ready, ONE + i + 1)
                if not first:
                    act.wait_ge(v_summed, ONE + (i - 1) * TILE_GROUPS)
                    act.wait_ge(var2_ready, ONE + i - 1)
                act.activation(inner[b], image(ximg), ACT.Identity, scale=col[:, 1:2], bias=col[:, 2:3]).then_inc(xn_ready, 1)

            def step(i, b, last_pair):
                act.wait_ge(k_stored, ONE + i * 48)
                for c in range(NCH):
                    cs = slice(c * CH, (c + 1) * CH)
                    act.wait_ge(k_summed, ONE + i * NCH + c + 1)
                    act.activation(kp[0][:, cs], ps_k[:, c % 2, :], ACT.Copy).then_inc(k1_ready, 1)
                    act.wait_ge(kres_ready, ONE + i * NCH + c + 1)
                    act.activation(kp[1][:, cs], kres[:, c % 2, :], ACT.Copy).then_inc(k2_ready, 1)
                act.wait_ge(q_summed, ONE + i + 1)
                act.activation(cat[:, :], ps_q[:, :], ACT.Copy, scale=1.0 / IMG).then_inc(cat_ready, 1)
                act.wait_ge(v_stored, ONE + i * 16)
                for c in range(NCH + 1):
                    if c < NCH:
                        act.wait_ge(v_summed, ONE + i * NCH + c + 1)
                        act.wait_ge(v_turned, ONE + i * NCH + c + 1)
                        act.activation(vc[:, c % 2, :], ps_k[:, c % 2, :], ACT.Copy).then_inc(vc_ready, 1)
                    if c:
                        g = c - 1
                        act.wait_ge(v_turned, ONE + i * NCH + c + 2)
                        act.activation(vparts[:, :, 4 * g:4 * g + 4, 0:DH],
                                       ps_v[:, g % 2, :].rearrange("p (t h c) -> p h t c", t=4, h=2),
                                       ACT.Copy).then_inc(v1_ready, 1)
                    if c == 1 and not last_pair:
                        normalize(i + 1, 1 - b)
                    if c == 3:
                        act.wait_ge(c1_done, ONE + i + 1)
                        act.activation(gates[:, :], ps_c[:, :], ACT.Sigmoid, bias=vecs[:, 0:1]).then_inc(gates_ready, 1)
                act.wait_ge(var2_ready, ONE + i + 1)
                act.activation(col[:, 3:4], mv[:, 1:2], ACT.Sqrt, bias=eps[:, 0:1]).then_inc(std2_ready, 1)
                act.wait_ge(qaff_ready, ONE + i + 1)
                act.activation(gated[:, :], gated[:, :], ACT.Identity, scale=col[:, 5:6], bias=col[:, 6:7]).then_inc(q_ready, 1)
                act.wait_ge(q_ready, ONE + i + 1)
                act.wait_ge(q_stored, ONE + i * 48)
                act.activation(qp[0][:, :], gated[:, :], ACT.Copy).then_inc(q1_ready, 1)
                if last_pair:
                    act.wait_ge(qres_ready, ONE + i + 1)
                    act.activation(qp[1][:, :], resid[:, :], ACT.Copy).then_inc(q2_ready, 1)

            normalize(0, 0, True)
            act.wait_ge(w_ready, ONE + 16 * N_CONV_W)
            pairs(act, step)

        @block.vector
        def _(dve):
            STEPS = 16
            dve.sem_inc(v_turned, 2)
            dve.sem_inc(v2_ready, 2)
            dve.wait_ge(zeroed, ONE + ZEROED)

            class Links:
                def __init__(s, turn):
                    s.turn, s.n = turn, 0

                def __call__(s, ins):
                    s.n += 1
                    ins.then_inc(dve_step, 1)
                    dve.wait_ge(dve_step, ONE + s.turn * STEPS + s.n)

                def end(s):
                    assert s.n <= STEPS
                    dve.sem_inc(dve_step, STEPS - s.n)

            def channel_stats(link, t):
                for c in range(NCH):
                    last = dve.bn_stats(stats[:, c, :], t[:, c * CH:(c + 1) * CH])
                link(last)

            def group_norm(link, i):
                dve.wait_ge(x_loaded, ONE + (i + 1) * 16)
                channel_stats(link, ximg)
                stand(dve, stood)
                link(dve.bn_aggr(mv[:, :], stats[:, :, :].rearrange("p a b -> p (a b)")))
                dve.tensor_copy(chan[:, 0:1], mv[:, 0:1])
                dve.scalar_tensor_tensor(chan[:, 1:2], mv[:, 0:1], mv[:, 0:1], mv[:, 1:2],
                                         ALU.mult, ALU.add).then_inc(chan_ready, 1)
                dve.wait_ge(grp_summed, ONE + i + 1)
                link(dve.tensor_copy(grp[:, :], ps_g[:, :]))
                link(dve.tensor_tensor(col[:, 7:8], grp[:, 0:1], grp[:, 0:1], ALU.mult))
                dve.tensor_tensor(grp[:, 1:2], col[:, 7:8], grp[:, 1:2], ALU.subtract).then_inc(var_ready, 1)
                dve.wait_ge(std_ready, ONE + i + 1)
                link(dve.reciprocal(col[:, 1:2], col[:, 0:1]))
                dve.tensor_scalar(col[:, 2:3], grp[:, 0:1], -1.0, col[:, 1:2], ALU.mult, ALU.mult).then_inc(affine_ready, 1)

            def sums(link, i, b, first=False):
                dve.wait_ge(xn_ready, ONE + i + 1)
                if not first:
                    dve.wait_ge(q_summed, ONE + i)
                dve.tensor_reduce(colsum[:, 1, 1:IMG + 1], inner[b].rearrange("p h w -> p w h"), AX.X, ALU.add)
                link(dve.tensor_reduce(rowsum[:, 1, 1:IMG + 1], inner[b], AX.X, ALU.add))
                for d, edge in ((0, IMG), (2, 1)):
                    dve.tensor_tensor(colsum[:, d, 1:IMG + 1], colsum[:, 1, 1:IMG + 1], xpads[b][:, edge, 1:IMG + 1], ALU.subtract)
                    dve.tensor_tensor(rowsum[:, d, 1:IMG + 1], rowsum[:, 1, 1:IMG + 1], xpads[b][:, 1:IMG + 1, edge],
                                      ALU.subtract).then_inc(sums_ready, 1)

            def step(i, b, last_pair):
                link = Links(i + 1)
                dve.wait_ge(k_stored, ONE + i * 48)
                for c in range(NCH + 1):
                    if c < NCH:
                        dve.wait_ge(k1_ready, ONE + i * NCH + c + 1)
                        if c > 1:
                            dve.wait_ge(k3_ready, ONE + i * NCH + c - 1)
                        dve.tensor_tensor(kres[:, c % 2, :], ps_k[:, c % 2, :], kp[0][:, c * CH:(c + 1) * CH],
                                          ALU.subtract).then_inc(kres_ready, 1)
                    if c:
                        dve.wait_ge(k2_ready, ONE + i * NCH + c)
                        cs = slice((c - 1) * CH, c * CH)
                        dve.tensor_tensor(kp[2][:, cs], kres[:, (c - 1) % 2, :], kp[1][:, cs],
                                          ALU.subtract).then_inc(k3_ready, 1)
                if not last_pair:
                    group_norm(link, i + 1)
                dve.wait_ge(v_stored, ONE + i * 16)
                for g in range(TILE_GROUPS):
                    dve.wait_ge(v1_ready, ONE + i * TILE_GROUPS + g + 1)
                    dve.tensor_tensor(vparts[:, :, 4 * g:4 * g + 4, DH:2 * DH],
                                      ps_v[:, g % 2, :].rearrange("p (t h c) -> p h t c", t=4, h=2),
                                      vparts[:, :, 4 * g:4 * g + 4, 0:DH], ALU.subtract).then_inc(v2_ready, 1)
                    if g == 1 and not last_pair:
                        sums(link, i + 1, 1 - b)
                    if g == 4:
                        dve.wait_ge(gates_ready, ONE + i + 1)
                        link(dve.tensor_tensor(image(gated), inner[b], gates[:, 0:IMG].unsqueeze(1).broadcast_to([P, IMG, IMG]), ALU.mult))
                    if g == 5:
                        link(dve.tensor_tensor(image(gated), image(gated),
                                               gates[:, IMG:2 * IMG].unsqueeze(2).broadcast_to([P, IMG, IMG]), ALU.mult))
                    if g == 6:
                        channel_stats(link, gated)
                        stand(dve, stood)
                        dve.bn_aggr(mv[:, :], stats[:, :, :].rearrange("p a b -> p (a b)")).then_inc(var2_ready, 1)
                dve.wait_ge(std2_ready, ONE + i + 1)
                link(dve.reciprocal(col[:, 4:5], col[:, 3:4]))
                link(dve.tensor_tensor(col[:, 5:6], col[:, 4:5], vecs[:, 1:2], ALU.mult))
                link(dve.tensor_tensor(col[:, 7:8], mv[:, 0:1], col[:, 5:6], ALU.mult))
                dve.tensor_tensor(col[:, 6:7], vecs[:, 2:3], col[:, 7:8], ALU.subtract).then_inc(qaff_ready, 1)
                dve.wait_ge(q1_ready, ONE + i + 1)
                dve.wait_ge(q3_ready, ONE + i)
                dve.tensor_tensor(resid[:, :], gated[:, :], qp[0][:, :], ALU.subtract).then_inc(qres_ready, 1)
                if last_pair:
                    dve.wait_ge(q2_ready, ONE + i + 1)
                    dve.wait_ge(q_stored, ONE + i * 48)
                    dve.tensor_tensor(qp[2][:, :], resid[:, :], qp[1][:, :], ALU.subtract).then_inc(q3_ready, 1)
                link.end()

            link = Links(0)
            group_norm(link, 0)
            sums(link, 0, 0, True)
            dve.wait_ge(w_ready, ONE + 16 * N_CONV_W)
            link.end()
            pairs(dve, step)


def attention_phase(nc, ctx, ident, q_split, k_split, v_split, attn_out):
    def sb(name, shape, dt=F32):
        return ctx.enter_context(nc.sbuf_tensor(name, shape, dt))

    sem, start_semaphores = phase_semaphores(nc, ctx, "")

    qa, qb, ka, kb, kc = ([sb(f"{n}{j}", [P, L], BF16) for j in range(2)] for n in ("q12_", "q13_", "k11_", "k22_", "k31_"))
    vv = [sb(f"v12_{j}", [P, QT, P], BF16) for j in range(2)]
    prob = [sb(f"prob{j}", [P, L]) for j in range(2)]
    hi, lo = sb("p_hi", [P, 2, CH], BF16), sb("p_lo", [P, 2, CH], BF16)
    mx, nmx = sb("mx", [P, 2, NCH]), sb("nmx", [P, 2])
    rs, rsum, rinv = sb("rs", [P, 2, 4]), sb("rsum", [P, 2]), sb("rinv", [P, 2])
    otmp = sb("otmp", [P, DH])
    oh = sb("o_head", [P, 2, QT, DH])
    ps_s = ctx.enter_context(nc.psum_tensor("ps_s", [P, 4, CH], F32))
    ps_t = ctx.enter_context(nc.psum_tensor("ps_t", [P, 2, CH], F32))
    ps_o = ctx.enter_context(nc.psum_tensor("ps_o", [P, 2, CH], F32))

    loaded = [sem(f"head_loaded{j}") for j in range(2)]
    s_ready, s_copied, max_ready, exp_ready = sem("s_ready"), sem("s_copied"), sem("max_ready"), sem("exp_ready")
    t_ready, hi_ready, lo_ready, pv_done = sem("t_ready"), sem("hi_ready"), sem("lo_ready"), sem("pv_done")
    o_ready, o_stored, fin_step = sem("o_ready"), sem("o_stored"), sem("fin_step")

    LOADS = 11
    SC = L // CH
    EC = SC // 2
    TG = L // CH
    scale = 1.0 / 16.0

    SCORES_AT = (0, 0, 1, 2, 3, 4, 5, 6)
    EXPS_AT = (0, 2, 4, 6)
    MAX_AT = 6
    FINISH_AT = 2

    def tiles(eng, head, step):
        step(head * QT, 0, 0, False, True)
        with eng.Fori(0, QT // 2 - 1) as it:
            for u in (1, 0):
                step(head * QT + it * 2 + 2 - u, it * 2 + 2 - u, u, True, True)
        step(head * QT + QT - 1, QT - 1, 1, True, False)

    def heads(eng, body):
        with eng.Fori(0, HEADS // 2) as hp:
            for j in range(2):
                body(hp * 2 + j, j, hp)

    start_semaphores()
    with nc.Block() as block:
        @block.sync
        def _(sp):
            def load(h, j):
                rows = ds(h * DH, DH)
                top, bottom = slice(0, DH), slice(DH, P)
                for dst, part, src in ((qa[j][top], 0, q_split), (qa[j][bottom], 1, q_split),
                                       (ka[j][top], 0, k_split), (ka[j][bottom], 0, k_split),
                                       (kb[j][top], 1, k_split), (kb[j][bottom], 1, k_split),
                                       (qb[j][top], 0, q_split), (qb[j][bottom], 2, q_split),
                                       (kc[j][top], 2, k_split), (kc[j][bottom], 0, k_split)):
                    sp.dma_start(dst, src[part, rows, :]).then_inc(loaded[j], 16)
                sp.dma_start(vv[j][:, :, :].rearrange("p t c -> p (t c)"), v_split[h]).then_inc(loaded[j], 16)

            def store(h, j):
                sp.wait_ge(o_ready, ONE + (h + 1) * QT + 1)
                sp.dma_start(attn_out[h], oh[:, j, :, :].rearrange("p t c -> p (t c)")).then_inc(o_stored, 16)

            load(0, 0)
            load(1, 1)
            with sp.Fori(1, HEADS // 2) as hp:
                for j in range(2):
                    store(hp * 2 + j - 2, j)
                    load(hp * 2 + j, j)
            store(HEADS - 2, 0)
            store(HEADS - 1, 1)
            sp.wait_ge(o_stored, ONE + 16 * HEADS)

        @block.tensor
        def _(pe):
            def head(h, j, hp):
                def scores(g, t, u, c):
                    pe.wait_ge(s_copied, ONE + g * SC + c + 1)
                    for n, (a, b) in enumerate(((qa, ka), (qa, kb), (qb, kc))):
                        last = pe.matmul(ps_s[:, c % 4, :], a[j][:, ds(t * P, P)], b[j][:, c * CH:(c + 1) * CH],
                                         start=(n == 0), stop=(n == 2))
                    last.then_inc(s_ready, 1)

                def transposes(g, t, u, k):
                    pe.wait_ge(exp_ready, ONE + g * EC + k // 2 + 1)
                    pe.wait_ge(lo_ready, ONE + g * TG + k + 1)
                    for m in range(4):
                        last = pe.transpose(ps_t[:, k % 2, m * P:(m + 1) * P],
                                            prob[u][:, (4 * k + m) * P:(4 * k + m + 1) * P], ident[:, :])
                    last.then_inc(t_ready, 1)

                def values(g, t, u, k):
                    pe.wait_ge(lo_ready, ONE + g * TG + k + 3)
                    if k == 0:
                        pe.wait_ge(o_ready, ONE + g)
                    for m in range(4):
                        for n, (part, cols) in enumerate(((hi, P), (lo, DH))):
                            last = pe.matmul(ps_o[:, u, 0:cols], part[:, k % 2, m * P:(m + 1) * P], vv[j][:, 4 * k + m, 0:cols],
                                             start=(k == 0 and m == 0 and n == 0), stop=(k == TG - 1 and m == 3 and n == 1))
                    last.then_inc(pv_done, 1)

                def step(g, t, u, before, after):
                    for k in range(TG):
                        if after:
                            for c in range(SC):
                                if SCORES_AT[c] == k:
                                    scores(g + 1, t + 1, 1 - u, c)
                        if k >= 2:
                            values(g, t, u, k - 2)
                        elif before:
                            values(g - 1, t - 1, 1 - u, TG - 2 + k)
                        transposes(g, t, u, k)
                    if not after:
                        values(g, t, u, TG - 2)
                        values(g, t, u, TG - 1)

                pe.wait_ge(loaded[j], ONE + (hp + 1) * 16 * LOADS)
                for c in range(SC):
                    scores(h * QT, 0, 0, c)
                tiles(pe, h, step)

            heads(pe, head)

        @block.scalar
        def _(act):
            def exps(g, u, c):
                if c == 0:
                    act.wait_ge(max_ready, ONE + g + 1)
                cs = slice(c * 2 * CH, (c + 1) * 2 * CH)
                act.activation(prob[u][:, cs], prob[u][:, cs], ACT.Exp, bias=nmx[:, u:u + 1],
                               accum_out=rs[:, u, c:c + 1]).then_inc(exp_ready, 1)

            def his(g, k):
                act.wait_ge(t_ready, ONE + g * TG + k + 1)
                act.wait_ge(pv_done, ONE + g * TG + k + 1)
                act.activation(hi[:, k % 2, :], ps_t[:, k % 2, :], ACT.Copy).then_inc(hi_ready, 1)

            def step(g, t, u, before, after):
                if not before:
                    exps(g, u, 0)
                for k in range(TG):
                    his(g, k)
                    if k in EXPS_AT:
                        c = EXPS_AT.index(k) + 1
                        if c < EC:
                            exps(g, u, c)
                        elif after:
                            exps(g + 1, 1 - u, 0)

            act.preload_act_table(ACT.Exp)
            heads(act, lambda h, j, hp: tiles(act, h, step))

        @block.vector
        def _(dve):
            def head(h, j, hp):
                def copies(g, u, c):
                    dve.wait_ge(s_ready, ONE + g * SC + c + 1)
                    dve.tensor_scalar(prob[u][:, c * CH:(c + 1) * CH], ps_s[:, c % 4, :], scale, -FLT_MAX,
                                      ALU.mult, ALU.max, accum_out=mx[:, u, c:c + 1]).then_inc(s_copied, 1)

                def maximum(g, u):
                    dve.wait_ge(s_copied, ONE + g * SC + SC + 4)
                    dve.tensor_reduce(nmx[:, u:u + 1], mx[:, u, :], AX.X, ALU.max, negate=True).then_inc(max_ready, 1)

                def los(g, u, k):
                    dve.wait_ge(hi_ready, ONE + g * TG + k + 1)
                    dve.tensor_tensor(lo[:, k % 2, :], ps_t[:, k % 2, :], hi[:, k % 2, :], ALU.subtract).then_inc(lo_ready, 1)

                def finish(g, t, u):
                    dve.tensor_reduce(rsum[:, u:u + 1], rs[:, u, :], AX.X, ALU.add).then_inc(fin_step, 1)
                    dve.wait_ge(fin_step, ONE + g * 3 + 1)
                    dve.reciprocal(rinv[:, u:u + 1], rsum[:, u:u + 1]).then_inc(fin_step, 1)
                    dve.wait_ge(fin_step, ONE + g * 3 + 2)
                    dve.wait_ge(pv_done, ONE + (g + 1) * TG + 2)
                    dve.tensor_scalar(otmp[:, :], ps_o[:, u, DH:P], rinv[:, u:u + 1], None, ALU.mult).then_inc(fin_step, 1)
                    dve.wait_ge(fin_step, ONE + g * 3 + 3)
                    dve.scalar_tensor_tensor(oh[:, j, ds(t, 1), :].rearrange("p a c -> p (a c)"), ps_o[:, u, 0:DH],
                                             rinv[:, u:u + 1], otmp[:, :], ALU.mult, ALU.add).then_inc(o_ready, 1)

                def step(g, t, u, before, after):
                    for k in range(TG):
                        if after:
                            for c in range(SC):
                                if SCORES_AT[c] == k:
                                    copies(g + 1, 1 - u, c)
                        if after and k == MAX_AT:
                            maximum(g + 1, 1 - u)
                        los(g, u, k)
                        if before and k == FINISH_AT:
                            finish(g - 1, t - 1, 1 - u)
                    if not after:
                        finish(g, t, u)

                if j == 0:
                    dve.wait_ge(o_stored, ONE + hp * 32)
                for c in range(SC):
                    copies(h * QT, 0, c)
                maximum(h * QT, 0)
                tiles(dve, h, step)

            dve.sem_inc(s_copied, 4)
            dve.sem_inc(lo_ready, 2)
            dve.sem_inc(pv_done, 2)
            dve.sem_inc(o_ready, 1)
            heads(dve, head)


def tokens_phase(nc, ctx, ident, x, attn_out, t1, u1):
    def sb(name, shape, dt=F32):
        return ctx.enter_context(nc.sbuf_tensor(name, shape, dt))

    sem, start_semaphores = phase_semaphores(nc, ctx, "")

    xin = sb("tk_x", [P, 2, 2, CH])
    oin = sb("tk_o", [P, 2, 4, 4 * DH])
    tt = sb("tk_t", [P, 2, 4, C])
    nt = sb("tk_n", [P, 2, 4, C])
    ut = sb("tk_u", [P, 2, 2, CH])
    stats, mv = sb("tk_stats", [P, 4, 6]), sb("tk_mv", [P, 4, 2])
    std, rstd, eps = sb("tk_std", [P, 4]), sb("tk_rstd", [P, 4]), sb("tk_eps", [P, 1])
    ps_x = ctx.enter_context(nc.psum_tensor("tk_ps_x", [P, 2, 2, CH], F32))
    ps_u = ctx.enter_context(nc.psum_tensor("tk_ps_u", [P, 2, 2, CH], F32))
    eps_ready = sem("tk_eps_ready")
    in_loaded = [sem(f"tk_in_loaded{j}") for j in range(2)]
    x_turned, t_ready, stats_step, var_ready, std_ready = (sem(f"tk_{n}") for n in ("x_turned", "t_ready", "stats_step", "var_ready", "std_ready"))
    n_ready, u_turned, u_ready, stood = (sem(f"tk_{n}") for n in ("n_ready", "u_turned", "u_ready", "stood"))
    stored = [sem(f"tk_stored{j}") for j in range(2)]
    N = B * NCH

    def chunks(eng, body):
        with eng.Fori(0, B) as b:
            with eng.Fori(0, NCH // 2) as h:
                for j in range(2):
                    body(b * NCH + h * 2 + j, j, b, h * 2 + j)

    start_semaphores()
    with nc.Block() as block:
        @block.sync
        def _(sp):
            def body(n, j, b, c):
                sp.wait_ge(t_ready, ONE + n * 2 + 2)
                stand(sp, stood)
                sp.dma_start(xin[:, j, :, :], x[ds(b * C, C), ds(c * CH, CH)].rearrange("(k p) l -> p k l", p=P)).then_inc(in_loaded[j], 16)
                sp.dma_start(oin[:, j, :, :], attn_out[ds(b * 4, 4), :, ds(c * 4 * DH, 4 * DH)].rearrange("g p n -> p g n")).then_inc(in_loaded[j], 16)
            chunks(sp, body)
            for j in range(2):
                sp.wait_ge(stored[j], ONE + 16 * N)

        @block.tensor
        def _(pe):
            def turn_x(n, j, loads):
                pe.wait_ge(in_loaded[j], ONE + loads * 32)
                pe.wait_ge(t_ready, ONE + n * 2 + 2)
                for t in range(4):
                    for k in range(2):
                        last = pe.transpose(ps_x[:, j, t // 2, (t % 2) * C + k * P:(t % 2) * C + (k + 1) * P],
                                            xin[:, j, k, t * P:(t + 1) * P], ident[:, :])
                last.then_inc(x_turned, 1)

            def turn_u(n, j):
                pe.wait_ge(n_ready, ONE + n + 1)
                pe.wait_ge(u_ready, ONE + n)
                for t in range(4):
                    for k in range(2):
                        last = pe.transpose(ps_u[:, j, k, t * P:(t + 1) * P], nt[:, j, t, k * P:(k + 1) * P], ident[:, :])
                last.then_inc(u_turned, 1)

            turn_x(0, 0, 1)
            with pe.Fori(0, N // 2 - 1) as h:
                for j in range(2):
                    turn_x(h * 2 + j + 1, 1 - j, h + 1 + j)
                    turn_u(h * 2 + j, j)
            turn_x(N - 1, 1, N // 2)
            turn_u(N - 2, 0)
            turn_u(N - 1, 1)

        @block.scalar
        def _(act):
            def body(n, j, b, c):
                act.wait_ge(var_ready, ONE + n + 1)
                act.activation(std[:, :], mv[:, :, 1], ACT.Sqrt, bias=eps[:, 0:1]).then_inc(std_ready, 1)
                act.wait_ge(t_ready, ONE + n * 2 + 6)
                stand(act, stood)
                act.dma_start(t1[n], tt[:, j, :, :].rearrange("p t c -> p (t c)")).then_inc(stored[j], 16)
                act.wait_ge(u_turned, ONE + n + 2)
                act.wait_ge(stored[j], ONE + b * (16 * NCH) + (c - j) * 16)
                act.activation(ut[:, j, :, :], ps_u[:, j, :, :], ACT.Copy).then_inc(u_ready, 1)
                act.wait_ge(u_ready, ONE + n + 2)
                stand(act, stood)
                act.dma_start(u1[n], ut[:, j, :, :].rearrange("p k l -> p (k l)")).then_inc(stored[j], 16)
            act.wait_ge(eps_ready, ONE + 1)
            chunks(act, body)

        @block.vector
        def _(dve):
            def body(n, j, b, c):
                dve.wait_ge(x_turned, ONE + n + 1)
                dve.wait_ge(stored[j], ONE + b * (16 * NCH) + (c - j) * 16)
                for h in range(2):
                    o = oin[:, j, :, :].rearrange("p g (t c) -> p t g c", t=4)[:, 2 * h:2 * h + 2]
                    dve.tensor_tensor(tt[:, j, 2 * h:2 * h + 2, :].rearrange("p t (g c) -> p t g c", g=4),
                                      ps_x[:, j, h, :].rearrange("p (t g c) -> p t g c", t=2, g=4), o, ALU.add).then_inc(t_ready, 1)
                dve.wait_ge(t_ready, ONE + n * 2 + 6)
                for t in range(4):
                    last = dve.bn_stats(stats[:, t, :], tt[:, j, t, :])
                last.then_inc(stats_step, 1)
                dve.wait_ge(stats_step, ONE + n * 2 + 1)
                stand(dve, stood)
                for t in range(4):
                    last = dve.bn_aggr(mv[:, t, :], stats[:, t, :])
                last.then_inc(var_ready, 1)
                dve.wait_ge(std_ready, ONE + n + 1)
                dve.reciprocal(rstd[:, :], std[:, :]).then_inc(stats_step, 1)
                dve.wait_ge(stats_step, ONE + n * 2 + 2)
                dve.wait_ge(u_turned, ONE + n)
                for t in range(4):
                    last = dve.tensor_scalar(nt[:, j, t, :], tt[:, j, t, :], mv[:, t, 0:1], rstd[:, t:t + 1],
                                             ALU.subtract, ALU.mult)
                last.then_inc(n_ready, 1)
            dve.memset(eps[:, :], GN_EPS).then_inc(eps_ready, 1)
            for t, v in ((t_ready, 4), (u_turned, 1), (u_ready, 1)):
                dve.sem_inc(t, v)
            chunks(dve, body)


def mamba_phase(nc, ctx, ident, w, u1, m_dirs):
    def sb(name, shape, dt=F32):
        return ctx.enter_context(nc.sbuf_tensor(name, shape, dt))

    sem, start_semaphores = phase_semaphores(nc, ctx, "mb_")

    N = B * NCH
    K = 4
    S = 16
    R = 16
    BC = 2 * S
    NX = 3 * BC + R
    W = CH + 3

    win = sb("win", [P, 2, 2, 8 * P])
    wx = sb("wx", [P, 2, K, NX])
    wdt = sb("wdt", [NX, 2, K * P])
    wout = sb("wout", [P, 2, K, C])
    cw, cb = sb("cw", [P, 2, K, 4]), sb("cb", [P, 2, K])
    dtb, dskip = sb("dtb", [P, 2, K]), sb("dskip", [P, 2, K])
    amat = sb("amat", [P, 2, K, S])
    keep = sb("keep", [P, N])
    one = sb("one", [P, 1])
    u = sb("mb_u", [P, 2, 2, CH])
    xpre = sb("xpre", [P, K, W])
    halo = sb("halo", [P, 2, K, 3])
    xs = sb("xs", [P, 2, K, CH])
    zs = sb("zs", [P, 2, K, CH])
    dt = sb("dt", [P, 2, K, CH])
    dtx = sb("dtx", [P, 2, K, CH])
    sp_tmp = sb("sp_tmp", [P, K, CH])
    xdt = sb("xdt", [NX, CH])
    xbc = sb("xbc", [3 * BC, 2, CH], BF16)
    xres = sb("xres", [3 * BC, CH])
    pick = sb("pick", [3 * BC, BC], BF16)
    bb, cc = sb("bb", [P, 4, CH]), sb("cc", [P, 4, CH])
    da = sb("da", [P, 2, K, CH])
    hh = sb("hh", [P, 4, K, CH])
    state = sb("state", [P, 2, K, S])
    mo = sb("mo", [P, 4, C])
    ps_a = ctx.enter_context(nc.psum_tensor("mb_ps_a", [P, 2, CH], F32))
    ps_b = ctx.enter_context(nc.psum_tensor("mb_ps_b", [P, 2, CH], F32))
    ps_y = ctx.enter_context(nc.psum_tensor("mb_ps_y", [P, K, CH], F32))

    win_loaded, w_loaded, consts, a_exp, a_neg = sem("win_loaded"), sem("w_loaded"), sem("consts"), sem("a_exp"), sem("a_neg")
    u_loaded = [sem(f"u_loaded{j}") for j in range(2)]
    a_ready, a_free = sem("a_ready"), sem("a_free")
    bc_ready, bc_copied = sem("bc_ready"), sem("bc_copied")
    tap_done, conv_step, conv_done, silu_done, soft_step, soft_done = (sem(n) for n in ("tap_done", "conv_step", "conv_done", "silu_done", "soft_step", "soft_done"))
    x_part1, x_res1, x_part2, x_split = (sem(n) for n in ("x_part1", "x_res1", "x_part2", "x_split"))
    dt_ready, dtx_ready = sem("dt_ready"), sem("dtx_ready")
    da_ready, dbx_ready, scanned, saved, hc_ready, summed = (sem(n) for n in ("da_ready", "dbx_ready", "scanned", "saved", "hc_ready", "summed"))
    kept, y_ready, gated, mo_stored, stood, out_copied = (sem(n) for n in ("kept", "y_ready", "gated", "mo_stored", "stood", "out_copied"))

    USES = 15

    PE_IN, PE_OUT, PE_X, PE_DT = (1, 2, 6, 7), (2, 4), 8, (11, 12)
    ACT_IN, ACT_OUT, ACT_TAP, ACT_SILU, ACT_X, ACT_DT, ACT_SOFT = (2, 3, 7, 8), (5, 6), 3, 8, 10, (12, 13), 13
    DVE_SKIP, DVE_CONV, DVE_SPLIT, DVE_WEIGH = 1, (4, 7), (10, 11), 14
    POOL_GATE = 3
    AHEAD = 4
    N_CONSTS = 9

    class Step:
        def __init__(s, n, j, tail=True, front=True):
            s.n, s.j, s.tail, s.front = n, j, tail, front
            s.k = n * 2 + j
            s.use0, s.bank0 = s.k * USES + USES - 4, (j + 1) % 2
            s.nj, s.nn = 1 - j, n + j
            s.fronts = s.k + 1
            s.scanning = True
            s.x_use, s.out_use = (0 if tail else 2), (K if front else 0)

    def before():
        s = Step(0, 0, tail=False)
        s.k, s.use0, s.bank0, s.nj, s.nn = -1, -2, 0, 0, 0
        s.scanning = False
        return s

    def after():
        s = Step(N, 0, front=False)
        s.use0, s.bank0 = s.use0 - (USES - 2), (s.bank0 + USES - 2) % 2
        s.fronts = s.k
        return s

    def run(eng, begin, step, end):
        begin(before())
        step(Step(0, 0, tail=False))
        step(Step(0, 1))
        with eng.Fori(1, N - 1) as n:
            for j in range(2):
                step(Step(n, j))
        step(Step(N - 1, 0))
        step(Step(N - 1, 1, front=False))
        end(after())

    def in_use(s, e):
        return s.x_use + e if e < K else 2 + e

    def bank(s, idx):
        return (s.bank0 + idx) % 2

    start_semaphores()
    with nc.Block() as block:
        @block.sync
        def _(sp):
            def load(k, j, n):
                sp.dma_start(u[:, j, :, :].rearrange("p k l -> p (k l)"), u1[n if j == 0 else (N - 1) - n]).then_inc(u_loaded[j], 16)

            load(0, 0, 0)
            sp.dma_start(win[:, 0], w["in_proj_w"][0].rearrange("k p e -> p k e")).then_inc(win_loaded, 16)
            n = 0
            for dst, src in ((wx[:, :, :, 0:BC], w["x_proj_w"][:, :, :, R:].rearrange("j k p e -> p j k e")),
                             (wx[:, :, :, BC:2 * BC], w["x_proj_w"][:, :, :, R:].rearrange("j k p e -> p j k e")),
                             (wx[:, :, :, 2 * BC:3 * BC], w["x_proj_w"][:, :, :, R:].rearrange("j k p e -> p j k e")),
                             (wx[:, :, :, 3 * BC:NX], w["x_proj_w"][:, :, :, 0:R].rearrange("j k p e -> p j k e")),
                             (wdt[3 * BC:NX, :, :], w["dt_proj_w"].rearrange("j r d -> r j d")),
                             (wout[:, :, :, :], w["out_proj_w"].rearrange("j k p e -> p j k e")),
                             (cw[:, :, :, :], w["conv_w"].rearrange("j (k p) t -> p j k t", p=P)),
                             (amat[:, :, :, :], w["A_log"].rearrange("j (k p) s -> p j k s", p=P))):
                for j in range(2):
                    sp.dma_start(dst[:, j], src[:, j]).then_inc(w_loaded, 16)
                    n += 1
            sp.dma_start(win[:, 1], w["in_proj_w"][1].rearrange("k p e -> p k e")).then_inc(w_loaded, 16)
            n += 1
            for dst, src in ((cb, "conv_b"), (dtb, "dt_proj_b"), (dskip, "Dp")):
                for j in range(2):
                    for k in range(K):
                        sp.dma_start(dst[:, j, k:k + 1], w[src][j, k * P:(k + 1) * P].unsqueeze(1)).then_inc(w_loaded, 16)
                        n += 1
            assert n == N_MAMBA_W

            def store(k, j, n):
                sp.wait_ge(out_copied, ONE + (k + 1) * 2)
                stand(sp, stood)
                sp.dma_start(m_dirs[j, n], mo[:, :, :].rearrange("p t c -> p (t c)")).then_inc(mo_stored, 16)

            load(1, 1, 0)
            with sp.Fori(0, N - 1) as n:
                for j in range(2):
                    sp.wait_ge(dtx_ready, ONE + n * 2 + j + 1)
                    stand(sp, stood)
                    load(n * 2 + j + 2, j, n + 1)
                    store(n * 2 + j, j, n)
            store(2 * N - 2, 0, N - 1)
            store(2 * N - 1, 1, N - 1)
            sp.wait_ge(mo_stored, ONE + 32 * N)

        @block.tensor
        def _(pe):
            def fill(s, idx, mms):
                pe.wait_ge(a_free, ONE + s.use0 + idx + 1)
                for out, lhsT, rhs, start, stop in mms(ps_a[:, bank(s, idx), :]):
                    last = pe.matmul(out, lhsT, rhs, start=start, stop=stop)
                last.then_inc(a_ready, 1)

            def in_proj(s, e):
                if e == 0:
                    pe.wait_ge(u_loaded[s.nj], ONE + (s.nn + 1) * 16)
                fill(s, in_use(s, e), lambda ps: [(ps, win[:, s.nj, k, e * P:(e + 1) * P], u[:, s.nj, k, :], k == 0, k == 1)
                                           for k in range(2)])

            def x_proj(s):
                if not s.scanning:
                    pe.wait_ge(w_loaded, ONE + 16 * N_MAMBA_W)
                pe.wait_ge(silu_done, ONE + (s.k + 2) * 2 - 1)
                fill(s, 10, lambda ps: [(ps[0:NX], wx[:, s.nj, k, :], xs[:, s.nj, k, :], k == 0, k == K - 1)
                                        for k in range(K)])

            def dt_proj(s, k):
                if k == 0:
                    pe.wait_ge(a_free, ONE + s.use0 + 13)
                fill(s, 11 + k, lambda ps: [(ps, wdt[3 * BC:NX, s.nj, k * P:(k + 1) * P], xdt[3 * BC:NX, :], True, True)])

            def spread(s, i):
                if i == S:
                    pe.wait_ge(x_split, ONE + s.k + 2)
                for n in range(2):
                    pe.wait_ge(bc_copied, ONE + s.k * 2 * S + 2 * i + n + 1)
                    row = S * n + i % S
                    pe.matmul(ps_b[:, n, :], pick[:, row:row + 1].broadcast_to([3 * BC, P]),
                              xbc[:, s.j if i < S else s.nj, :], start=True, stop=True).then_inc(bc_ready, 1)

            def accumulate(s, i):
                pe.wait_ge(hc_ready, ONE + s.k * S + i + 5)
                if i == 0:
                    pe.wait_ge(y_ready, ONE + s.k * K)
                for k in range(K):
                    last = pe.matmul(ps_y[:, k, :], ident[:, :], hh[:, i % 4, k, :], start=(i == 0), stop=(i % S == S - 1))
                last.then_inc(summed, 1)

            def tail(s, h):
                if h == 0:
                    pe.wait_ge(gated, ONE + s.k)
                fill(s, s.out_use + h, lambda ps: [(ps[:, t * C:(t + 1) * C], sp_tmp[:, k, (2 * h + t) * P:(2 * h + t + 1) * P],
                                                    wout[:, s.nj, k, :], k == 0, k == K - 1) for t in range(2) for k in range(K)])

            def front(s, slot=None):
                for q, place in enumerate(PE_IN):
                    if slot in (None, place):
                        in_proj(s, 2 * q)
                        in_proj(s, 2 * q + 1)
                if slot in (None, PE_X):
                    x_proj(s)
                for q, place in enumerate(PE_DT):
                    if slot in (None, place):
                        dt_proj(s, 2 * q)
                        dt_proj(s, 2 * q + 1)

            def step(s):
                for i in range(S):
                    if s.front:
                        front(s, i)
                    if i + AHEAD < S or s.front:
                        spread(s, i + AHEAD)
                    if i or s.tail:
                        accumulate(s, i - 1)
                    if i in PE_OUT and s.tail:
                        tail(s, PE_OUT.index(i))

            def begin(s):
                front(s)
                for i in range(AHEAD):
                    spread(s, S + i)

            def end(s):
                accumulate(s, -1)
                tail(s, 0)
                tail(s, 1)

            pe.wait_ge(consts, ONE + N_CONSTS)
            pe.wait_ge(win_loaded, ONE + 16)
            run(pe, begin, step, end)

        @block.scalar
        def _(act):
            def data(j):
                return slice(3, W) if j == 0 else slice(0, CH)

            def in_copy(s, e):
                act.wait_ge(a_ready, ONE + s.use0 + in_use(s, e) + 1)
                if e == 0:
                    act.wait_ge(conv_done, ONE + s.k + 1)
                if e == K and s.tail:
                    act.wait_ge(gated, ONE + s.k)
                dst = xpre[:, e, data(s.nj)] if e < K else zs[:, s.nj, e - K, :]
                act.activation(dst, ps_a[:, bank(s, in_use(s, e)), :], ACT.Copy).then_inc(a_free, 1)

            def own_tap(s):
                if not s.scanning:
                    act.wait_ge(w_loaded, ONE + 16 * N_MAMBA_W)
                    act.activation(amat[:], amat[:], ACT.Exp).then_inc(a_exp, 1)
                act.wait_ge(a_free, ONE + s.use0 + s.x_use + K + 2)
                if s.tail:
                    act.wait_ge(gated, ONE + s.k)
                for k in range(K):
                    last = act.activation(xs[:, s.nj, k, :], xpre[:, k, data(s.nj)], ACT.Identity,
                                          scale=cw[:, s.nj, k, 3:4], bias=cb[:, s.nj, k:k + 1])
                last.then_inc(tap_done, 1)

            def silus(s):
                act.wait_ge(conv_done, ONE + s.k + 2)
                act.activation(xs[:, s.nj], xs[:, s.nj], ACT.Silu).then_inc(silu_done, 1)
                act.wait_ge(a_free, ONE + s.use0 + 2 + 8 + 2)
                act.activation(zs[:, s.nj], zs[:, s.nj], ACT.Silu).then_inc(silu_done, 1)
                act.preload_act_table_set("natural_log_exp_and_others")

            def x_copy(s):
                act.wait_ge(a_ready, ONE + s.use0 + 11)
                act.activation(xbc[:, s.nj, :], ps_a[0:3 * BC, bank(s, 10), :], ACT.Copy).then_inc(x_part1, 1)
                act.activation(xdt[3 * BC:NX, :], ps_a[3 * BC:NX, bank(s, 10), :], ACT.Copy)
                act.wait_ge(x_res1, ONE + s.k + 2)
                for q in (1, 2):
                    rows = slice(q * BC, (q + 1) * BC)
                    last = act.activation(xbc[rows, s.nj, :], xres[rows, :], ACT.Copy)
                last.then_inc(x_part2, 1)
                act.wait_ge(x_part2, ONE + s.k + 2)
                act.sem_inc(a_free, 1)

            def dt_parts(s, k):
                act.wait_ge(a_ready, ONE + s.use0 + 12 + k)
                if k == 0:
                    if s.scanning:
                        act.wait_ge(da_ready, ONE + s.k * S * K)
                    act.wait_ge(dt_ready, ONE + s.k + 1)
                act.activation(dt[:, s.nj, k, :], ps_a[:, bank(s, 11 + k), :], ACT.Relu, bias=dtb[:, s.nj, k:k + 1])
                act.activation(sp_tmp[:, k, :], ps_a[:, bank(s, 11 + k), :], ACT.Abs, bias=dtb[:, s.nj, k:k + 1]).then_inc(a_free, 1)

            def soft(s):
                act.wait_ge(a_free, ONE + s.use0 + USES + 2)
                act.activation(sp_tmp[:], sp_tmp[:], ACT.Exp, scale=-1.0).then_inc(soft_step, 1)
                act.wait_ge(soft_step, ONE + s.k + 2)
                act.activation(sp_tmp[:], sp_tmp[:], ACT.Ln, bias=one[:, 0:1]).then_inc(soft_done, 1)

            def spread_copy(s, i):
                act.wait_ge(bc_ready, ONE + s.k * 2 * S + 2 * i + 1)
                act.wait_ge(dbx_ready, ONE + s.k * S + i + 1)
                act.activation(bb[:, i % 4, :], ps_b[:, 0, :], ACT.Copy).then_inc(bc_copied, 1)
                act.wait_ge(bc_ready, ONE + s.k * 2 * S + 2 * i + 2)
                act.wait_ge(hc_ready, ONE + s.k * S + i + 1)
                act.activation(cc[:, i % 4, :], ps_b[:, 1, :], ACT.Copy).then_inc(bc_copied, 1)

            def decays(s, i):
                act.wait_ge(scanned, ONE + s.k * S + i + 1)
                j = s.j if i < S else s.nj
                if i == S:
                    act.wait_ge(dt_ready, ONE + s.k + 2)
                for k in range(K):
                    act.activation(da[:, i % 2, k, :], dt[:, j, k, :], ACT.Exp,
                                   scale=amat[:, j, k, i % S:i % S + 1]).then_inc(da_ready, 1)

            def tail(s, h):
                if h == 0:
                    act.wait_ge(mo_stored, ONE + s.k * 16 - 16)
                act.wait_ge(a_ready, ONE + s.use0 + s.out_use + h + 1)
                act.activation(mo[:, 2 * h:2 * h + 2, :].rearrange("p t c -> p (t c)"), ps_a[:, bank(s, s.out_use + h), :],
                               ACT.Copy).then_inc(a_free, 1)
                if h == 1:
                    act.wait_ge(a_free, ONE + s.use0 + s.out_use + 2 + 2)
                    act.sem_inc(out_copied, 2)

            def front(s, slot=None):
                for q, place in enumerate(ACT_IN):
                    if slot in (None, place):
                        in_copy(s, 2 * q)
                        in_copy(s, 2 * q + 1)
                if slot in (None, ACT_TAP):
                    own_tap(s)
                if slot in (None, ACT_SILU):
                    silus(s)
                if slot in (None, ACT_X):
                    x_copy(s)
                for q, place in enumerate(ACT_DT):
                    if slot in (None, place):
                        dt_parts(s, 2 * q)
                        dt_parts(s, 2 * q + 1)
                if slot in (None, ACT_SOFT):
                    soft(s)

            def step(s):
                for i in range(S):
                    if i + 2 < S or s.front:
                        spread_copy(s, i + 2)
                    if i + 1 < S or s.front:
                        decays(s, i + 1)
                    if i in ACT_OUT and s.tail:
                        tail(s, ACT_OUT.index(i))
                    if s.front:
                        front(s, i)


            def begin(s):
                front(s)
                act.wait_ge(a_neg, ONE + 1)
                spread_copy(s, S)
                spread_copy(s, S + 1)
                decays(s, S)

            run(act, begin, step, lambda s: [tail(s, h) for h in range(2)])

        @block.gpsimd
        def _(pool):
            def inputs(s, i):
                if i == 0:
                    pool.wait_ge(dtx_ready, ONE + s.k + 1)
                pool.wait_ge(bc_copied, ONE + s.k * 2 * S + 2 * i + 3)
                pool.wait_ge(summed, ONE + s.k * S + i + 1)
                pool.tensor_tensor(hh[:, i % 4, :, :], dtx[:, s.j, :, :], bb[:, i % 4, :].unsqueeze(1).broadcast_to([P, K, CH]),
                                   ALU.mult).then_inc(dbx_ready, 1)

            def tail(s):
                pool.wait_ge(y_ready, ONE + s.k * K)
                pool.wait_ge(dt_ready, ONE + s.fronts)
                dst = sp_tmp[:] if s.nj == 0 else sp_tmp[:, :, ::-1]
                pool.tensor_tensor(dst, xs[:, s.nj], zs[:, s.nj], ALU.mult).then_inc(gated, 1)

            def step(s):
                for i in range(S):
                    inputs(s, i)
                    if i == POOL_GATE and s.tail:
                        tail(s)

            pool.memset(keep[:, :], 1.0).then_inc(consts, 1)
            pool.wait_ge(consts, ONE + 1)
            pool.memset(keep[:, :].rearrange("p (b n) -> p b n", b=B)[:, :, 0:1], 0.0).then_inc(consts, 1)
            pool.memset(one[:, :], 1.0).then_inc(consts, 1)
            pool.memset(state[:], 0.0).then_inc(consts, 1)
            pool.memset(halo[:], 0.0).then_inc(consts, 1)
            pool.memset(pick[:, :], 0.0).then_inc(consts, 1)
            for q in range(3):
                pool.wait_ge(consts, ONE + 6 + q)
                pool.affine_select(out=pick[:, :], in_=pick[:, :], compare_op=ALU.not_equal, fill=1.0, base=-q * BC,
                                   pattern=[[-1, BC]], channel_multiplier=1).then_inc(consts, 1)
            pool.wait_ge(consts, ONE + N_CONSTS)
            run(pool, lambda s: None, step, tail)

        @block.vector
        def _(dve):
            TAPS = 4

            def conv(s, part):
                j = s.nj
                edge, spot = (slice(CH, W), slice(0, 3)) if j == 0 else (slice(0, 3), slice(CH, W))
                base = (s.k + 1) * TAPS
                if part == 0:
                    dve.wait_ge(a_free, ONE + s.use0 + s.x_use + K + 2)
                    dve.wait_ge(conv_done, ONE + s.k + 1)
                    dve.tensor_scalar(xpre[:, :, spot], halo[:, j], keep[:, s.nn:s.nn + 1] if isinstance(s.nn, int) else keep[:, ds(s.nn, 1)],
                                      None, ALU.mult).then_inc(conv_step, 1)
                    dve.wait_ge(conv_step, ONE + base + 1)
                    dve.tensor_copy(halo[:, j], xpre[:, :, edge]).then_inc(conv_step, 1)
                    dve.wait_ge(tap_done, ONE + s.k + 2)
                for tap in ((2,) if part == 0 else (1, 0)):
                    at = tap if j == 0 else 3 - tap
                    for k in range(K):
                        src = xpre[:, k, at:at + CH]
                        last = dve.scalar_tensor_tensor(xs[:, j, k, :], src, cw[:, j, k, tap:tap + 1], xs[:, j, k, :],
                                                        ALU.mult, ALU.add)
                    if tap:
                        last.then_inc(conv_step, 1)
                        dve.wait_ge(conv_step, ONE + base + 2 + 3 - tap)
                    else:
                        last.then_inc(conv_done, 1)

            def leave(s):
                dve.wait_ge(x_part1, ONE + s.k + 2)
                for q in (1, 2):
                    rows = slice(q * BC, (q + 1) * BC)
                    last = dve.tensor_tensor(xres[rows, :], ps_a[rows, bank(s, 10), :], xbc[rows, s.nj, :], ALU.subtract)
                last.then_inc(x_res1, 1)

            def split(s):
                dve.wait_ge(x_part2, ONE + s.k + 2)
                rows = slice(2 * BC, 3 * BC)
                dve.tensor_tensor(xbc[rows, s.nj, :], xres[rows, :], xbc[rows, s.nj, :], ALU.subtract).then_inc(x_split, 1)

            def scans(s, i):
                dve.wait_ge(dbx_ready, ONE + s.k * S + i + 5)
                if i == 0:
                    dve.wait_ge(kept, ONE + s.k + 1)
                for k in range(K):
                    dve.wait_ge(da_ready, ONE + (s.k * S + i) * K + k + 1)
                    h, a = hh[:, i % 4, k, :], da[:, i % 2, k, :]
                    if s.j:
                        h, a = h[:, ::-1], a[:, ::-1]
                    last = dve.tensor_tensor_scan(h, a, h, state[:, s.j, k, i:i + 1], ALU.mult, ALU.add)
                last.then_inc(scanned, 1)

            def save(s, i):
                dve.wait_ge(scanned, ONE + s.k * S + i + 3)
                j = s.j if i >= 0 else s.nj
                end = CH - 1 if j == 0 else 0
                dve.tensor_copy(state[:, j, :, i % S:i % S + 1], hh[:, i % 4, :, end:end + 1]).then_inc(saved, 1)

            def weigh(s):
                dve.wait_ge(soft_done, ONE + s.k + 2)
                dve.tensor_tensor(dt[:, s.nj], dt[:, s.nj], sp_tmp[:], ALU.add).then_inc(dt_ready, 1)
                dve.wait_ge(dt_ready, ONE + s.k + 2)
                if s.scanning:
                    dve.wait_ge(dbx_ready, ONE + s.k * S + 4)
                dve.tensor_tensor(dtx[:, s.nj], dt[:, s.nj], xs[:, s.nj], ALU.mult).then_inc(dtx_ready, 1)

            def outputs(s, i):
                dve.wait_ge(saved, ONE + s.k * S + i + 1)
                dve.wait_ge(bc_copied, ONE + s.k * 2 * S + 2 * i + 4)
                dve.tensor_tensor(hh[:, i % 4], hh[:, i % 4], cc[:, i % 4, :].unsqueeze(1).broadcast_to([P, K, CH]),
                                  ALU.mult).then_inc(hc_ready, 1)

            def tail(s):
                dve.wait_ge(summed, ONE + s.k * S + 4)
                for k in range(K):
                    dve.scalar_tensor_tensor(xs[:, s.nj, k, :], xs[:, s.nj, k, :], dskip[:, s.nj, k:k + 1], ps_y[:, k, :],
                                             ALU.mult, ALU.add).then_inc(y_ready, 1)

            def front(s, slot=None):
                for part, place in enumerate(DVE_CONV):
                    if slot in (None, place):
                        conv(s, part)
                if slot in (None, DVE_SPLIT[0]):
                    leave(s)
                if slot in (None, DVE_SPLIT[1]):
                    split(s)
                if slot in (None, DVE_WEIGH):
                    weigh(s)

            def step(s):
                for i in range(S):
                    if i or s.tail:
                        save(s, i - 1)
                    if i == 0:
                        dve.wait_ge(saved, ONE + s.k * S)
                        dve.tensor_scalar(state[:, s.j], state[:, s.j], keep[:, s.n:s.n + 1] if isinstance(s.n, int) else keep[:, ds(s.n, 1)],
                                          None, ALU.mult).then_inc(kept, 1)
                    scans(s, i)
                    if i or s.tail:
                        outputs(s, i - 1)
                    if i == DVE_SKIP and s.tail:
                        tail(s)
                    if s.front:
                        front(s, i)

            def end(s):
                save(s, -1)
                outputs(s, -1)
                tail(s)

            for t, v in ((a_free, 2), (bc_copied, 2), (dbx_ready, 4), (scanned, 2), (hc_ready, 4), (summed, 4)):
                dve.sem_inc(t, v)
            dve.wait_ge(a_exp, ONE + 1)
            dve.tensor_scalar(amat[:], amat[:], -1.0, None, ALU.mult).then_inc(a_neg, 1)
            dve.wait_ge(consts, ONE + N_CONSTS)
            run(dve, front, step, end)


def mlp_phase(nc, ctx, ident, w, t1, m_dirs, t2, xn, lg, xbuf):
    def sb(name, shape, dt=F32):
        return ctx.enter_context(nc.sbuf_tensor("ml_" + name, shape, dt))

    sem, start_semaphores = phase_semaphores(nc, ctx, "ml_")

    N = B * NCH
    FB = 4
    w1, w2 = sb("w1", [P, 2, FB * P]), sb("w2", [P, FB, C])
    gw = sb("gw", [P, 2, EXPERTS])
    b1, lng, lnb = sb("b1", [P, FB]), sb("lng", [P, 2]), sb("lnb", [P, 2])
    b2, gb = sb("b2", [P, C]), sb("gb", [P, EXPERTS])
    eps, zero = sb("eps", [P, 1]), sb("zero", [P, EXPERTS * CAP // (N * P) * C])
    min_, bin_, tin = sb("m", [P, 2, 4, C]), sb("back", [P, 2, 4, C]), sb("t1", [P, 2, 4, C])
    stats, mv = sb("stats", [P, 8, 6]), sb("mv", [P, 8, 2])
    std, rstd = sb("std", [P, 8]), sb("rstd", [P, 8])
    ht, xt = sb("ht", [P, 2, 2, CH]), sb("xt", [P, 2, CH])
    t2cur, xcur = sb("t2", [P, 2, 4, C]), sb("xn", [P, 2, 4, C])
    hid, pt = sb("hid", [P, 2, CH]), sb("pt", [P, FB, CH])
    ps_t = ctx.enter_context(nc.psum_tensor("ml_ps_t", [P, 2, CH], F32))
    ps_f = ctx.enter_context(nc.psum_tensor("ml_ps_f", [P, 2, CH], F32))
    ps_y = ctx.enter_context(nc.psum_tensor("ml_ps_y", [P, 2, CH], F32))
    ps_l = ctx.enter_context(nc.psum_tensor("ml_ps_l", [P, 4 * EXPERTS], F32))

    w_loaded, consts, zeroed = sem("w_loaded"), sem("consts"), sem("zeroed")
    m_loaded = [sem(f"m_loaded{j}") for j in range(2)]
    t_loaded = [sem(f"t_loaded{j}") for j in range(2)]
    t2_stored = [sem(f"t2_stored{j}") for j in range(2)]
    xn_stored = [sem(f"xn_stored{j}") for j in range(2)]
    m_ready, skip_step, skip_ready, bn_step, var_ready, std_ready, rstd_ready = (
        sem(n) for n in ("m_ready", "skip_step", "skip_ready", "bn_step", "var_ready", "std_ready", "rstd_ready"))
    h_normed, x_normed, turned, turned_copied = (sem(n) for n in ("h_normed", "x_normed", "turned", "turned_copied"))
    f_ready, hid_ready, act_ready, y_ready, t2_ready = (sem(n) for n in ("f_ready", "hid_ready", "act_ready", "y_ready", "t2_ready"))
    l_ready, lg_ready, stood, m_copied = sem("l_ready"), sem("lg_ready"), sem("stood"), sem("m_copied")

    def run(eng, step):
        step(-1, 1, None)
        step(0, 0, None)
        step(1, 1, None)
        with eng.Fori(0, (N - 4) // 2) as h:
            step(h * 2 + 2, 0, h)
            step(h * 2 + 3, 1, h)
        step(N - 2, 0, None)
        step(N - 1, 1, None)
        step(N, 0, None)

    def has(i, what):
        if not isinstance(i, int):
            return True
        return {"load": i + 2 < N, "a": i + 1 < N, "b": 0 <= i < N, "c": i >= 1, "l": i >= 2}[what]

    def loads(i, j, h):
        return h + 2 + j if h is not None else (i + 1) // 2 + 1

    def use(i, what):
        if isinstance(i, int) and i <= 0:
            return i + 1
        if isinstance(i, int) and i >= N - 1:
            return i + N - 1
        return i * 2 + (what == "c")

    start_semaphores()
    with nc.Block() as block:
        @block.sync
        def _(sp):
            n = 0
            for dst, src in ((w1[:, :, :], w["attn_w1"].rearrange("k p e -> p k e")),
                             (w2[:, :, :], w["attn_w2"].rearrange("k p e -> p k e")),
                             (gw[:, :, :], w["ffn_gate_w"].rearrange("(k p) e -> p k e", p=P)),
                             (b2[:, :], w["attn_b2"].partition_broadcast(P)),
                             (gb[:, :], w["ffn_gate_b"].partition_broadcast(P))):
                sp.dma_start(dst, src).then_inc(w_loaded, 16)
                n += 1
            for dst, src, cut in ((b1, "attn_b1", FB), (lng, "attn_ln_g", 2), (lnb, "attn_ln_b", 2)):
                for k in range(cut):
                    sp.dma_start(dst[:, k:k + 1], w[src][k * P:(k + 1) * P].unsqueeze(1)).then_inc(w_loaded, 16)
                    n += 1
            assert n == N_MLP_W

            def flat(t):
                return t.rearrange("p t c -> p (t c)")

            def load_m(c, j):
                sp.dma_start(flat(bin_[:, j]), m_dirs[1, (c + NCH) % N]).then_inc(m_loaded[j], 16)
                sp.dma_start(flat(min_[:, j]), m_dirs[0, c]).then_inc(m_loaded[j], 16)

            def step(i, j, h):
                q = 1 - j
                if has(i, "a"):
                    sp.wait_ge(t2_ready, ONE + i * 2 + 4)
                    stand(sp, stood)
                    sp.dma_start(flat(tin[:, q]), t1[i + 1]).then_inc(t_loaded[q], 16)
                    sp.dma_start(rows[i + 1], zero[:, :]).then_inc(zeroed, 16)
                if has(i, "load") and not (isinstance(i, int) and i < 0):
                    sp.wait_ge(m_copied, ONE + i + 1)
                    sp.wait_ge(skip_ready, ONE + i + 1)
                    stand(sp, stood)
                    load_m(i + 2, j)
                if has(i, "c"):
                    sp.wait_ge(x_normed, ONE + i)
                    stand(sp, stood)
                    sp.dma_start(xn[i - 1], flat(xcur[:, q])).then_inc(xn_stored[q], 16)
                if has(i, "b"):
                    sp.wait_ge(t2_ready, ONE + i * 2 + 6)
                    stand(sp, stood)
                    sp.dma_start(t2[i], flat(t2cur[:, j])).then_inc(t2_stored[j], 16)

            rows = xbuf[0:EXPERTS * CAP, :].rearrange("(n p t) c -> n p (t c)", n=N, p=P)

            load_m(0, 0)
            load_m(1, 1)
            sp.wait_ge(consts, ONE + 1)
            run(sp, step)
            for j in range(2):
                sp.wait_ge(xn_stored[j], ONE + 8 * N)
                sp.wait_ge(t2_stored[j], ONE + 8 * N)
            sp.wait_ge(zeroed, ONE + 16 * N)

        @block.gpsimd
        def _(pool):
            pool.memset(zero[:, :], 0.0).then_inc(consts, 1)
            pool.memset(eps[:, :], GN_EPS).then_inc(consts, 1)
            pool.memset(mv[:, :, :], 1.0).then_inc(consts, 1)
            pool.wait_ge(w_loaded, ONE + 16 * N_MLP_W)

            def step(i, j, h):
                q = 1 - j
                if has(i, "a"):
                    pool.wait_ge(m_loaded[q], ONE + loads(i, j, h) * 32)
                    pool.tensor_tensor(min_[:, q], min_[:, q], bin_[:, q], ALU.add).then_inc(m_ready, 1)
                    pool.wait_ge(m_ready, ONE + i + 2)
                    pool.wait_ge(t_loaded[q], ONE + loads(i, j, h) * 16)
                    pool.tensor_tensor(tin[:, q], tin[:, q], min_[:, q], ALU.add).then_inc(skip_step, 1)
                    pool.wait_ge(skip_step, ONE + i + 2)
                    pool.tensor_tensor(tin[:, q], tin[:, q], b2[:, :].unsqueeze(1).broadcast_to([P, 4, C]), ALU.add).then_inc(skip_ready, 1)
            run(pool, step)

        @block.tensor
        def _(pe):
            def turn(i, what, src, count):
                pe.wait_ge(count, ONE + (i + 2 if what == "a" else i))
                pe.wait_ge(turned_copied, ONE + use(i, what))
                for t in range(4):
                    for k in range(2):
                        last = pe.transpose(ps_t[:, k, t * P:(t + 1) * P], src(t, k), ident[:, :])
                last.then_inc(turned, 1)

            def logits(i):
                pe.wait_ge(turned_copied, ONE + use(i, "c") + 1)
                pe.wait_ge(lg_ready, ONE + i - 1)
                for t in range(4):
                    for k in range(2):
                        last = pe.matmul(ps_l[:, t * EXPERTS:(t + 1) * EXPERTS], xt[:, k, t * P:(t + 1) * P], gw[:, k, :],
                                         start=(k == 0), stop=(k == 1))
                last.then_inc(l_ready, 1)

            def step(i, j, h):
                q = 1 - j
                if has(i, "b"):
                    pe.wait_ge(m_copied, ONE + i + 1)
                    for f in range(FB):
                        pe.wait_ge(hid_ready, ONE + i * FB + f + 1)
                        for k in range(2):
                            last = pe.matmul(ps_f[:, f % 2, :], w1[:, k, f * P:(f + 1) * P], ht[:, j, k, :], start=(k == 0), stop=(k == 1))
                        last.then_inc(f_ready, 1)
                    if has(i, "l"):
                        logits(i - 1)
                    pe.wait_ge(act_ready, ONE + (i + 1) * FB + 2)
                    pe.wait_ge(t2_ready, ONE + i * 2 + 4)
                    for t in range(4):
                        for f in range(FB):
                            last = pe.matmul(ps_y[:, t // 2, (t % 2) * C:(t % 2 + 1) * C], pt[:, f, t * P:(t + 1) * P], w2[:, f, :],
                                             start=(f == 0), stop=(f == FB - 1))
                    last.then_inc(y_ready, 1)
                if has(i, "a"):
                    turn(i, "a", lambda t, k: bin_[:, q, t, k * P:(k + 1) * P], h_normed)
                if isinstance(i, int) and i == N:
                    logits(i - 1)
                if has(i, "c"):
                    turn(i, "c", lambda t, k: xcur[:, q, t, k * P:(k + 1) * P], x_normed)
                if isinstance(i, int) and i == N:
                    logits(i)

            pe.wait_ge(w_loaded, ONE + 16 * N_MLP_W)
            run(pe, step)

        @block.scalar
        def _(act):
            def step(i, j, h):
                q = 1 - j

                def biased(f):
                    act.wait_ge(f_ready, ONE + i * FB + f + 1)
                    act.wait_ge(act_ready, ONE + i * FB + f + 1)
                    act.activation(hid[:, f % 2, :], ps_f[:, f % 2, :], ACT.Identity, bias=b1[:, f:f + 1]).then_inc(hid_ready, 1)

                if has(i, "b"):
                    biased(0)
                    biased(1)
                act.wait_ge(var_ready, ONE + i + 2)
                act.activation(std[:, :], mv[:, :, 1], ACT.Sqrt, bias=eps[:, 0:1]).then_inc(std_ready, 1)
                if has(i, "b"):
                    biased(2)
                    biased(3)
                if has(i, "a"):
                    act.wait_ge(turned, ONE + use(i, "a") + 1)
                    for k in range(2):
                        last = act.activation(ht[:, q, k, :], ps_t[:, k, :], ACT.Identity, scale=lng[:, k:k + 1], bias=lnb[:, k:k + 1])
                    last.then_inc(turned_copied, 1)
                    act.wait_ge(turned_copied, ONE + use(i, "a") + 1)
                    act.sem_inc(m_copied, 1)
                if has(i, "c"):
                    act.wait_ge(turned, ONE + use(i, "c") + 1)
                    act.wait_ge(l_ready, ONE + i - 1)
                    act.activation(xt[:, :, :], ps_t[:, :, :], ACT.Copy).then_inc(turned_copied, 1)

            act.wait_ge(consts, ONE + 3)
            act.wait_ge(w_loaded, ONE + 16 * N_MLP_W)
            run(act, step)

        @block.vector
        def _(dve):
            def biased_logits(i):
                dve.wait_ge(l_ready, ONE + i)
                dst = lg[:, 4 * i - 4:4 * i, :] if isinstance(i, int) else lg[:, ds(i * 4 - 4, 4), :]
                dve.tensor_tensor(dst, ps_l[:, :].rearrange("p (t e) -> p t e", e=EXPERTS),
                                  gb[:, :].unsqueeze(1).broadcast_to([P, 4, EXPERTS]), ALU.add).then_inc(lg_ready, 1)

            def step(i, j, h):
                q = 1 - j
                if has(i, "a"):
                    dve.wait_ge(m_ready, ONE + i + 2)
                    for t in range(4):
                        last = dve.bn_stats(stats[:, t, :], min_[:, q, t, :])
                if has(i, "c"):
                    dve.wait_ge(t2_ready, ONE + i * 2 + 4)
                    for t in range(4):
                        last = dve.bn_stats(stats[:, 4 + t, :], t2cur[:, q, t, :])
                last.then_inc(bn_step, 1)
                dve.wait_ge(bn_step, ONE + i + 2)
                stand(dve, stood)
                for t in range(8):
                    if has(i, "a") if t < 4 else has(i, "c"):
                        last = dve.bn_aggr(mv[:, t, :], stats[:, t, :])
                last.then_inc(var_ready, 1)
                if has(i, "b"):
                    for f in range(FB):
                        dve.wait_ge(hid_ready, ONE + i * FB + f + 3)
                        if f == 0:
                            dve.wait_ge(y_ready, ONE + i)
                        dve.scalar_tensor_tensor(pt[:, f, :], hid[:, f % 2, :], 0.01, hid[:, f % 2, :], ALU.mult, ALU.max).then_inc(act_ready, 1)
                if has(i, "l"):
                    biased_logits(i - 1)
                dve.wait_ge(std_ready, ONE + i + 2)
                dve.reciprocal(rstd[:, :], std[:, :]).then_inc(rstd_ready, 1)
                dve.wait_ge(rstd_ready, ONE + i + 2)
                if has(i, "a"):
                    for t in range(4):
                        last = dve.tensor_scalar(bin_[:, q, t, :], min_[:, q, t, :], mv[:, t, 0:1], rstd[:, t:t + 1], ALU.subtract, ALU.mult)
                    last.then_inc(h_normed, 1)
                if has(i, "c"):
                    dve.wait_ge(xn_stored[q], ONE + (h + j if h is not None else (i - 1) // 2) * 16)
                    for t in range(4):
                        last = dve.tensor_scalar(xcur[:, q, t, :], t2cur[:, q, t, :], mv[:, 4 + t, 0:1], rstd[:, 4 + t:5 + t], ALU.subtract, ALU.mult)
                    last.then_inc(x_normed, 1)
                if has(i, "b"):
                    dve.wait_ge(y_ready, ONE + i + 1)
                    dve.wait_ge(skip_ready, ONE + i + 1)
                    if has(i, "c"):
                        dve.wait_ge(x_normed, ONE + i - 1)
                        dve.wait_ge(t2_stored[j], ONE + (h + 1 if h is not None else i // 2) * 16)
                    for g in range(2):
                        dve.tensor_tensor(t2cur[:, j, 2 * g:2 * g + 2, :].rearrange("p t c -> p (t c)"), ps_y[:, g, :],
                                          tin[:, j, 2 * g:2 * g + 2, :].rearrange("p t c -> p (t c)"), ALU.add).then_inc(t2_ready, 1)
                if isinstance(i, int) and i == N:
                    biased_logits(i)

            for t, v in ((t2_ready, 4), (hid_ready, 2), (act_ready, 2)):
                dve.sem_inc(t, v)
            dve.wait_ge(consts, ONE + 3)
            dve.wait_ge(w_loaded, ONE + 16 * N_MLP_W)
            run(dve, step)


def routing_phase(nc, ctx, lg, tri, slot, scat, weight):
    def sb(name, shape, dt=F32):
        return ctx.enter_context(nc.sbuf_tensor("rt_" + name, shape, dt))

    sem, start_semaphores = phase_semaphores(nc, ctx, "rt_")

    T, E = B * QT, EXPERTS
    mx, sh, ex, sm = sb("mx", [P, T]), sb("sh", [P, T, E]), sb("ex", [P, T, E]), sb("sm", [P, T])
    num, ones = sb("num", [P, E]), sb("ones", [P, P])
    cand, idx = sb("cand", [P, T, E]), sb("idx", [P, T])
    hot, tot, inc = sb("hot", [P, T, E]), sb("tot", [P, T, E]), sb("inc", [P, T, E])
    pos, kept, fslot, fscat = sb("pos", [P, T]), sb("kept", [P, T]), sb("fslot", [P, T]), sb("fscat", [P, T])
    ps_c = ctx.enter_context(nc.psum_tensor("rt_ps_c", [P, T * E], F32))
    ps_n = ctx.enter_context(nc.psum_tensor("rt_ps_n", [P, T * E], F32))
    consts, dve_step, sh_ready, ex_ready, hot_ready, counted, done = (
        sem(n) for n in ("consts", "dve_step", "sh_ready", "ex_ready", "hot_ready", "counted", "done"))
    wide = lambda t: t[:, :].unsqueeze(2).broadcast_to([P, T, E])
    flat = lambda t: t[:, :, :].rearrange("p t e -> p (t e)")

    start_semaphores()
    with nc.Block() as block:
        @block.gpsimd
        def _(pool):
            pool.memset(tri[:, :], 1.0).then_inc(consts, 1)
            pool.memset(ones[:, :], 1.0).then_inc(consts, 1)
            pool.iota(num[:, :], pattern=[[1, E]], base=0, channel_multiplier=0,
                      allow_small_or_imprecise_dtypes=True).then_inc(consts, 1)
            pool.wait_ge(consts, ONE + 3)
            pool.affine_select(out=tri[:, :], in_=tri[:, :], compare_op=ALU.is_ge, fill=0.0, base=0,
                               pattern=[[1, P]], channel_multiplier=-1).then_inc(consts, 1)

        @block.scalar
        def _(act):
            act.wait_ge(sh_ready, ONE + 1)
            act.activation(ex[:, :, :], sh[:, :, :], ACT.Exp).then_inc(ex_ready, 1)

        @block.tensor
        def _(pe):
            pe.wait_ge(consts, ONE + 4)
            pe.wait_ge(hot_ready, ONE + 1)
            pe.matmul(ps_c[:, :], tri[:, :], flat(hot), start=True, stop=True)
            pe.matmul(ps_n[:, :], ones[:, :], flat(hot), start=True, stop=True).then_inc(counted, 1)

        @block.vector
        def _(dve):
            n = [0]

            def link(ins):
                n[0] += 1
                ins.then_inc(dve_step, 1)
                dve.wait_ge(dve_step, ONE + n[0])

            dve.wait_ge(consts, ONE + 4)
            link(dve.tensor_reduce(mx[:, :], lg[:, :, :], AX.X, ALU.max))
            dve.tensor_tensor(sh[:, :, :], lg[:, :, :], wide(mx), ALU.subtract).then_inc(sh_ready, 1)
            dve.wait_ge(sh_ready, ONE + 1)
            link(dve.tensor_scalar(cand[:, :, :], sh[:, :, :], 0.0, -float(E), ALU.is_equal, ALU.mult))
            link(dve.scalar_tensor_tensor(cand[:, :, :], cand[:, :, :], float(E), num[:, :].unsqueeze(1).broadcast_to([P, T, E]), ALU.add, ALU.add))
            link(dve.tensor_reduce(idx[:, :], cand[:, :, :], AX.X, ALU.min))
            dve.tensor_tensor(hot[:, :, :], num[:, :].unsqueeze(1).broadcast_to([P, T, E]), wide(idx), ALU.is_equal).then_inc(hot_ready, 1)
            dve.wait_ge(ex_ready, ONE + 1)
            link(dve.tensor_reduce(sm[:, :], ex[:, :, :], AX.X, ALU.add))
            link(dve.reciprocal(weight[:, :], sm[:, :]))
            dve.wait_ge(counted, ONE + 1)
            link(dve.tensor_copy(flat(tot), ps_n[:, :]))
            for e in range(E):
                last = dve.tensor_tensor_scan(inc[:, :, e], ones[:, 0:T], tot[:, :, e], 0.0, ALU.mult, ALU.add)
            link(last)
            link(dve.tensor_tensor(flat(inc), flat(inc), flat(tot), ALU.subtract))
            link(dve.tensor_tensor(flat(inc), ps_c[:, :], flat(inc), ALU.add))
            link(dve.tensor_tensor(inc[:, :, :], inc[:, :, :], hot[:, :, :], ALU.mult))
            link(dve.tensor_reduce(pos[:, :], inc[:, :, :], AX.X, ALU.add))
            link(dve.tensor_scalar(kept[:, :], pos[:, :], float(CAP), None, ALU.is_le))
            link(dve.tensor_scalar(fslot[:, :], pos[:, :], float(CAP), -1.0, ALU.min, ALU.add))
            link(dve.scalar_tensor_tensor(fslot[:, :], idx[:, :], float(CAP), fslot[:, :], ALU.mult, ALU.add))
            link(dve.tensor_tensor(weight[:, :], weight[:, :], kept[:, :], ALU.mult))
            link(dve.tensor_scalar(fscat[:, :], kept[:, :], -float(E * CAP), float(E * CAP), ALU.mult, ALU.add))
            link(dve.tensor_tensor(fscat[:, :], fscat[:, :], fslot[:, :], ALU.add))
            link(dve.tensor_copy(slot[:, :], fslot[:, :]))
            link(dve.tensor_copy(scat[:, :], fscat[:, :]))


def experts_phase(nc, ctx, ident, w, xn, scat, xbuf, ybuf):
    def sb(name, shape, dt=F32):
        return ctx.enter_context(nc.sbuf_tensor("ex_" + name, shape, dt))

    sem, start_semaphores = phase_semaphores(nc, ctx, "ex_")

    E, F = EXPERTS, 1024
    FB, RC = F // P, 256
    M = CAP // RC
    w1, w2 = sb("w1", [P, 2, 2, F]), sb("w2", [P, 2, FB, C])
    b1, b2 = sb("b1", [P, E, FB]), sb("b2", [P, E, C])
    xr, xt = sb("xr", [P, 2, 2, C]), sb("xt", [P, 2, 2, RC])
    hid = sb("hid", [P, 2, FB, RC])
    yr = sb("yr", [P, 2, 2, C])
    ps_x = ctx.enter_context(nc.psum_tensor("ex_ps_x", [P, 2, CH], F32))
    ps_h = ctx.enter_context(nc.psum_tensor("ex_ps_h", [P, 4, CH], F32))
    ps_y = ctx.enter_context(nc.psum_tensor("ex_ps_y", [P, 2, CH], F32))
    b1c, b2c = sb("b1c", [P, 2, FB]), sb("b2c", [P, 2, C])
    b_loaded, bias_ready = sem("b_loaded"), sem("bias_ready")
    w_loaded = [sem(f"w_loaded{j}") for j in range(2)]
    x_loaded = [sem(f"x_loaded{j}") for j in range(2)]
    turned, x_copied, h_ready, relued, y_ready, y_added, stood = (
        sem(n) for n in ("turned", "x_copied", "h_ready", "relued", "y_ready", "y_added", "stood"))
    y_stored = [sem(f"y_stored{j}") for j in range(2)]
    rows = sb("rows", [P, 4, 4, C])
    rows_loaded = [sem(f"rows_loaded{j}") for j in range(4)]
    scattered = [sem(f"scattered{j}", 0) for j in range(4)]
    N = B * NCH
    TURN = 2 * M

    def loop(eng, chunk):
        with eng.Fori(0, E // 2) as r:
            for m in range(TURN):
                chunk(r * TURN + m, m, r)

    start_semaphores()
    with nc.Block() as block:
        @block.sync
        def _(sp):
            def load_rows(n):
                sp.dma_start(rows[:, n % 4].rearrange("p t c -> p (t c)"), xn[n]).then_inc(rows_loaded[n % 4], 16)

            for n in range(4):
                load_rows(n)
            sp.dma_start(b1[:, :, :], w["b1"]).then_inc(b_loaded, 16)
            sp.dma_start(b2[:, :, :].rearrange("p e c -> p (e c)"), w["b2"].rearrange("e c -> (e c)").partition_broadcast(P)).then_inc(b_loaded, 16)

            def load_w(e, j):
                sp.dma_start(w1[:, j], w["w1"][e].rearrange("(k p) f -> p k f", p=P)).then_inc(w_loaded[j], 16)
                sp.dma_start(w2[:, j], w["w2"][e].rearrange("(f p) c -> p f c", p=P)).then_inc(w_loaded[j], 16)

            def load_x(n, j):
                sp.dma_start(xr[:, j], xbuf[ds(n * RC, RC), :].rearrange("(t p) c -> p t c", p=P)).then_inc(x_loaded[j], 16)

            load_w(0, 0)
            load_w(1, 1)
            for n in range(4, N):
                sp.wait_ge(scattered[n % 4], 64 * (n // 4))
                load_rows(n)
            for j in range(4):
                sp.wait_ge(scattered[j], 64 * (N // 4))
            load_x(0, 0)
            load_x(1, 1)

            def chunk(n, m, r, last=False):
                if not (last and m >= TURN - 2):
                    sp.wait_ge(turned, ONE + n + 1)
                    stand(sp, stood)
                    load_x(n + 2, m % 2)
                if not last and m in (M, TURN - 1):
                    j = 0 if m == M else 1
                    sp.wait_ge(y_ready, ONE + (n if m == M else n + 1))
                    stand(sp, stood)
                    load_w(r * 2 + 2 + j, j)
                sp.wait_ge(y_added, ONE + (n + 1) * 2)
                stand(sp, stood)
                sp.dma_start(ybuf[ds(n * RC, RC), :].rearrange("(t p) c -> p t c", p=P), yr[:, m % 2]).then_inc(y_stored[m % 2], 16)

            with sp.Fori(0, E // 2 - 1) as r:
                for m in range(TURN):
                    chunk(r * TURN + m, m, r)
            for m in range(TURN):
                chunk((E // 2 - 1) * TURN + m, m, None, last=True)
            for j in range(2):
                sp.wait_ge(y_stored[j], ONE + 16 * E * M // 2)

        @block.gpsimd
        def _(pool):
            for n in range(N):
                pool.wait_ge(rows_loaded[n % 4], ONE + 16 * (n // 4 + 1))
                for t in range(4):
                    pool.indirect_dma_start(
                        out=xbuf, out_offset=bass.IndirectOffsetOnAxis(ap=scat[:, 4 * n + t:4 * n + t + 1], axis=0),
                        in_=rows[:, n % 4, t, :], in_offset=None, bounds_check=EXPERTS * CAP - 1,
                        oob_is_err=False).then_inc(scattered[n % 4], 16)

        @block.tensor
        def _(pe):
            def turn(n, q, loads):
                pe.wait_ge(x_loaded[q], ONE + loads)
                pe.wait_ge(x_copied, ONE + n)
                for t in range(2):
                    for k in range(2):
                        last = pe.transpose(ps_x[:, q, k * RC + t * P:k * RC + (t + 1) * P], xr[:, q, t, k * P:(k + 1) * P], ident[:, :])
                last.then_inc(turned, 1)

            def chunk(n, m, r, last=False):
                j, q = m // M, m % 2
                if m % M == 0:
                    pe.wait_ge(w_loaded[j], ONE + (r + 1) * 32)
                pe.wait_ge(x_copied, ONE + n + 2)
                for f in range(FB):
                    pe.wait_ge(relued, ONE + n * FB + f + 1)
                    for k in range(2):
                        ins = pe.matmul(ps_h[:, f % 4, 0:RC], w1[:, j, k, f * P:(f + 1) * P], xt[:, q, k, :], start=(k == 0), stop=(k == 1))
                    ins.then_inc(h_ready, 1)
                if not (last and m == TURN - 1):
                    turn(n + 1, 1 - q, (r * (TURN // 2) + (m + 1) // 2 + 1) * 16)
                pe.wait_ge(relued, ONE + (n + 1) * FB + 4)
                pe.wait_ge(y_added, ONE + n * 2)
                for t in range(2):
                    for f in range(FB):
                        ins = pe.matmul(ps_y[:, t, 0:C], hid[:, q, f, t * P:(t + 1) * P], w2[:, j, f, :], start=(f == 0), stop=(f == FB - 1))
                ins.then_inc(y_ready, 1)

            turn(0, 0, 16)
            with pe.Fori(0, E // 2 - 1) as r:
                for m in range(TURN):
                    chunk(r * TURN + m, m, r)
            for m in range(TURN):
                chunk((E // 2 - 1) * TURN + m, m, E // 2 - 1, last=True)

        @block.scalar
        def _(act):
            def chunk(n, m, r):
                q = m % 2
                if m % M == 0:
                    act.wait_ge(bias_ready, ONE + r * 2 + m // M + 1)
                for f in range(FB):
                    act.wait_ge(h_ready, ONE + n * FB + f + 1)
                    act.activation(hid[:, q, f, :], ps_h[:, f % 4, 0:RC], ACT.Relu, bias=b1c[:, m // M, f:f + 1]).then_inc(relued, 1)
            loop(act, chunk)

        @block.vector
        def _(dve):
            def copy(n, q):
                dve.wait_ge(turned, ONE + n + 1)
                dve.tensor_copy(xt[:, q], ps_x[:, q, :].rearrange("p (k r) -> p k r", k=2)).then_inc(x_copied, 1)

            def chunk(n, m, r, last=False):
                q = m % 2
                if m % M == 0:
                    dve.wait_ge(y_ready, ONE + n)
                    dve.tensor_copy(b2c[:, m // M, :], b2[:, ds(r * 2 + m // M, 1), :].rearrange("p a c -> p (a c)"))
                    dve.tensor_copy(b1c[:, m // M, :], b1[:, ds(r * 2 + m // M, 1), :].rearrange("p a f -> p (a f)")).then_inc(bias_ready, 1)
                    dve.wait_ge(bias_ready, ONE + r * 2 + m // M + 1)
                if not (last and m == TURN - 1):
                    copy(n + 1, 1 - q)
                dve.wait_ge(y_ready, ONE + n + 1)
                dve.wait_ge(y_stored[q], ONE + r * (TURN // 2) * 16 + m // 2 * 16)
                for t in range(2):
                    dve.tensor_tensor(yr[:, q, t, :], ps_y[:, t, 0:C], b2c[:, m // M, :], ALU.add).then_inc(y_added, 1)

            dve.wait_ge(b_loaded, ONE + 32)
            dve.sem_inc(x_copied, 1)
            dve.sem_inc(relued, 4)
            copy(0, 0)
            with dve.Fori(0, E // 2 - 1) as r:
                for m in range(TURN):
                    chunk(r * TURN + m, m, r)
            for m in range(TURN):
                chunk((E // 2 - 1) * TURN + m, m, E // 2 - 1, last=True)


def gather_phase(nc, ctx, ident, ybuf, slot, weight, t2, out):
    def sb(name, shape, dt=F32):
        return ctx.enter_context(nc.sbuf_tensor("ga_" + name, shape, dt))

    sem, _ = phase_semaphores(nc, ctx, "ga_")

    N = B * NCH
    D = 4
    yg, tin = sb("yg", [P, D, 4, C]), sb("t2", [P, D, 4, C])
    safe, fin, same = sb("safe", [P, 2, 4, C]), sb("fin", [P, 2, 4 * C], I32), sb("same", [P, 2, 4 * C], I32)
    bounded, fin_ready, cleared = sem("bounded"), sem("fin_ready"), sem("cleared")
    zero = sb("zero", [P, 4 * C])
    bound = sb("bound", [P, 2, 4, C])
    lim = sb("lim", [P, 2, 4, C])
    ot = sb("ot", [P, 2, 2, CH])
    ps_o = ctx.enter_context(nc.psum_tensor("ga_ps_o", [P, 2, 2, CH], F32))
    t_loaded = [sem(f"t_loaded{j}") for j in range(D)]
    y_loaded = [sem(f"y_loaded{j}") for j in range(D)]
    zeroed, weighed, masked, chosen, kept_step, added, turned, copied = (
        sem(n) for n in ("zeroed", "weighed", "masked", "chosen", "kept_step", "added", "turned", "copied"))
    stored = [sem(f"stored{j}") for j in range(2)]
    flat = lambda t: t.rearrange("p t c -> p (t c)")

    with nc.Block() as block:
        @block.gpsimd
        def _(pool):
            def fetch(n):
                j = n % D
                for t in range(4):
                    pool.indirect_dma_start(
                        out=yg[:, j, t, :], out_offset=None, in_=ybuf,
                        in_offset=bass.IndirectOffsetOnAxis(ap=slot[:, 4 * n + t:4 * n + t + 1], axis=0),
                        bounds_check=EXPERTS * CAP - 1, oob_is_err=False).then_inc(y_loaded[j], 16)

            for n in range(D):
                fetch(n)
            for n in range(N):
                j, q = n % D, n % 2
                pool.wait_ge(t_loaded[j], 16 * (n // D + 1))
                pool.wait_ge(kept_step, n + 1)
                pool.tensor_tensor(tin[:, j], tin[:, j], safe[:, q], ALU.add).then_inc(added, 1)
                if n + D < N:
                    fetch(n + D)

        @block.sync
        def _(sp):
            for n in range(N):
                j = n % D
                if n >= D:
                    sp.wait_ge(turned, n - D + 1)
                sp.dma_start(flat(tin[:, j]), t2[n]).then_inc(t_loaded[j], 16)

        @block.vector
        def _(dve):
            dve.memset(zero[:, :], 0.0).then_inc(zeroed, 1)
            for n in range(N):
                j, q = n % D, n % 2
                y = yg[:, j]
                dve.wait_ge(weighed, n + 1)
                if n:
                    dve.wait_ge(kept_step, n)
                dve.tensor_tensor(same[:, q, :], flat(y), flat(y), ALU.is_equal)
                dve.tensor_scalar(flat(bound[:, q]), flat(y), FLT_MAX, -FLT_MAX, ALU.min, ALU.max).then_inc(bounded, 1)
                dve.tensor_scalar(flat(lim[:, q]), flat(y), 1e4, -1e4, ALU.min, ALU.max).then_inc(masked, 1)
                dve.wait_ge(bounded, n + 1)
                dve.tensor_tensor(fin[:, q, :], flat(bound[:, q]), flat(y), ALU.is_equal).then_inc(fin_ready, 1)
                dve.wait_ge(masked, n + 1)
                dve.wait_ge(cleared, n + 1)
                dve.copy_predicated(flat(safe[:, q]), same[:, q, :], flat(lim[:, q])).then_inc(chosen, 1)
                dve.wait_ge(chosen, n + 1)
                dve.wait_ge(fin_ready, n + 1)
                dve.copy_predicated(flat(safe[:, q]), fin[:, q, :], flat(y)).then_inc(kept_step, 1)

        @block.tensor
        def _(pe):
            for n in range(N):
                j, q = n % D, n % 2
                pe.wait_ge(added, n + 1)
                if n >= 2:
                    pe.wait_ge(copied, n - 1)
                for t in range(4):
                    for k in range(2):
                        last = pe.transpose(ps_o[:, q, k, t * P:(t + 1) * P], tin[:, j, t, k * P:(k + 1) * P], ident[:, :])
                last.then_inc(turned, 1)

        @block.scalar
        def _(act):
            def prepare(n):
                j, q = n % D, n % 2
                act.wait_ge(y_loaded[j], 64 * (n // D + 1))
                for t in range(4):
                    last = act.activation(yg[:, j, t, :], yg[:, j, t, :], ACT.Copy, scale=weight[:, 4 * n + t:4 * n + t + 1])
                last.then_inc(weighed, 1)
                if n >= 2:
                    act.wait_ge(added, n - 1)
                act.activation(flat(safe[:, q]), zero[:, :], ACT.Copy).then_inc(cleared, 1)

            act.wait_ge(zeroed, 1)
            prepare(0)
            for n in range(N):
                q = n % 2
                if n + 1 < N:
                    prepare(n + 1)
                act.wait_ge(turned, n + 1)
                if n >= 2:
                    act.wait_ge(stored[q], 16 * (n // 2))
                act.activation(ot[:, q], ps_o[:, q], ACT.Copy).then_inc(copied, 1)
                act.wait_ge(copied, n + 1)
                b, c = divmod(n, NCH)
                act.dma_start(out[b * C:(b + 1) * C, c * CH:(c + 1) * CH].rearrange("(k p) l -> p k l", p=P), ot[:, q]).then_inc(stored[q], 16)
            for j in range(2):
                act.wait_ge(stored[j], 8 * N)


N_CONV_W = 3 * 8 + 2 * 4
N_MAMBA_W = 8 * 2 + 1 + 3 * 2 * 4
N_MLP_W = 5 + 8


def hybrid_kernel(nc, a, out):
    x = a["x"].rearrange("b c h w -> (b c) (h w)")
    q_split = scratch(nc, "q_split", (3, C * B, L), BF16)
    k_split = scratch(nc, "k_split", (3, C * B, L), BF16)
    v_split = scratch(nc, "v_split", (HEADS, P, QT * P), BF16)
    attn_out = scratch(nc, "attn_out", (HEADS, P, QT * DH))
    with ExitStack() as whole:
        ident = whole.enter_context(nc.sbuf_tensor("ident", [P, P], F32))
        ident_ready = whole.enter_context(nc.semaphore("ident_ready"))
        with nc.Block() as block:
            @block.gpsimd
            def _(pool):
                pool.memset(ident[:, :], 0.0).then_inc(ident_ready, 1)
                pool.wait_ge(ident_ready, 1)
                pool.affine_select(out=ident[:, :], in_=ident[:, :], compare_op=ALU.not_equal, fill=1.0, base=0,
                                   pattern=[[-1, P]], channel_multiplier=1).then_inc(ident_ready, 1)
                pool.wait_ge(ident_ready, 2)
        with ExitStack() as ctx:
            conv_phase(nc, ctx, ident, x, a["L0_conv_qw"], a["L0_conv_kw"], a["L0_conv_vw"], a["L0_conv_c1w"],
                       a["L0_conv_c1b"], a["L0_conv_gnw"], a["L0_conv_gnb"], q_split, k_split, v_split)
        with ExitStack() as ctx:
            attention_phase(nc, ctx, ident, q_split, k_split, v_split, attn_out)
        t1 = scratch(nc, "t1", (B * NCH, P, 4 * C))
        u1 = scratch(nc, "u1", (B * NCH, P, 2 * CH))
        m_dirs = scratch(nc, "m_dirs", (2, B * NCH, P, 4 * C))
        with ExitStack() as ctx:
            tokens_phase(nc, ctx, ident, x, attn_out, t1, u1)
        with ExitStack() as ctx:
            mamba_phase(nc, ctx, ident, {k[8:]: v for k, v in a.items() if k.startswith("L1_attn_")}, u1, m_dirs)
        t2 = scratch(nc, "t2", (B * NCH, P, 4 * C))
        xn = scratch(nc, "xn", (B * NCH, P, 4 * C))
        xbuf = scratch(nc, "xbuf", (EXPERTS * CAP, C))
        ybuf = scratch(nc, "ybuf", (EXPERTS * CAP, C))
        lg, weight = (whole.enter_context(nc.sbuf_tensor(*v, F32)) for v in (("lg", [P, B * QT, EXPERTS]), ("weight", [P, B * QT])))
        slot, scat = (whole.enter_context(nc.sbuf_tensor(n, [P, B * QT], U32)) for n in ("slot", "scat"))
        tri = whole.enter_context(nc.sbuf_tensor("tri", [P, P], F32))
        w = {k[3:]: v for k, v in a.items() if k.startswith("L1_")}
        with ExitStack() as ctx:
            mlp_phase(nc, ctx, ident, w, t1, m_dirs, t2, xn, lg, xbuf)
        with ExitStack() as ctx:
            routing_phase(nc, ctx, lg, tri, slot, scat, weight)
        with ExitStack() as ctx:
            experts_phase(nc, ctx, ident, {k[4:]: v for k, v in w.items() if k.startswith("ffn_")}, xn, scat, xbuf, ybuf)
        with ExitStack() as ctx:
            gather_phase(nc, ctx, ident, ybuf, slot, weight, t2, out.rearrange("b c h w -> (b c) (h w)"))

def _layout(inputs, np):
    w = {k: np.ascontiguousarray(v) for k, v in inputs.items()}
    for n in ("qw", "kw", "vw"):
        t = w[f"L0_conv_{n}"].reshape(4, 16, 16, 9)
        w[f"L0_conv_{n}"] = t.transpose(0, 2, 3, 1)
    for n, cut in (("in_proj_w", 2), ("x_proj_w", 4), ("out_proj_w", 4)):
        t = w[f"L1_attn_{n}"].transpose(0, 2, 1)
        w[f"L1_attn_{n}"] = t.reshape(2, cut, P, t.shape[2])
    for n, cut in (("w1", 2), ("w2", 4)):
        t = w[f"L1_attn_{n}"].T
        w[f"L1_attn_{n}"] = t.reshape(cut, P, t.shape[1])
    w["L1_ffn_b1"] = w["L1_ffn_b1"].reshape(EXPERTS, -1, P).transpose(2, 0, 1)
    w["L1_attn_dt_proj_w"] = w["L1_attn_dt_proj_w"].transpose(0, 2, 1)
    w["L0_conv_c1w"] = w["L0_conv_c1w"][:, :, 0, 0].T
    return {k: np.ascontiguousarray(v) for k, v in w.items()}


def kernel(**inputs):
    import numpy as _np
    import concourse.bacc as _bacc
    from concourse.bass_utils import run_bass_kernel_spmd as _run

    nc = _bacc.Bacc("TRN2", target_bir_lowering=False, num_devices=1)
    arrays, args = {}, {}
    for name, a in _layout(inputs, _np).items():
        arrays[f"in_{name}"] = a
        args[name] = nc.dram_tensor(f"in_{name}", a.shape, mybir.dt.from_np(a.dtype), kind="ExternalInput").ap()
    out = nc.dram_tensor("out_x", (B, C, IMG, IMG), F32, kind="ExternalOutput").ap()
    hybrid_kernel(nc, args, out)
    r = _run(nc, [arrays], core_ids=[0])
    return r.results[0]["out_x"]
```
